# Optimizing a Trainium2 kernel written in Bass

```python
import numpy as np
import jax
import jax.numpy as jnp

def _softmax(x, axis=-1):
    return jax.nn.softmax(x, axis=axis)

def _gelu(x):
    return jax.nn.gelu(x, approximate=True)

def _silu(x):
    return jax.nn.silu(x)

def _sigmoid(x):
    return jax.nn.sigmoid(x)

def _layernorm(x, axis=-1, eps=1e-05):
    m = jnp.mean(x, axis=axis, keepdims=True)
    v = jnp.var(x, axis=axis, keepdims=True)
    return (x - m) / jnp.sqrt(v + eps)

def _scatter_add(tgt, idx, src, axis=0):
    return tgt.at[idx].add(src)

def _segment_sum(src, seg, n):
    return jax.ops.segment_sum(src, seg, n)
kernel_name = 'mk_gps_d2_gnn_r8_5436ca'

def setup_inputs(seed: int=0):
    np.random.seed(seed)
    _w = jnp.asarray

    def _rec_inputs():
        import jax
        import jax.numpy as jnp
        _gk = jax.random.key(seed)
        x = -8.776e-05 + 1 * jax.random.normal(jax.random.fold_in(_gk, 1), (1250, 512), jnp.float32)
        src = jax.random.randint(jax.random.fold_in(_gk, 2), (40000,), 0, 1250, jnp.int32)
        dst = jax.random.randint(jax.random.fold_in(_gk, 3), (40000,), 0, 1250, jnp.int32)
        _o = jnp.argsort(dst, stable=True)
        src = src[_o]
        dst = dst[_o]
        edge_weight = jax.random.uniform(jax.random.fold_in(_gk, 14), (40000,), jnp.float32, 0.0, 1)
        return (x, src, dst, edge_weight)
    x, src, dst, edge_weight = _rec_inputs()

    def _L0_gnn_setup():
        import jax, jax.numpy as jnp
        import numpy as np
        N_NODES = 1250
        N_EDGES = 20000
        IN_DIM = 512
        OUT_DIM = 512
        LN_EPS = 1e-05
        key = jax.random.key(seed)
        k_x, k_src, k_ws, k_wn = jax.random.split(key, 4)
        x = jax.random.normal(k_x, (N_NODES, IN_DIM), dtype=jnp.float32)
        edge_src = jax.random.randint(k_src, (N_EDGES,), 0, N_NODES, dtype=jnp.int32)
        edge_dst = jnp.repeat(jnp.arange(N_NODES, dtype=jnp.int32), N_EDGES // N_NODES)
        deg = jnp.full((N_NODES,), float(N_EDGES // N_NODES), dtype=jnp.float32)
        scale = 1.0 / np.sqrt(IN_DIM)
        W_self = jax.random.normal(k_ws, (OUT_DIM, IN_DIM), dtype=jnp.float32) * scale
        W_neigh = jax.random.normal(k_wn, (OUT_DIM, IN_DIM), dtype=jnp.float32) * scale
        bias = jnp.zeros((OUT_DIM,), dtype=jnp.float32)
        gamma = jnp.ones((OUT_DIM,), dtype=jnp.float32)
        beta = jnp.zeros((OUT_DIM,), dtype=jnp.float32)
        return {'x': x, 'edge_src': edge_src, 'edge_dst': edge_dst, 'deg': deg, 'W_self': W_self, 'W_neigh': W_neigh, 'bias': bias, 'gamma': gamma, 'beta': beta}
    _L0_gnn_all = _L0_gnn_setup()
    _L0_gnn_in = {k: v for k, v in _L0_gnn_all.items() if k in ('W_self', 'W_neigh', 'bias', 'gamma', 'beta')}
    del _L0_gnn_all

    def _L0_mix_setup():
        import jax, jax.numpy as jnp
        import numpy as np
        EPS = 1e-06
        H = 8
        DH = 64
        LN_EPS = 1e-05

        def _layernorm(x, g, b):
            m = jnp.mean(x, axis=-1, keepdims=True)
            v = jnp.mean(jnp.square(x - m), axis=-1, keepdims=True)
            return (x - m) / jnp.sqrt(v + LN_EPS) * g + b

        def _flow_attention(x, Wq, bq, Wk, bk, Wv, bv, Wo, bo):
            B, L, D = x.shape
            S = L
            q = jax.nn.sigmoid((x @ Wq + bq).reshape(B, L, H, DH).transpose(0, 2, 1, 3))
            k = jax.nn.sigmoid((x @ Wk + bk).reshape(B, S, H, DH).transpose(0, 2, 1, 3))
            v = (x @ Wv + bv).reshape(B, S, H, DH).transpose(0, 2, 1, 3)
            sink_incoming = 1.0 / jnp.einsum('nhld,nhd->nhl', q + EPS, k.sum(axis=2) + EPS)
            source_outgoing = 1.0 / jnp.einsum('nhld,nhd->nhl', k + EPS, q.sum(axis=2) + EPS)
            conserved_sink = jnp.einsum('nhld,nhd->nhl', q + EPS, (k * source_outgoing[..., None]).sum(axis=2) + EPS)
            conserved_source = jnp.einsum('nhld,nhd->nhl', k + EPS, (q * sink_incoming[..., None]).sum(axis=2) + EPS)
            conserved_source = jnp.clip(conserved_source, -1.0, 1.0)
            sink_allocation = jax.nn.sigmoid(conserved_sink * (float(L) / float(S)))
            source_competition = jax.nn.softmax(conserved_source, axis=-1) * float(S)
            kv = jnp.einsum('nhld,nhlm->nhdm', k, v * source_competition[..., None])
            o = jnp.einsum('nhld,nhdm->nhlm', q * sink_incoming[..., None], kv)
            o = o * sink_allocation[..., None]
            o = o.transpose(0, 2, 1, 3).reshape(B, L, D)
            return o @ Wo + bo
        key = jax.random.key(seed)
        ks = jax.random.split(key, 16)
        B, L, D, F = (2, 2048, 512, 256)
        s = 0.02
        inp = {'x': jax.random.normal(ks[0], (B, L, D), dtype=jnp.float32), 'Wq': jax.random.normal(ks[1], (D, D), dtype=jnp.float32) * s, 'bq': jnp.zeros((D,), jnp.float32), 'Wk': jax.random.normal(ks[2], (D, D), dtype=jnp.float32) * s, 'bk': jnp.zeros((D,), jnp.float32), 'Wv': jax.random.normal(ks[3], (D, D), dtype=jnp.float32) * s, 'bv': jnp.zeros((D,), jnp.float32), 'Wo': jax.random.normal(ks[4], (D, D), dtype=jnp.float32) * s, 'bo': jnp.zeros((D,), jnp.float32), 'W1': jax.random.normal(ks[5], (D, F), dtype=jnp.float32) * s, 'b1': jnp.zeros((F,), jnp.float32), 'W2': jax.random.normal(ks[6], (F, D), dtype=jnp.float32) * s, 'b2': jnp.zeros((D,), jnp.float32), 'g1': jnp.ones((D,), jnp.float32), 'be1': jnp.zeros((D,), jnp.float32), 'g2': jnp.ones((D,), jnp.float32), 'be2': jnp.zeros((D,), jnp.float32)}
        return inp
    _L0_mix_all = _L0_mix_setup()
    _L0_mix_in = {k: v for k, v in _L0_mix_all.items() if k in ('Wq', 'bq', 'Wk', 'bk', 'Wv', 'bv', 'Wo', 'bo', 'W1', 'b1', 'W2', 'b2', 'g1', 'be1', 'g2', 'be2')}
    del _L0_mix_all

    def _L0_ffn_setup():
        import jax, jax.numpy as jnp
        import numpy as np
        B, S, D, E, O = (1024, 256, 512, 16, 512)
        key = jax.random.key(seed)
        k_x, k_wg, k_bg, k_we, k_be = jax.random.split(key, 5)
        scale_g = 1.0 / np.sqrt(D)
        scale_e = 1.0 / np.sqrt(D)
        return {'x': jax.random.normal(k_x, (B, S, D), dtype=jnp.float32), 'Wg': jax.random.uniform(k_wg, (D, E), jnp.float32, -scale_g, scale_g), 'bg': jax.random.uniform(k_bg, (E,), jnp.float32, -scale_g, scale_g), 'We': jax.random.uniform(k_we, (E, D, O), jnp.float32, -scale_e, scale_e), 'be': jax.random.uniform(k_be, (E, O), jnp.float32, -scale_e, scale_e)}
    _L0_ffn_all = _L0_ffn_setup()
    _L0_ffn_in = {k: v for k, v in _L0_ffn_all.items() if k in ('Wg', 'bg', 'We', 'be')}
    del _L0_ffn_all

    def _L1_gnn_setup():
        import jax, jax.numpy as jnp
        import numpy as np
        N = 6250
        E = 200000
        F_IN = 512
        H = 128
        key = jax.random.key(seed)
        k0, k1, k2, k3 = jax.random.split(key, 4)
        x = jax.random.normal(k0, (N, F_IN), dtype=jnp.float32)
        edge_index = jax.random.randint(k1, (2, E), 0, N, dtype=jnp.int32)
        edge_weight = jnp.ones((E,), dtype=jnp.float32)
        W_conv = jax.random.normal(k2, (F_IN, H), dtype=jnp.float32) * np.sqrt(2.0 / (F_IN + H)).astype(np.float32)
        b_conv = jnp.zeros((H,), dtype=jnp.float32)
        W_lin = jax.random.normal(k3, (H, F_IN), dtype=jnp.float32) * np.sqrt(2.0 / (H + F_IN)).astype(np.float32)
        b_lin = jnp.zeros((F_IN,), dtype=jnp.float32)
        return {'x': x, 'edge_index': edge_index, 'edge_weight': edge_weight, 'W_conv': W_conv, 'b_conv': b_conv, 'W_lin': W_lin, 'b_lin': b_lin}
    _L1_gnn_all = _L1_gnn_setup()
    _L1_gnn_in = {k: v for k, v in _L1_gnn_all.items() if k in ('W_conv', 'b_conv', 'W_lin', 'b_lin')}
    del _L1_gnn_all

    def _L1_mix_setup():
        import jax, jax.numpy as jnp
        import numpy as np
        N, B, C, H = (512, 8, 512, 8)
        D = C // H
        EPS = 1e-06

        def _dot(a, b):
            return jnp.einsum('bhsd,bhd->bhs', a, b)
        key = jax.random.key(seed)
        ks = jax.random.split(key, 6)
        scale = 0.02
        return {'query': jax.random.normal(ks[0], (N, B, C), dtype=jnp.float32), 'Wq': jax.random.normal(ks[1], (C, C), dtype=jnp.float32) * scale, 'bq': jnp.zeros((C,), dtype=jnp.float32), 'Wk': jax.random.normal(ks[2], (C, C), dtype=jnp.float32) * scale, 'bk': jnp.zeros((C,), dtype=jnp.float32), 'Wv': jax.random.normal(ks[3], (C, C), dtype=jnp.float32) * scale, 'bv': jnp.zeros((C,), dtype=jnp.float32), 'Wo': jax.random.normal(ks[4], (C, C), dtype=jnp.float32) * scale, 'bo': jnp.zeros((C,), dtype=jnp.float32), 'temperature': jnp.ones((1,), dtype=jnp.float32)}
    _L1_mix_all = _L1_mix_setup()
    _L1_mix_in = {k: v for k, v in _L1_mix_all.items() if k in ('Wq', 'bq', 'Wk', 'bk', 'Wv', 'bv', 'Wo', 'bo', 'temperature')}
    del _L1_mix_all

    def _L1_ffn_setup():
        import jax, jax.numpy as jnp
        import numpy as np
        D = 512
        E = 8
        K = 2
        EXP = 4
        LN_EPS = 1e-05
        key = jax.random.key(seed)
        ks = jax.random.split(key, 8)
        B, T = (8, 256)
        Dh = D * EXP
        x = jax.random.normal(ks[0], (B, T, D), dtype=jnp.float32)
        ln_g = jnp.ones((D,), dtype=jnp.float32)
        ln_b = jnp.zeros((D,), dtype=jnp.float32)
        lim_r = np.sqrt(6.0 / (D + E)).astype(np.float32)
        w_r = jax.random.uniform(ks[1], (E, D), dtype=jnp.float32, minval=-lim_r, maxval=lim_r)
        b_r = jnp.zeros((E,), dtype=jnp.float32)
        lim1 = np.sqrt(6.0 / (D + Dh)).astype(np.float32)
        W1 = jax.random.uniform(ks[2], (E, D, Dh), dtype=jnp.float32, minval=-lim1, maxval=lim1)
        b1 = jnp.zeros((E, Dh), dtype=jnp.float32)
        W2 = jax.random.uniform(ks[3], (E, Dh, D), dtype=jnp.float32, minval=-lim1, maxval=lim1)
        b2 = jnp.zeros((E, D), dtype=jnp.float32)
        return {'x': x, 'ln_g': ln_g, 'ln_b': ln_b, 'w_r': w_r, 'b_r': b_r, 'W1': W1, 'b1': b1, 'W2': W2, 'b2': b2}
    _L1_ffn_all = _L1_ffn_setup()
    _L1_ffn_in = {k: v for k, v in _L1_ffn_all.items() if k in ('ln_g', 'ln_b', 'w_r', 'b_r', 'W1', 'b1', 'W2', 'b2')}
    del _L1_ffn_all
    return {'x': x, 'src': src, 'dst': dst, 'edge_weight': edge_weight, 'L0_gnn_W_self': _L0_gnn_in['W_self'], 'L0_gnn_W_neigh': _L0_gnn_in['W_neigh'], 'L0_gnn_bias': _L0_gnn_in['bias'], 'L0_gnn_gamma': _L0_gnn_in['gamma'], 'L0_gnn_beta': _L0_gnn_in['beta'], 'L0_mix_Wq': _L0_mix_in['Wq'], 'L0_mix_bq': _L0_mix_in['bq'], 'L0_mix_Wk': _L0_mix_in['Wk'], 'L0_mix_bk': _L0_mix_in['bk'], 'L0_mix_Wv': _L0_mix_in['Wv'], 'L0_mix_bv': _L0_mix_in['bv'], 'L0_mix_Wo': _L0_mix_in['Wo'], 'L0_mix_bo': _L0_mix_in['bo'], 'L0_mix_W1': _L0_mix_in['W1'], 'L0_mix_b1': _L0_mix_in['b1'], 'L0_mix_W2': _L0_mix_in['W2'], 'L0_mix_b2': _L0_mix_in['b2'], 'L0_mix_g1': _L0_mix_in['g1'], 'L0_mix_be1': _L0_mix_in['be1'], 'L0_mix_g2': _L0_mix_in['g2'], 'L0_mix_be2': _L0_mix_in['be2'], 'L0_ffn_Wg': _L0_ffn_in['Wg'], 'L0_ffn_bg': _L0_ffn_in['bg'], 'L0_ffn_We': _L0_ffn_in['We'], 'L0_ffn_be': _L0_ffn_in['be'], 'L1_gnn_W_conv': _L1_gnn_in['W_conv'], 'L1_gnn_b_conv': _L1_gnn_in['b_conv'], 'L1_gnn_W_lin': _L1_gnn_in['W_lin'], 'L1_gnn_b_lin': _L1_gnn_in['b_lin'], 'L1_mix_Wq': _L1_mix_in['Wq'], 'L1_mix_bq': _L1_mix_in['bq'], 'L1_mix_Wk': _L1_mix_in['Wk'], 'L1_mix_bk': _L1_mix_in['bk'], 'L1_mix_Wv': _L1_mix_in['Wv'], 'L1_mix_bv': _L1_mix_in['bv'], 'L1_mix_Wo': _L1_mix_in['Wo'], 'L1_mix_bo': _L1_mix_in['bo'], 'L1_mix_temperature': _L1_mix_in['temperature'], 'L1_ffn_ln_g': _L1_ffn_in['ln_g'], 'L1_ffn_ln_b': _L1_ffn_in['ln_b'], 'L1_ffn_w_r': _L1_ffn_in['w_r'], 'L1_ffn_b_r': _L1_ffn_in['b_r'], 'L1_ffn_W1': _L1_ffn_in['W1'], 'L1_ffn_b1': _L1_ffn_in['b1'], 'L1_ffn_W2': _L1_ffn_in['W2'], 'L1_ffn_b2': _L1_ffn_in['b2']}

def reference(x, src, dst, edge_weight, L0_gnn_W_self, L0_gnn_W_neigh, L0_gnn_bias, L0_gnn_gamma, L0_gnn_beta, L0_mix_Wq, L0_mix_bq, L0_mix_Wk, L0_mix_bk, L0_mix_Wv, L0_mix_bv, L0_mix_Wo, L0_mix_bo, L0_mix_W1, L0_mix_b1, L0_mix_W2, L0_mix_b2, L0_mix_g1, L0_mix_be1, L0_mix_g2, L0_mix_be2, L0_ffn_Wg, L0_ffn_bg, L0_ffn_We, L0_ffn_be, L1_gnn_W_conv, L1_gnn_b_conv, L1_gnn_W_lin, L1_gnn_b_lin, L1_mix_Wq, L1_mix_bq, L1_mix_Wk, L1_mix_bk, L1_mix_Wv, L1_mix_bv, L1_mix_Wo, L1_mix_bo, L1_mix_temperature, L1_ffn_ln_g, L1_ffn_ln_b, L1_ffn_w_r, L1_ffn_b_r, L1_ffn_W1, L1_ffn_b1, L1_ffn_W2, L1_ffn_b2):
    import jax
    import jax.numpy as jnp

    def _L0_gnn_ref(x, edge_src, edge_dst, deg, W_self, W_neigh, bias, gamma, beta):
        import jax, jax.numpy as jnp
        import numpy as np
        N_NODES = 1250
        N_EDGES = 20000
        IN_DIM = 512
        OUT_DIM = 512
        LN_EPS = 1e-05
        n = x.shape[0]
        h_self = jnp.einsum('nd,od->no', x, W_self)
        neigh_sum = jax.ops.segment_sum(x[edge_src], edge_dst, num_segments=n)
        neigh_mean = neigh_sum / jnp.maximum(deg, 1.0)[:, None]
        h_neigh = jnp.einsum('nd,od->no', neigh_mean, W_neigh)
        h = h_self + h_neigh + bias
        mu = jnp.mean(h, axis=-1, keepdims=True)
        var = jnp.mean(jnp.square(h - mu), axis=-1, keepdims=True)
        h = (h - mu) * jax.lax.rsqrt(var + LN_EPS)
        return h * gamma + beta

    def _L0_mix_ref(x, Wq, bq, Wk, bk, Wv, bv, Wo, bo, W1, b1, W2, b2, g1, be1, g2, be2):
        import jax, jax.numpy as jnp
        import numpy as np
        EPS = 1e-06
        H = 8
        DH = 64
        LN_EPS = 1e-05

        def _layernorm(x, g, b):
            m = jnp.mean(x, axis=-1, keepdims=True)
            v = jnp.mean(jnp.square(x - m), axis=-1, keepdims=True)
            return (x - m) / jnp.sqrt(v + LN_EPS) * g + b

        def _flow_attention(x, Wq, bq, Wk, bk, Wv, bv, Wo, bo):
            B, L, D = x.shape
            S = L
            q = jax.nn.sigmoid((x @ Wq + bq).reshape(B, L, H, DH).transpose(0, 2, 1, 3))
            k = jax.nn.sigmoid((x @ Wk + bk).reshape(B, S, H, DH).transpose(0, 2, 1, 3))
            v = (x @ Wv + bv).reshape(B, S, H, DH).transpose(0, 2, 1, 3)
            sink_incoming = 1.0 / jnp.einsum('nhld,nhd->nhl', q + EPS, k.sum(axis=2) + EPS)
            source_outgoing = 1.0 / jnp.einsum('nhld,nhd->nhl', k + EPS, q.sum(axis=2) + EPS)
            conserved_sink = jnp.einsum('nhld,nhd->nhl', q + EPS, (k * source_outgoing[..., None]).sum(axis=2) + EPS)
            conserved_source = jnp.einsum('nhld,nhd->nhl', k + EPS, (q * sink_incoming[..., None]).sum(axis=2) + EPS)
            conserved_source = jnp.clip(conserved_source, -1.0, 1.0)
            sink_allocation = jax.nn.sigmoid(conserved_sink * (float(L) / float(S)))
            source_competition = jax.nn.softmax(conserved_source, axis=-1) * float(S)
            kv = jnp.einsum('nhld,nhlm->nhdm', k, v * source_competition[..., None])
            o = jnp.einsum('nhld,nhdm->nhlm', q * sink_incoming[..., None], kv)
            o = o * sink_allocation[..., None]
            o = o.transpose(0, 2, 1, 3).reshape(B, L, D)
            return o @ Wo + bo
        sa = _flow_attention(_layernorm(x, g1, be1), Wq, bq, Wk, bk, Wv, bv, Wo, bo)[0]
        x = x + sa
        h = _layernorm(x, g2, be2)
        h = jax.nn.gelu(h @ W1 + b1, approximate=False) @ W2 + b2
        return x + h

    def _L0_ffn_ref(x, Wg, bg, We, be):
        import jax, jax.numpy as jnp
        import numpy as np
        B, S, D, E, O = (1024, 256, 512, 16, 512)
        scores = jax.nn.softmax(jnp.mean(x, axis=1) @ Wg + bg, axis=-1)
        idx = jnp.argmax(scores, axis=-1)
        gate = jnp.take_along_axis(scores, idx[:, None], axis=-1)
        W_sel = We[idx]
        b_sel = be[idx]
        y = jnp.einsum('bsd,bdo->bso', x, W_sel) + b_sel[:, None, :]
        return gate[:, :, None] * y

    def _L1_gnn_ref(x, edge_index, edge_weight, W_conv, b_conv, W_lin, b_lin):
        import jax, jax.numpy as jnp
        import numpy as np
        N = 6250
        E = 200000
        F_IN = 512
        H = 128
        n = x.shape[0]
        src, dst = (edge_index[0], edge_index[1])
        loop = jnp.arange(n, dtype=edge_index.dtype)
        src_f = jnp.concatenate([src, loop])
        dst_f = jnp.concatenate([dst, loop])
        w = jnp.concatenate([edge_weight, jnp.ones((n,), x.dtype)])
        deg = jax.ops.segment_sum(w, dst_f, num_segments=n)
        dinv = jnp.where(deg > 0, jax.lax.rsqrt(deg), 0.0)
        norm = dinv[src_f] * w * dinv[dst_f]
        h = x @ W_conv
        agg = jax.ops.segment_sum(h[src_f] * norm[:, None], dst_f, num_segments=n) + b_conv
        return agg @ W_lin + b_lin

    def _L1_mix_ref(query, Wq, bq, Wk, bk, Wv, bv, Wo, bo, temperature):
        import jax, jax.numpy as jnp
        import numpy as np
        N, B, C, H = (512, 8, 512, 8)
        D = C // H
        EPS = 1e-06

        def _dot(a, b):
            return jnp.einsum('bhsd,bhd->bhs', a, b)
        n, b, c = query.shape
        q = (query @ Wq + bq).reshape(n, b, H, D).transpose(1, 2, 0, 3)
        k = (query @ Wk + bk).reshape(n, b, H, D).transpose(1, 2, 0, 3)
        v = (query @ Wv + bv).reshape(n, b, H, D).transpose(1, 2, 0, 3)
        q = jax.nn.sigmoid(q)
        k = jax.nn.sigmoid(k)
        hw = k.shape[2]
        sink_incoming = 1.0 / (_dot(q + EPS, k.sum(axis=2) + EPS) + EPS)
        source_outgoing = 1.0 / (_dot(k + EPS, q.sum(axis=2) + EPS) + EPS)
        conserved_sink = _dot(q + EPS, (k * source_outgoing[..., None]).sum(axis=2) + EPS) + EPS
        conserved_source = _dot(k + EPS, (q * sink_incoming[..., None]).sum(axis=2) + EPS) + EPS
        conserved_source = jnp.clip(conserved_source, -1.0, 1.0)
        sink_allocation = jax.nn.sigmoid(conserved_sink * (float(n) / float(hw)))
        source_competition = jax.nn.softmax(conserved_source / temperature, axis=-1) * float(c)
        kv = jnp.einsum('bhsd,bhse->bhde', k, v * source_competition[..., None])
        out_update = jnp.einsum('bhnd,bhde->bhne', q, kv)
        out_update = out_update * sink_incoming[..., None] * sink_allocation[..., None]
        out = out_update.reshape(b, n, c)
        out = out @ Wo + bo
        out = out.transpose(1, 0, 2)
        return query + out

    def _L1_ffn_ref(x, ln_g, ln_b, w_r, b_r, W1, b1, W2, b2):
        import jax, jax.numpy as jnp
        import numpy as np
        D = 512
        E = 8
        K = 2
        EXP = 4
        LN_EPS = 1e-05
        B, T, d = x.shape
        mu = jnp.mean(x, axis=-1, keepdims=True)
        var = jnp.mean(jnp.square(x - mu), axis=-1, keepdims=True)
        h = (x - mu) * jax.lax.rsqrt(var + LN_EPS) * ln_g + ln_b
        logits = jnp.einsum('btd,ed->bte', h, w_r) + b_r
        topk_vals, topk_idx = jax.lax.top_k(logits, K)
        gates = jax.nn.softmax(topk_vals, axis=-1)
        hf = h.reshape(B * T, d)
        hid = jax.nn.gelu(jnp.einsum('nd,edf->nef', hf, W1) + b1, approximate=False)
        expert_stack = jnp.einsum('nef,efd->ned', hid, W2) + b2
        idx_flat = topk_idx.reshape(B * T, K)
        gates_flat = gates.reshape(B * T, K)
        gathered = jnp.take_along_axis(expert_stack, idx_flat[:, :, None], axis=1)
        mixed = jnp.sum(gathered * gates_flat[:, :, None], axis=1).reshape(B, T, d)
        return x + mixed
    edge_index = jnp.stack([src, dst])
    deg = jnp.maximum(jax.ops.segment_sum(jnp.ones(dst.shape, jnp.float32), dst, num_segments=1250), 1.0)
    xn = _layernorm(x, axis=-1)
    x = x + _L0_gnn_ref(xn, src, dst, deg, L0_gnn_W_self, L0_gnn_W_neigh, L0_gnn_bias, L0_gnn_gamma, L0_gnn_beta) + _L0_mix_ref(xn[None], L0_mix_Wq, L0_mix_bq, L0_mix_Wk, L0_mix_bk, L0_mix_Wv, L0_mix_bv, L0_mix_Wo, L0_mix_bo, L0_mix_W1, L0_mix_b1, L0_mix_W2, L0_mix_b2, L0_mix_g1, L0_mix_be1, L0_mix_g2, L0_mix_be2)[0]
    x = x + _L0_ffn_ref(_layernorm(x, axis=-1)[None], L0_ffn_Wg, L0_ffn_bg, L0_ffn_We, L0_ffn_be)[0]
    xn = _layernorm(x, axis=-1)
    x = x + _L1_gnn_ref(xn, edge_index, edge_weight, L1_gnn_W_conv, L1_gnn_b_conv, L1_gnn_W_lin, L1_gnn_b_lin) + _L1_mix_ref(xn[None], L1_mix_Wq, L1_mix_bq, L1_mix_Wk, L1_mix_bk, L1_mix_Wv, L1_mix_bv, L1_mix_Wo, L1_mix_bo, L1_mix_temperature)[0]
    x = x + _L1_ffn_ref(_layernorm(x, axis=-1)[None], L1_ffn_ln_g, L1_ffn_ln_b, L1_ffn_w_r, L1_ffn_b_r, L1_ffn_W1, L1_ffn_b1, L1_ffn_W2, L1_ffn_b2)[0]
    return x

_drawn_inputs = setup_inputs


def setup_inputs(seed=0):
    import zlib

    import numpy as np

    out = dict(_drawn_inputs(seed))
    spreads = {'L0_gnn_bias': (0.0, 0.1),
     'L0_gnn_gamma': (1.0, 0.2),
     'L0_gnn_beta': (0.0, 0.1),
     'L0_mix_bq': (0.0, 2.0),
     'L0_mix_bk': (0.0, 2.0),
     'L0_mix_bv': (0.0, 0.281),
     'L0_mix_bo': (0.0, 0.1),
     'L0_mix_b1': (0.0, 0.8),
     'L0_mix_b2': (0.0, 0.1),
     'L0_mix_g1': (1.0, 0.6),
     'L0_mix_be1': (0.0, 0.8),
     'L0_mix_g2': (1.0, 0.6),
     'L0_mix_be2': (0.0, 0.8),
     'L1_gnn_b_conv': (0.0, 0.8),
     'L1_gnn_b_lin': (0.0, 2.0),
     'L1_mix_bq': (0.0, 2.0),
     'L1_mix_bk': (0.0, 2.0),
     'L1_mix_bv': (0.0, 0.1),
     'L1_mix_bo': (0.0, 2.0),
     'L1_ffn_ln_g': (1.0, 0.6),
     'L1_ffn_ln_b': (0.0, 0.8),
     'L1_ffn_b_r': (0.0, 2.0),
     'L1_ffn_b1': (0.0, 0.8),
     'L1_ffn_b2': (0.0, 2.0)}
    factors = {'edge_weight': 8.0,
     'L0_mix_Wq': 40.325,
     'L0_mix_Wk': 43.922,
     'L0_mix_Wv': 3.08,
     'L0_ffn_Wg': 3.378,
     'L0_ffn_bg': 3.374,
     'L0_ffn_We': 3.341,
     'L0_ffn_be': 8.0,
     'L1_gnn_W_conv': 8.0,
     'L1_gnn_W_lin': 8.0,
     'L1_mix_Wq': 64.0,
     'L1_mix_Wk': 64.0,
     'L1_ffn_w_r': 8.0,
     'L1_ffn_W1': 8.0,
     'L1_ffn_W2': 8.0}
    for name, (base, spread) in spreads.items():
        noise = np.random.default_rng([zlib.crc32(name.encode()), seed]).standard_normal(out[name].shape)
        drawn = base * np.exp(spread * noise) if base else spread * noise
        out[name] = jnp.asarray(drawn.astype(out[name].dtype))
    for name, factor in factors.items():
        out[name] = (out[name] * factor).astype(out[name].dtype)
    return out
```

```python
from contextlib import ExitStack, contextmanager

import concourse.bass as bass
from concourse import mybir

ALU = mybir.AluOpType
ACT = mybir.ActivationFunctionType
F32 = mybir.dt.float32
F32R = mybir.dt.float32r
I32 = mybir.dt.int32
U32 = mybir.dt.uint32
AX_X = mybir.AxisListType.X

P = 128
D = 512
KD = D // P
NODES = 1250
NT = 125
T = NODES // NT
HEADS, DH = 8, 64
LN_EPS = 1e-5
FLOW_EPS = 1e-6

EDGES = 40000
EP = EDGES // NT
BUCKET = 32
NB = -(-NODES // BUCKET)
GROUP = 256
NG = (EDGES + NB * (GROUP - 1)) // GROUP
NG += NG % 2
CHUNKS = GROUP // P
SLOTS_PER_P = NG * CHUNKS
ONE_HOT = T * BUCKET
DST = NB * BUCKET

EXPERTS_0 = 16
EXPERTS = 8
DFF = 2048
GCN = 128
SLOT_TILES = (2 * NODES + EXPERTS * (P - 1)) // P


class Steps:

    def __init__(self, engine, semaphore):
        self.engine, self.semaphore = engine, semaphore
        self.before, self.done, self.round, self.per_round = 0, 0, None, 0

    def count(self):
        if self.round is None:
            return self.before + self.done
        return self.round * self.per_round + (self.before + self.done)

    def step(self, instruction):
        instruction.then_inc(self.semaphore, 1)
        self.done += 1

    def settle(self):
        self.engine.wait_ge(self.semaphore, self.count())

    def link(self, instruction):
        self.step(instruction)
        self.settle()

    @contextmanager
    def rounds(self, n, per_round):
        self.before, self.done = self.before + self.done, 0
        with self.engine.Fori(0, n) as j:
            self.round, self.per_round = j, per_round
            yield j
            assert self.done == per_round, (self.done, per_round)
        self.before, self.done, self.round = self.before + n * per_round, 0, None


def staggered(steps, per_round, first, second, third, n=T):
    first(0, 0)
    first(1, 1)
    second(0, 0)
    first(2, 0)
    second(1, 1)
    third(0, 0)
    rounds = (n - 4) // 2
    with steps.rounds(rounds, per_round) as j:
        for u in range(2):
            t = j * 2 + (u + 2)
            first(t + 1, 1 - u)
            second(t, u)
            third(t - 1, 1 - u)
    for t in range(2 + 2 * rounds, n):
        if t + 1 < n:
            first(t + 1, (t + 1) % 2)
        second(t, t % 2)
        third(t - 1, (t - 1) % 2)
    third(n - 1, (n - 1) % 2)


def nothing(t, u):
    pass


def is_tile(t, n):
    return isinstance(t, int) and t == n


def tile(a, t):
    return a[0:NT, t, :] if isinstance(t, int) else a[0:NT, bass.ds(t, 1), :].squeeze(1)


def column(a, t):
    return a[0:NT, t:t + 1] if isinstance(t, int) else a[0:NT, bass.ds(t, 1)]


def heads(a):
    return a.rearrange("p (h d) -> p h d", h=HEADS)


def over_head(a):
    return a.unsqueeze(2).broadcast_to([NT, HEADS, DH])


class Memory:

    def __init__(self, nc, stack, prefix=""):
        self.nc, self.stack, self.prefix, self.numbers = nc, stack, prefix, []
        if prefix:
            stack.callback(self.clear)

    def sb(self, name, shape, dtype=F32):
        return self.stack.enter_context(self.nc.sbuf_tensor(self.prefix + name, shape, dtype))

    def psum(self, name, shape, dtype=F32):
        return self.stack.enter_context(self.nc.psum_tensor(self.prefix + name, shape, dtype))

    def sem(self, name):
        semaphore = self.stack.enter_context(self.nc.semaphore(self.prefix + name))
        self.numbers.append(semaphore.num)
        return semaphore

    def clear(self):
        first = self.numbers[0]
        for i, number in enumerate(self.numbers):
            if i + 1 == len(self.numbers) or self.numbers[i + 1] != number + 1:
                self.nc.gpsimd.sem_clear(range(first, number + 1))
                first = self.numbers[min(i + 1, len(self.numbers) - 1)]


class Norm:

    def __init__(self, m, name):
        self.stats = m.sb(name + "_stats", [P, T, 6])
        self.mean, self.diff, self.var, self.std, self.rstd = (
            m.sb(f"{name}_{n}", [P, T]) for n in ("mean", "diff", "var", "std", "rstd"))
        self.var_ready = m.sem(name + "_var_ready")
        self.std_ready = m.sem(name + "_std_ready")

    def tile_stats(self, x, t):
        return self.stats[0:NT, t, :] if isinstance(t, int) else self.stats[0:NT, bass.ds(t, 1), :].squeeze(1)

    def all_stats(self, nc, steps, x):
        with steps.rounds(T // 2, 2) as j:
            for u in range(2):
                t = j * 2 + u
                steps.step(nc.vector.bn_stats(tile(self.stats, t), tile(x, t)))
        steps.settle()

    def variance(self, nc, steps):
        st, r = self.stats[0:NT], slice(0, NT)
        steps.step(nc.vector.tensor_tensor(self.mean[r, :], st[:, :, 1], st[:, :, 4], ALU.add))
        steps.step(nc.vector.tensor_tensor(self.diff[r, :], st[:, :, 1], st[:, :, 4], ALU.subtract))
        steps.link(nc.vector.tensor_tensor(self.var[r, :], st[:, :, 2], st[:, :, 5], ALU.add))
        steps.step(nc.vector.tensor_scalar(self.mean[r, :], self.mean[r, :], 0.5, None, ALU.mult))
        steps.step(nc.vector.tensor_tensor(self.diff[r, :], self.diff[r, :], self.diff[r, :], ALU.mult))
        steps.link(nc.vector.tensor_scalar(self.var[r, :], self.var[r, :], 1.0 / D, LN_EPS, ALU.mult, ALU.add))
        nc.vector.scalar_tensor_tensor(self.var[r, :], self.diff[r, :], 0.25, self.var[r, :],
                                       ALU.mult, ALU.add).then_inc(self.var_ready, 1)
        steps.engine.wait_ge(self.std_ready, 1)
        steps.link(nc.vector.reciprocal(self.rstd[r, :], self.std[r, :]))
        steps.link(nc.vector.tensor_tensor(self.std[r, :], self.rstd[r, :], self.rstd[r, :], ALU.mult))
        steps.link(nc.vector.tensor_tensor(self.std[r, :], self.std[r, :], self.var[r, :], ALU.mult))
        steps.link(nc.vector.tensor_scalar(self.std[r, :], self.std[r, :], -0.5, 1.5, ALU.mult, ALU.add))
        steps.link(nc.vector.tensor_tensor(self.rstd[r, :], self.rstd[r, :], self.std[r, :], ALU.mult))

    def root(self, nc, act):
        act.wait_ge(self.var_ready, 1)
        nc.scalar.activation(self.std[0:NT, :], self.var[0:NT, :], ACT.Sqrt).then_inc(self.std_ready, 1)

    def apply(self, nc, out, x, t):
        return nc.vector.tensor_scalar(out, x, column(self.mean, t), column(self.rstd, t),
                                       ALU.subtract, ALU.mult)


def edge_positions(nc, A, g):
    with ExitStack() as stack:
        m = Memory(nc, stack, "ep_")
        src_i, dst_i = m.sb("src_i", [P, EP], I32), m.sb("dst_i", [P, EP], I32)
        weight = m.sb("weight", [P, EP])
        bucket_i, low_i = m.sb("bucket_i", [P, EP], I32), m.sb("low_i", [P, EP], I32)
        bucket, low, block, rank = (m.sb(n, [P, EP]) for n in ("bucket", "low", "block", "rank"))
        high_r = m.sb("high_r", [P, EP], F32R)
        bucket_no, in_buckets = m.sb("bucket_no", [P, NB]), m.sb("in_buckets", [P, 8, EP])
        ones_e = m.sb("ones_e", [P, EP])
        counts, totals_f, groups_f, ends = (m.sb(n, [P, NB]) for n in ("counts", "totals_f", "groups_f", "ends"))
        totals_i = m.sb("totals_i", [P, NB], I32)
        first_rank, ones_b = m.sb("first_rank", [P, NB]), m.sb("ones_b", [P, NB])
        member, running, placed = m.sb("member", [P, 2, EP]), m.sb("running", [P, 2, EP]), m.sb("placed", [P, 2, EP])
        before = m.sb("before", [P, P])
        group_no, past = m.sb("group_no", [P, 2]), m.sb("past", [P, 2, NB])
        group_bucket = m.sb("group_bucket", [P, 2])
        fill, zeros = m.sb("fill", [P, SLOTS_PER_P, 4]), m.sb("zeros", [P, D])
        ps_before, ps_total = m.psum("ps_before", [P, NB]), m.psum("ps_total", [P, NB])
        ps_table = m.psum("ps_table", [P, 2 * NG // 2])
        loaded = m.sem("loaded")
        made, table_ready = m.sem("made"), m.sem("table_ready")
        counted, summed, chain = m.sem("counted"), m.sem("summed"), m.sem("chain")
        filled = m.sem("filled")
        half = NG // 2
        block_ctx = stack.enter_context(nc.Block())

        @block_ctx.sync
        def _(sp):
            sp.dma_start(dst_i[0:NT, :], A["dst"].rearrange("(p e) -> p e", e=EP)).then_inc(loaded, 16)
            sp.dma_start(src_i[0:NT, :], A["src"].rearrange("(p e) -> p e", e=EP)).then_inc(loaded, 16)
            sp.dma_start(weight[0:NT, :], A["edge_weight"].rearrange("(p e) -> p e", e=EP)).then_inc(loaded, 16)
            sp.dma_start(g.x[0:NT], A["x"].rearrange("(t p) d -> p t d", p=NT)).then_inc(g.x_loaded, 16)
            sp.wait_ge(made, 7)
            sp.dma_start(g.sorted_edges.rearrange("(p s) f -> p s f", p=P), fill[:]).then_inc(filled, 16)
            sp.dma_start(g.slot_rows.rearrange("(n p) d -> p n d", p=P),
                         zeros[:].unsqueeze(1).broadcast_to([P, g.slot_tiles, D])).then_inc(filled, 16)
            sp.wait_ge(filled, 32)
            sp.wait_ge(g.x_loaded, 16)

        @block_ctx.gpsimd
        def _(pool):
            nc.gpsimd.memset(g.ones[:], 1.0).then_inc(made, 1)
            nc.gpsimd.memset(g.ident[:], 0.0).then_inc(made, 1)
            nc.gpsimd.iota(bucket_no[:], pattern=[[1, NB]], base=0, channel_multiplier=0,
                           allow_small_or_imprecise_dtypes=True).then_inc(made, 1)
            nc.gpsimd.memset(fill[:], -1.0).then_inc(made, 1)
            nc.gpsimd.memset(zeros[:], 0.0).then_inc(made, 1)
            pool.wait_ge(made, 2)
            nc.gpsimd.affine_select(out=g.ident[:], in_=g.ident[:], compare_op=ALU.not_equal, fill=1.0, base=0,
                                    pattern=[[-1, P]], channel_multiplier=1).then_inc(made, 1)
            nc.gpsimd.affine_select(out=before[:], in_=g.ones[:], compare_op=ALU.is_gt, fill=0.0, base=0,
                                    pattern=[[1, P]], channel_multiplier=-1).then_inc(made, 1)
            nc.gpsimd.affine_select(out=g.before[:], in_=g.ones[:], compare_op=ALU.is_gt, fill=0.0, base=0,
                                    pattern=[[1, P]], channel_multiplier=-1).then_inc(made, 1)
            nc.gpsimd.iota(g.iota[:], pattern=[[1, ONE_HOT]], base=0, channel_multiplier=0,
                           allow_small_or_imprecise_dtypes=True).then_inc(made, 1)
            nc.gpsimd.iota(group_no[:], pattern=[[half, 2]], base=0, channel_multiplier=1,
                           allow_small_or_imprecise_dtypes=True).then_inc(made, 1)
            pool.wait_ge(made, 10)

        @block_ctx.vector
        def _(dve):
            c = Steps(dve, chain)
            r = slice(0, NT)
            v = nc.vector
            dve.wait_ge(loaded, 48)
            c.step(v.memset(ones_e[:], 1.0))
            c.step(v.memset(ones_b[:], 1.0))
            c.step(v.memset(block[:], 0.0))
            c.step(v.memset(rank[:], -1.0))
            c.step(v.tensor_scalar(bucket_i[r, :], dst_i[r, :], 5, None, ALU.logical_shift_right))
            c.link(v.tensor_scalar(low_i[r, :], dst_i[r, :], BUCKET - 1, None, ALU.bitwise_and))
            c.link(v.tensor_copy(bucket[r, :], bucket_i[r, :]))
            dve.wait_ge(made, 10)
            for b in range(0, NB, 8):
                c.link(v.tensor_tensor(in_buckets[r], bucket[r, :].unsqueeze(1).broadcast_to([NT, 8, EP]),
                                       bucket_no[r, b:b + 8].unsqueeze(2).broadcast_to([NT, 8, EP]), ALU.is_equal))
                if b == NB - 8:
                    v.reduce_sum(counts[r, b:b + 8], in_buckets[r], AX_X).then_inc(counted, 1)
                else:
                    c.link(v.reduce_sum(counts[r, b:b + 8], in_buckets[r], AX_X))
            src_f = placed[r, 0, :]
            c.step(v.tensor_copy(low[r, :], low_i[r, :]))
            c.link(v.tensor_copy(src_f, src_i[r, :]))
            for n in range(1, T):
                c.link(v.scalar_tensor_tensor(block[r, :], src_f, float(NT * n), block[r, :], ALU.is_ge, ALU.add))
            c.step(v.scalar_tensor_tensor(g.records[r, :, 0], block[r, :], -float(NT), src_f, ALU.mult, ALU.add))
            c.step(v.scalar_tensor_tensor(g.records[r, :, 1], block[r, :], float(BUCKET), low[r, :], ALU.mult, ALU.add))
            c.link(v.tensor_copy(high_r[r, :], weight[r, :]))
            c.step(v.tensor_copy(g.records[r, :, 2], high_r[r, :]))
            c.link(v.tensor_tensor(g.records[r, :, 3], weight[r, :], high_r[r, :], ALU.subtract))
            dve.wait_ge(summed, 2)
            c.link(v.tensor_scalar(totals_f[r, :], ps_total[r, :], float(GROUP - 1), None, ALU.add))
            c.link(v.tensor_copy(totals_i[r, :], totals_f[r, :]))
            c.link(v.tensor_scalar(totals_i[r, :], totals_i[r, :], 8, None, ALU.logical_shift_right))
            c.link(v.tensor_copy(groups_f[r, :], totals_i[r, :]))
            c.link(v.tensor_tensor_scan(ends[r, :], ones_b[r, :], groups_f[r, :], 0.0, ALU.mult, ALU.add))
            c.link(v.tensor_tensor(first_rank[r, :], ends[r, :], groups_f[r, :], ALU.subtract))
            c.link(v.scalar_tensor_tensor(first_rank[r, :], first_rank[r, :], float(GROUP), ps_before[r, :],
                                          ALU.mult, ALU.add))
            for h in range(2):
                c.link(v.tensor_scalar(past[0:half, h, :], ends[0:half, :], group_no[0:half, h:h + 1], None, ALU.is_le))
            c.link(v.reduce_sum(group_bucket[0:half, :], past[0:half], AX_X))
            v.tensor_scalar(group_bucket[0:half, :], group_bucket[0:half, :], float(NB - 1), float(BUCKET),
                            ALU.min, ALU.mult).then_inc(table_ready, 1)
            with c.rounds(NB // 2, 8) as j:
                for u in range(2):
                    c.step(v.tensor_scalar(member[r, u, :], bucket[r, :], bucket_no[r, bass.ds(j * 2 + u, 1)], None,
                                           ALU.is_equal))
                c.settle()
                for u in range(2):
                    c.step(v.tensor_tensor_scan(running[r, u, :], ones_e[r, :], member[r, u, :],
                                                first_rank[r, bass.ds(j * 2 + u, 1)], ALU.mult, ALU.add))
                c.settle()
                for u in range(2):
                    c.step(v.tensor_tensor(placed[r, u, :], running[r, u, :], member[r, u, :], ALU.mult))
                c.settle()
                for u in range(2):
                    c.link(v.tensor_tensor(rank[r, :], rank[r, :], placed[r, u, :], ALU.add))
            c.link(v.tensor_copy(dst_i[r, :], rank[r, :]))
            c.step(v.tensor_scalar(low_i[r, :], dst_i[r, :], P - 1, None, ALU.bitwise_and))
            c.link(v.tensor_scalar(bucket_i[r, :], dst_i[r, :], 7, None, ALU.logical_shift_right))
            c.link(v.scalar_tensor_tensor(g.edge_slot[r, :], low_i[r, :], float(SLOTS_PER_P), bucket_i[r, :],
                                          ALU.mult, ALU.add))
            dve.wait_ge(summed, 3)
            c.link(v.tensor_copy(g.group_offset[0:1, :], ps_table[0:1, :]))

        @block_ctx.tensor
        def _(pe):
            pe.wait_ge(made, 10)
            pe.wait_ge(counted, 1)
            pe.matmul(ps_before[0:NT, :], before[0:NT, 0:NT], counts[0:NT, :], start=True, stop=True).then_inc(summed, 1)
            pe.matmul(ps_total[0:NT, :], g.ones[0:NT, 0:NT], counts[0:NT, :], start=True, stop=True).then_inc(summed, 1)
            pe.wait_ge(table_ready, 1)
            for h in range(2):
                last = pe.matmul(ps_table[0:1, h * half:(h + 1) * half], group_bucket[0:half, h:h + 1],
                                 g.ident[0:half, 0:half], start=True, stop=True)
            last.then_inc(summed, 1)


class Shared:

    def __init__(self, nc, stack):
        m = Memory(nc, stack)
        self.x, self.xn = m.sb("x_rows", [P, T, D]), m.sb("xn_rows", [P, T, D])
        self.ones, self.ident = m.sb("ones", [P, P]), m.sb("ident", [P, P])
        self.before, self.iota = m.sb("before", [P, P]), m.sb("iota", [P, ONE_HOT])
        self.records = m.sb("records", [P, EP, 4])
        self.edge_slot = m.sb("edge_slot", [P, EP], U32)
        self.slots, self.gates = m.sb("slots", [P, 2, T], U32), m.sb("gates", [P, 2, T])
        self.dinv = m.sb("dinv", [P, T])
        self.group_offset = m.sb("group_offset", [1, NG], I32)
        self.x_loaded = m.sem("x_loaded")
        self.scattered, self.rows_scattered = m.sem("scattered"), m.sem("rows_scattered")
        self.gathered = [m.sem(f"gathered{t}") for t in range(T)]
        self.slot_tiles = SLOT_TILES
        self.sorted_edges = nc.dram_tensor("sorted_edges", (NG * GROUP, 4), F32).ap()
        self.slot_rows = nc.dram_tensor("slot_rows", (SLOT_TILES * P, D), F32).ap()
        self.slot_out = nc.dram_tensor("slot_out", (SLOT_TILES * P, D), F32).ap()
def load_matrix(sp, buffer, matrix, arrived):
    sp.dma_start(buffer[:], matrix.rearrange("(k p) n -> p k n", p=P)).then_inc(arrived, 16)


def load_row(sp, buffer, vector, arrived):
    sp.dma_start(buffer[:], vector.partition_broadcast(P)).then_inc(arrived, 16)


def flow_attention(nc, A, g):
    with ExitStack() as stack:
        m = Memory(nc, stack, "fa_")
        w = {n: m.sb(n, [P, KD, D]) for n in ("Wq", "Wk", "Wv", "Wo")}
        w1, w2 = m.sb("W1", [P, KD, 2 * P]), m.sb("W2", [P, 2, D])
        rows = {n: m.sb(n, [P, D]) for n in ("bq", "bk", "bv", "bo", "g1", "be1", "g2", "be2", "b2")}
        b1 = m.sb("b1", [P, 2])
        q, k, v_ = (m.sb(n, [P, T, D]) for n in ("q", "k", "v"))
        k_sum, q_sum = m.sb("k_sum", [P, D]), m.sb("q_sum", [P, D])
        work = m.sb("work", [P, 2, D])
        work2 = m.sb("work2", [P, 2, D])
        turned = m.sb("turned", [P, 2, KD, NT])
        hidden = m.sb("hidden", [P, 2, 2, NT])
        sink, source = m.sb("sink", [P, T, HEADS]), m.sb("source", [P, T, HEADS])
        to_sink, to_source = m.sb("to_sink", [P, T, HEADS]), m.sb("to_source", [P, T, HEADS])
        share, e_sum = m.sb("share", [P, T, HEADS]), m.sb("e_sum", [P, HEADS])
        kv_t = m.sb("kv_t", [P, KD, P])
        mixed_w = m.sb("mixed_w", [P, KD, D])
        n1, n2, n3 = Norm(m, "n1"), Norm(m, "n2"), Norm(m, "n3")
        ps_t = m.psum("ps_t", [P, 2, D])
        ps_a, ps_b, ps_c = (m.psum(n, [P, D]) for n in ("ps_a", "ps_b", "ps_c"))
        ps_k, ps_q = m.psum("ps_k", [P, D]), m.psum("ps_q", [P, D])
        ps_e = m.psum("ps_e", [P, HEADS])
        names = ("weights in_ready turned_out turned_ready q_done k_done v_done q_out k_out v_out q_ready k_ready "
                 "sums_done sums_out scaled_ready scaled_used sums2_done sums2_out allocated exponent clipped "
                 "w_ready w_used kv_done kv_out mix_done mix_out x1_ready "
                 "d_in d_turned d_ready d_done d_out f_in f_turned f_ready h_done h_ready f_done f_out chain")
        s = {n: m.sem(n) for n in names.split()}
        block = stack.enter_context(nc.Block())

        def out(ps, t_rows=NT):
            return ps[0:NT, :]

        @block.sync
        def _(sp):
            for n in ("Wq", "Wk", "Wv"):
                load_matrix(sp, w[n], A["L0_mix_" + n], s["weights"])
            for n in ("g1", "be1", "bq", "bk", "bv", "g2", "be2", "bo", "b2"):
                load_row(sp, rows[n], A["L0_mix_" + n], s["weights"])
            load_matrix(sp, w["Wo"], A["L0_mix_Wo"], s["weights"])
            load_matrix(sp, w1, A["L0_mix_W1"], s["weights"])
            load_matrix(sp, w2, A["L0_mix_W2"], s["weights"])
            sp.dma_start(b1[:], A["L0_mix_b1"].rearrange("(k p) -> p k", p=P), allow_slow_non_contiguous=True).then_inc(s["weights"], 16)
            sp.wait_ge(s["weights"], 16 * 16)

        @block.gpsimd
        def _(pool):
            for e in range(EP):
                nc.gpsimd.indirect_dma_start(
                    g.sorted_edges, bass.IndirectOffsetOnAxis(ap=g.edge_slot[0:NT, e:e + 1], axis=0),
                    g.records[0:NT, e, :], None).then_inc(g.scattered, 16)
            pool.wait_ge(g.scattered, 16 * EP)

        @block.vector
        def _(dve):
            v = nc.vector
            c = Steps(dve, s["chain"])
            r = slice(0, NT)
            dve.wait_ge(g.x_loaded, 16)
            n1.all_stats(nc, c, g.x)
            n1.variance(nc, c)
            with c.rounds(T // 2, 2) as j:
                for u in range(2):
                    t = j * 2 + u
                    c.step(n1.apply(nc, tile(g.xn, t), tile(g.x, t), t))
            c.settle()
            n2.all_stats(nc, c, g.xn)
            n2.variance(nc, c)
            dve.wait_ge(s["weights"], 16 * 16)

            def prepare(t, u):
                dve.wait_ge(s["turned_out"], t + 1)
                c.link(n2.apply(nc, work[r, u, :], tile(g.xn, t), t))
                c.link(v.tensor_tensor(work[r, u, :], work[r, u, :], rows["g1"][r, :], ALU.mult))
                v.tensor_tensor(work[r, u, :], work[r, u, :], rows["be1"][r, :], ALU.add).then_inc(s["in_ready"], 1)

            def add_biases(t, u):
                for name, ps, to in (("q", ps_a, q), ("k", ps_b, k), ("v", ps_c, v_)):
                    dve.wait_ge(s[name + "_done"], t + (3 if name == "v" else 1))
                    v.tensor_tensor(tile(to, t), out(ps), rows["b" + name][r, :], ALU.add).then_inc(s[name + "_out"], 1)

            staggered(c, 4, prepare, add_biases, nothing)

            def softened(ps, to):
                c.step(v.tensor_scalar(to[:], ps[:], FLOW_EPS, None, ALU.add))

            def dots(sink_to, source_to):
                with c.rounds(T // 2, 8) as j:
                    for u in range(2):
                        t = j * 2 + u
                        for buf, a, b_, to in ((work, q, k_sum, sink_to), (work2, k, q_sum, source_to)):
                            c.step(v.scalar_tensor_tensor(buf[r, u, :], tile(a, t), FLOW_EPS, b_[r, :], ALU.add, ALU.mult))
                    c.settle()
                    for u in range(2):
                        t = j * 2 + u
                        for buf, to in ((work, sink_to), (work2, source_to)):
                            c.step(v.reduce_sum(tile(to, t), heads(buf[r, u, :]), AX_X))
                    c.settle()

            dve.wait_ge(s["q_ready"], T)
            dve.wait_ge(s["k_ready"], T)
            dve.wait_ge(s["sums_done"], 1)
            softened(ps_k, k_sum)
            softened(ps_q, q_sum)
            c.settle()
            dots(sink, source)
            c.settle()
            c.step(v.reciprocal(sink[r], sink[r]))
            c.link(v.reciprocal(source[r], source[r]))

            with c.rounds(T // 2, 0) as j:
                for u in range(2):
                    t = j * 2 + u
                    dve.wait_ge(s["scaled_used"], t + 1)
                    v.tensor_tensor(heads(work[r, u, :]), heads(tile(q, t)), over_head(tile(sink, t)),
                                    ALU.mult).then_inc(s["scaled_ready"], 1)
                    v.tensor_tensor(heads(work2[r, u, :]), heads(tile(k, t)), over_head(tile(source, t)),
                                    ALU.mult).then_inc(s["scaled_ready"], 1)
            dve.wait_ge(s["sums2_done"], 1)
            softened(ps_k, k_sum)
            softened(ps_q, q_sum)
            c.settle()
            dots(to_sink, to_source)
            c.settle()
            v.tensor_scalar(to_source[r], to_source[r], -1.0, 1.0, ALU.max, ALU.min).then_inc(s["clipped"], 1)
            dve.wait_ge(s["exponent"], 2)
            c.link(v.tensor_tensor(sink[r], sink[r], to_sink[r], ALU.mult))

            with c.rounds(T // 2, 0) as j:
                for u in range(2):
                    t = j * 2 + u
                    dve.wait_ge(s["w_used"], t + 1)
                    v.tensor_tensor(heads(work[r, u, :]), heads(tile(v_, t)), over_head(tile(share, t)),
                                    ALU.mult).then_inc(s["w_ready"], 1)
            c.step(v.memset(kv_t[:], 0.0))
            dve.wait_ge(s["kv_done"], 1)
            c.link(v.reciprocal(e_sum[r, :], ps_e[r, :]))
            c.link(v.tensor_scalar(e_sum[r, :], e_sum[r, :], float(NODES), None, ALU.mult))
            c.step(v.tensor_tensor(sink[r], sink[r], e_sum[r, :].unsqueeze(1).broadcast_to([NT, T, HEADS]), ALU.mult))
            kv = ps_a[:].rearrange("p (k n) -> p k n", k=KD)
            v.tensor_copy(kv_t[0:DH, :, 0:DH], kv[0:DH, :, 0:DH]).then_inc(s["kv_out"], 1)
            v.tensor_copy(kv_t[DH:P, :, DH:P], kv[DH:P, :, DH:P]).then_inc(s["kv_out"], 1)
            c.settle()

            def scale_q(t, u):
                dve.wait_ge(s["d_turned"], t + 1)
                v.tensor_tensor(heads(work[r, u, :]), heads(tile(q, t)), over_head(tile(sink, t)),
                                ALU.mult).then_inc(s["d_in"], 1)

            def attended(t, u):
                dve.wait_ge(s["d_done"], t + 3)
                c.link(v.tensor_tensor(work2[r, u, :], out(ps_b), rows["bo"][r, :], ALU.add))
                v.tensor_tensor(tile(v_, t), work2[r, u, :], tile(g.xn, t), ALU.add).then_inc(s["d_out"], 1)

            staggered(c, 2, scale_q, attended, nothing)
            dve.wait_ge(s["d_out"], T + 1)
            n3.all_stats(nc, c, v_)
            n3.variance(nc, c)

            def prepare_ff(t, u):
                dve.wait_ge(s["f_turned"], t + 1)
                c.link(n3.apply(nc, work[r, u, :], tile(v_, t), t))
                c.link(v.tensor_tensor(work[r, u, :], work[r, u, :], rows["g2"][r, :], ALU.mult))
                v.tensor_tensor(work[r, u, :], work[r, u, :], rows["be2"][r, :], ALU.add).then_inc(s["f_in"], 1)

            def add_up(t, u):
                c.link(v.tensor_tensor(work2[r, u, :], tile(v_, t), rows["b2"][r, :], ALU.add))
                dve.wait_ge(s["f_done"], t + 3)
                v.tensor_tensor(work2[r, u, :], work2[r, u, :], ps_c[r, :], ALU.add).then_inc(s["f_out"], 1)
                dve.wait_ge(s["f_out"], t + 2)
                c.step(v.tensor_tensor(tile(g.x, t), tile(g.x, t), work2[r, u, :], ALU.add))

            staggered(c, 8, prepare_ff, nothing, add_up)
            c.settle()

        @block.scalar
        def _(act):
            n1.root(nc, act)
            n2.root(nc, act)

            def copy_turned(done, ready, used, t, u):
                act.wait_ge(done, t + 3)
                act.wait_ge(used, t + 1)
                nc.scalar.copy(turned[:, u].rearrange("p k n -> p (k n)"), ps_t[:, u, 0:KD * NT]).then_inc(ready, 1)

            def evacuate(t, u):
                copy_turned(s["turned_out"], s["turned_ready"], s["v_done"], t, u)

            def sigmoids(t, u):
                for name, to in (("q", q), ("k", k)):
                    act.wait_ge(s[name + "_out"], t + 2)
                    nc.scalar.activation(tile(to, t), tile(to, t), ACT.Sigmoid).then_inc(s[name + "_ready"], 1)

            a = Steps(act, s["allocated"])
            staggered(a, 0, evacuate, sigmoids, nothing)
            act.wait_ge(s["clipped"], 1)
            nc.scalar.activation(to_sink[0:NT], to_sink[0:NT], ACT.Sigmoid).then_inc(s["exponent"], 1)
            nc.scalar.activation(share[0:NT], to_source[0:NT], ACT.Exp).then_inc(s["exponent"], 1)
            for i in range(KD):
                act.wait_ge(s["mix_done"], i + 1)
                nc.scalar.copy(mixed_w[:, i, :], (ps_b, ps_c)[i % 2][:]).then_inc(s["mix_out"], 1)
            staggered(a, 0, lambda t, u: copy_turned(s["d_turned"], s["d_ready"], s["d_done"], t, u), nothing, nothing)
            n3.root(nc, act)

            def evacuate_ff(t, u):
                copy_turned(s["f_turned"], s["f_ready"], s["h_done"], t, u)

            def gelu(t, u):
                act.wait_ge(s["h_done"], t + 3)
                act.wait_ge(s["f_done"], t + 1)
                nc.scalar.activation(hidden[:, u, 0, :], ps_a[:, 0:NT], ACT.Gelu, bias=b1[:, 0:1]).then_inc(s["h_ready"], 1)
                nc.scalar.activation(hidden[:, u, 1, :], ps_b[:, 0:NT], ACT.Gelu, bias=b1[:, 1:2]).then_inc(s["h_ready"], 1)

            staggered(a, 0, evacuate_ff, gelu, nothing)

        @block.tensor
        def _(pe):
            for n in ("turned_out", "v_done", "scaled_used", "w_used", "d_turned", "d_done", "f_turned", "h_done", "f_done"):
                pe.sem_inc(s[n], 2)
            pe.sem_inc(s["q_out"], 1)
            pe.sem_inc(s["k_out"], 1)
            pe.sem_inc(s["v_out"], 1)
            pe.sem_inc(s["d_out"], 1)
            pe.sem_inc(s["f_out"], 1)
            pe.sem_inc(s["h_ready"], 2)
            pe.wait_ge(s["weights"], 16 * 16)
            b = Steps(pe, s["allocated"])
            ones = g.ones[0:NT, :]

            def turn(ready, done, source):
                def f(t, u):
                    pe.wait_ge(ready, t + 1)
                    for i in range(KD):
                        last = pe.transpose(ps_t[:, u, i * NT:(i + 1) * NT], source[0:NT, u, i * P:(i + 1) * P],
                                            g.ident[0:NT, 0:NT])
                    last.then_inc(done, 1)
                return f

            def linear(ps, u, weight):
                for i in range(KD):
                    last = pe.matmul(ps[0:NT, :], turned[:, u, i, :], weight[:, i, :], start=(i == 0), stop=(i == KD - 1))
                return last

            def project(t, u):
                pe.wait_ge(s["turned_ready"], t + 1)
                for name, ps in (("q", ps_a), ("k", ps_b), ("v", ps_c)):
                    pe.wait_ge(s[name + "_out"], t + 1)
                    linear(ps, u, w["W" + name]).then_inc(s[name + "_done"], 1)

            def add_sums(t, u):
                pe.wait_ge(s["q_ready"], t + 1)
                pe.matmul(ps_q[:], ones, tile(q, t), start=is_tile(t, 0), stop=is_tile(t, T - 1))
                pe.wait_ge(s["k_ready"], t + 1)
                last = pe.matmul(ps_k[:], ones, tile(k, t), start=is_tile(t, 0), stop=is_tile(t, T - 1))
                if is_tile(t, T - 1):
                    last.then_inc(s["sums_done"], 1)

            staggered(b, 0, turn(s["in_ready"], s["turned_out"], work), project, add_sums)

            def add_scaled(t, u):
                pe.wait_ge(s["scaled_ready"], t * 2 + 2)
                pe.matmul(ps_q[:], ones, work[0:NT, u, :], start=is_tile(t, 0), stop=is_tile(t, T - 1))
                pe.matmul(ps_k[:], ones, work2[0:NT, u, :], start=is_tile(t, 0),
                          stop=is_tile(t, T - 1)).then_inc(s["scaled_used"], 1)
                if is_tile(t, T - 1):
                    pe.wait_ge(s["scaled_used"], T + 2)
                    pe.sem_inc(s["sums2_done"], 1)

            staggered(b, 0, nothing, add_scaled, nothing)

            def products(t, u):
                pe.wait_ge(s["w_ready"], t + 1)
                pe.matmul(ps_e[:], ones, tile(share, t), start=is_tile(t, 0), stop=is_tile(t, T - 1))
                for i in range(KD):
                    last = pe.matmul(ps_a[:, i * P:(i + 1) * P], work[0:NT, u, i * P:(i + 1) * P],
                                     tile(k, t)[:, i * P:(i + 1) * P], start=is_tile(t, 0) and i == 0,
                                     stop=is_tile(t, T - 1), skip_group_check=True)
                last.then_inc(s["w_used"], 1)
                if is_tile(t, T - 1):
                    pe.wait_ge(s["w_used"], T + 2)
                    pe.sem_inc(s["kv_done"], 1)

            staggered(b, 0, nothing, products, nothing)
            pe.wait_ge(s["kv_out"], 2)
            for i in range(KD):
                if i >= 2:
                    pe.wait_ge(s["mix_out"], i - 1)
                pe.matmul((ps_b, ps_c)[i % 2][:], kv_t[:, i, :], w["Wo"][:, i, :], start=True,
                          stop=True).then_inc(s["mix_done"], 1)
            pe.wait_ge(s["mix_out"], KD)

            def attend(t, u):
                pe.wait_ge(s["d_ready"], t + 1)
                pe.wait_ge(s["d_out"], t + 1)
                linear(ps_b, u, mixed_w).then_inc(s["d_done"], 1)

            staggered(b, 0, turn(s["d_in"], s["d_turned"], work), attend, nothing)
            pe.wait_ge(s["d_out"], T + 1)

            def ff_up(t, u):
                pe.wait_ge(s["f_ready"], t + 1)
                pe.wait_ge(s["h_ready"], t * 2 + 2)
                for half, ps in enumerate((ps_a, ps_b)):
                    for i in range(KD):
                        last = pe.matmul(ps[:, 0:NT], w1[:, i, half * P:(half + 1) * P], turned[:, u, i, :],
                                         start=(i == 0), stop=(i == KD - 1))
                last.then_inc(s["h_done"], 1)

            def ff_down(t, u):
                pe.wait_ge(s["h_ready"], t * 2 + 4)
                pe.wait_ge(s["f_out"], t + 1)
                for i in range(2):
                    last = pe.matmul(ps_c[0:NT, :], hidden[:, u, i, :], w2[:, i, :], start=(i == 0), stop=(i == 1))
                last.then_inc(s["f_done"], 1)

            staggered(b, 0, turn(s["f_in"], s["f_turned"], work), ff_up, ff_down)


def adjacency(nc, g, counts, weights):
    with ExitStack() as stack:
        m = Memory(nc, stack, "ad_")
        edges = m.sb("edges", [P, SLOTS_PER_P, 4])
        to = m.sb("to", [P, 2, CHUNKS, ONE_HOT], F32R)
        row = m.sb("row", [P, 2, CHUNKS, P], F32R)
        row_high, row_low = m.sb("row_high", [P, 2, CHUNKS, P], F32R), m.sb("row_low", [P, 2, CHUNKS, P], F32R)
        ps_c, ps_w = m.psum("ps_c", [P, 2, 512]), m.psum("ps_w", [P, 2, 512])
        loaded, zeroed, one_hots, scaled, used, added, chain = (
            m.sem(n) for n in ("loaded", "zeroed", "one_hots", "scaled", "used", "added", "chain"))
        block = stack.enter_context(nc.Block())

        def field(g_no, c, f):
            s = g_no * CHUNKS + c
            return edges[:, s, f:f + 1] if isinstance(s, int) else edges[:, bass.ds(s, 1), f:f + 1].squeeze(1)

        @block.sync
        def _(sp):
            sp.dma_start(edges[:], g.sorted_edges.rearrange("(p s) f -> p s f", p=P)).then_inc(loaded, 16)
            sp.wait_ge(loaded, 16)

        @block.gpsimd
        def _(pool):
            nc.gpsimd.memset(weights[:], 0.0).then_inc(zeroed, 1)
            pool.wait_ge(zeroed, 1)

        @block.vector
        def _(dve):
            v = nc.vector
            v.memset(counts[:], 0.0).then_inc(chain, 1)
            dve.wait_ge(chain, 1)
            dve.wait_ge(zeroed, 1)
            dve.wait_ge(loaded, 16)

            def build(t, u):
                dve.wait_ge(used, t + 1)
                for c in range(CHUNKS):
                    v.tensor_scalar(to[:, u, c, :], g.iota[:], field(t, c, 1), None, ALU.is_equal)
                    last = v.tensor_scalar(row[:, u, c, :], g.iota[:, 0:P], field(t, c, 0), None, ALU.is_equal)
                last.then_inc(one_hots, 1)

            def add(t, u):
                at = dve.value_load(g.group_offset[0:1, t:t + 1] if isinstance(t, int)
                                    else g.group_offset[0:1, bass.ds(t, 1)], min_val=0, max_val=DST - BUCKET)
                dve.wait_ge(used, t + 3)
                dve.wait_ge(added, t + 2)
                for ps, total in ((ps_c, counts), (ps_w, weights)):
                    part = total[:, :, bass.ds(at, BUCKET)]
                    last = v.tensor_tensor(part, part, ps[:, u, 0:ONE_HOT].rearrange("p (b n) -> p b n", b=T), ALU.add)
                last.then_inc(added, 1)

            staggered(Steps(dve, chain), 0, build, add, nothing, NG)
            dve.wait_ge(added, NG + 2)
            for b in range(T):
                own = weights[0:NT, b, b * NT:(b + 1) * NT]
                last = v.tensor_tensor(own, own, g.ident[0:NT, 0:NT], ALU.add)
            last.then_inc(chain, 1)
            dve.wait_ge(chain, 2)

        @block.scalar
        def _(act):
            act.wait_ge(loaded, 16)

            def scale(t, u):
                act.wait_ge(one_hots, t + 1)
                act.wait_ge(used, t + 1)
                for c in range(CHUNKS):
                    nc.scalar.activation(row_high[:, u, c, :], row[:, u, c, :].bitcast(F32), ACT.Copy, scale=field(t, c, 2))
                    last = nc.scalar.activation(row_low[:, u, c, :], row[:, u, c, :].bitcast(F32), ACT.Copy,
                                                scale=field(t, c, 3))
                last.then_inc(scaled, 1)

            staggered(Steps(act, chain), 0, scale, nothing, nothing, NG)

        @block.tensor
        def _(pe):
            pe.sem_inc(used, 2)
            pe.sem_inc(added, 2)

            def product(t, u):
                pe.wait_ge(scaled, t + 1)
                pe.wait_ge(added, t + 1)
                for c in range(CHUNKS):
                    ends = dict(start=(c == 0), stop=(c == CHUNKS - 1))
                    pe.matmul(ps_c[:, u, 0:ONE_HOT], row[:, u, c, :], to[:, u, c, :], **ends)
                    pe.matmul(ps_w[:, u, 0:ONE_HOT], row_high[:, u, c, :], to[:, u, c, :], start=(c == 0), stop=False)
                    last = pe.matmul(ps_w[:, u, 0:ONE_HOT], row_low[:, u, c, :], to[:, u, c, :], start=False,
                                     stop=(c == CHUNKS - 1))
                last.then_inc(used, 1)

            staggered(Steps(pe, chain), 0, nothing, product, nothing, NG)


def graph_conv_0(nc, A, g, counts, weights):
    with ExitStack() as stack:
        m = Memory(nc, stack, "gc_")
        w_self, w_neigh = m.sb("w_self", [P, KD, D]), m.sb("w_neigh", [P, KD, D])
        rows = {n: m.sb(n, [P, D]) for n in ("bias", "gamma", "beta")}
        h = m.sb("h", [P, T, D])
        work, turned, around = m.sb("work", [P, 2, D]), m.sb("turned", [P, 2, KD, NT]), m.sb("around", [P, KD, 2 * NT])
        in_sum = h[:].rearrange("p t d -> p (t d)")[:, T * D - 2 * DST:].rearrange("p (m n) -> p m n", m=2)
        degree, inverse, positive = m.sb("degree", [P, T]), m.sb("inverse", [P, T]), m.sb("positive", [P, T])
        n1 = Norm(m, "n1")
        ps_t = m.psum("ps_t", [P, 2, D])
        ps_around = m.psum("ps_around", [P, KD, 256])
        ps_self, ps_neigh = m.psum("ps_self", [P, D]), m.psum("ps_neigh", [P, D])
        ps_degree = m.psum("ps_degree", [P, 2, T])
        names = "arrived copied turned_out turned_ready around_done around_ready linear_done taken summed degrees root root_ready used chain"
        s = {n: m.sem(n) for n in names.split()}
        block = stack.enter_context(nc.Block())

        @block.sync
        def _(sp):
            load_matrix(sp, w_self, A["L0_gnn_W_self"], s["arrived"])
            load_matrix(sp, w_neigh, A["L0_gnn_W_neigh"], s["arrived"])
            for n in rows:
                load_row(sp, rows[n], A["L0_gnn_" + n], s["arrived"])
            sp.wait_ge(s["arrived"], 16 * 5)

        @block.gpsimd
        def _(pool):
            def copy(t, u):
                pool.wait_ge(s["turned_out"], t + 1)
                nc.gpsimd.tensor_copy(work[0:NT, u, :], tile(g.xn, t)).then_inc(s["copied"], 1)

            staggered(Steps(pool, s["used"]), 0, copy, nothing, nothing)

        @block.scalar
        def _(act):
            def evacuate(t, u):
                act.wait_ge(s["turned_out"], t + 3)
                act.wait_ge(s["linear_done"], t + 1)
                nc.scalar.copy(turned[:, u].rearrange("p k n -> p (k n)"), ps_t[:, u, 0:KD * NT]).then_inc(s["turned_ready"], 1)

            def evacuate_around(t, u):
                if u == 0:
                    act.wait_ge(s["around_done"], t + 2)
                    act.wait_ge(s["linear_done"], t + 2)
                    nc.scalar.copy(around[:], ps_around[:, :, 0:2 * NT]).then_inc(s["around_ready"], 2)

            staggered(Steps(act, s["used"]), 0, evacuate, evacuate_around, nothing)
            act.wait_ge(s["root"], 1)
            nc.scalar.activation(inverse[0:NT, :], degree[0:NT, :], ACT.Sqrt).then_inc(s["root_ready"], 1)
            n1.root(nc, act)

        @block.vector
        def _(dve):
            v = nc.vector
            c = Steps(dve, s["chain"])
            r = slice(0, NT)
            v.reduce_sum(in_sum[:, 0, :], counts[:].rearrange("p b n -> p n b"), AX_X).then_inc(s["summed"], 1)
            v.reduce_sum(in_sum[:, 1, :], weights[:].rearrange("p b n -> p n b"), AX_X).then_inc(s["summed"], 1)
            dve.wait_ge(s["degrees"], 1)
            c.link(v.tensor_scalar(degree[r, :], ps_degree[r, 0, :], 1.0, None, ALU.max))
            c.link(v.reciprocal(degree[r, :], degree[r, :]))
            dve.wait_ge(s["arrived"], 16 * 5)

            def combine(t, u):
                dve.wait_ge(s["linear_done"], t + 3)
                c.link(v.scalar_tensor_tensor(tile(h, t), ps_neigh[r, :], column(degree, t), rows["bias"][r, :],
                                              ALU.mult, ALU.add))
                v.tensor_tensor(tile(h, t), tile(h, t), ps_self[r, :], ALU.add).then_inc(s["taken"], 1)

            staggered(c, 2, nothing, combine, nothing)
            c.link(v.tensor_scalar(positive[r, :], ps_degree[r, 1, :], 0.0, None, ALU.is_gt))
            c.link(v.tensor_tensor(degree[r, :], ps_degree[r, 1, :], positive[r, :], ALU.mult))
            c.link(v.tensor_tensor(degree[r, :], degree[r, :], positive[r, :], ALU.subtract))
            v.tensor_scalar(degree[r, :], degree[r, :], 1.0, None, ALU.add).then_inc(s["root"], 1)
            dve.wait_ge(s["root_ready"], 1)
            c.link(v.reciprocal(g.dinv[r, :], inverse[r, :]))
            c.link(v.tensor_tensor(inverse[r, :], g.dinv[r, :], g.dinv[r, :], ALU.mult))
            c.link(v.tensor_tensor(inverse[r, :], inverse[r, :], degree[r, :], ALU.mult))
            c.link(v.tensor_scalar(inverse[r, :], inverse[r, :], -0.5, 1.5, ALU.mult, ALU.add))
            c.link(v.tensor_tensor(g.dinv[r, :], g.dinv[r, :], inverse[r, :], ALU.mult))
            c.link(v.tensor_tensor(g.dinv[r, :], g.dinv[r, :], positive[r, :], ALU.mult))
            n1.all_stats(nc, c, h)
            n1.variance(nc, c)
            with c.rounds(T // 2, 8) as j:
                for u in range(2):
                    t = j * 2 + u
                    c.link(n1.apply(nc, tile(h, t), tile(h, t), t))
                    c.link(v.tensor_tensor(tile(h, t), tile(h, t), rows["gamma"][r, :], ALU.mult))
                    c.link(v.tensor_tensor(tile(h, t), tile(h, t), rows["beta"][r, :], ALU.add))
                    c.step(v.tensor_tensor(tile(g.x, t), tile(g.x, t), tile(h, t), ALU.add))
            c.settle()

        @block.tensor
        def _(pe):
            for n in ("turned_out", "linear_done"):
                pe.sem_inc(s[n], 2)
            pe.sem_inc(s["taken"], 1)
            pe.wait_ge(s["arrived"], 16 * 5)

            def degrees():
                pe.wait_ge(s["summed"], 2)
                for n in range(2):
                    for t in range(T):
                        last = pe.matmul(ps_degree[0:NT, n, t:t + 1], in_sum[0:NT, n, t * NT:(t + 1) * NT],
                                         g.ones[0:NT, 0:1], start=True, stop=True)
                last.then_inc(s["degrees"], 1)

            def gather_and_turn(t, u):
                if u == 0:
                    for k in range(KD):
                        for b in range(T):
                            into = counts[0:NT, b, t * NT:(t + 2) * NT] if isinstance(t, int) \
                                else counts[0:NT, b, bass.ds(t * NT, 2 * NT)]
                            last = pe.matmul(ps_around[:, k, 0:2 * NT], g.xn[0:NT, b, k * P:(k + 1) * P], into,
                                             start=(b == 0), stop=(b == T - 1))
                    last.then_inc(s["around_done"], 2)
                pe.wait_ge(s["copied"], t + 1)
                for k in range(KD):
                    last = pe.transpose(ps_t[:, u, k * NT:(k + 1) * NT], work[0:NT, u, k * P:(k + 1) * P],
                                        g.ident[0:NT, 0:NT])
                last.then_inc(s["turned_out"], 1)
                if is_tile(t, 0):
                    degrees()

            def linears(t, u):
                pe.wait_ge(s["turned_ready"], t + 1)
                pe.wait_ge(s["taken"], t + 1)
                if u == 0:
                    pe.wait_ge(s["around_ready"], t + 2)
                for k in range(KD):
                    pe.matmul(ps_self[0:NT, :], turned[:, u, k, :], w_self[:, k, :], start=(k == 0), stop=(k == KD - 1))
                for k in range(KD):
                    last = pe.matmul(ps_neigh[0:NT, :], around[:, k, u * NT:(u + 1) * NT], w_neigh[:, k, :],
                                     start=(k == 0), stop=(k == KD - 1))
                last.then_inc(s["linear_done"], 1)

            staggered(Steps(pe, s["used"]), 0, gather_and_turn, linears, nothing)


def expert_choice_0(nc, A, g):
    with ExitStack() as stack:
        m = Memory(nc, stack, "ec_")
        gate_w, gate_b = m.sb("gate_w", [EXPERTS_0, D]), m.sb("gate_b", [EXPERTS_0, 1])
        expert, bias = m.sb("expert", [P, KD, D]), m.sb("bias", [P, D])
        mean, products = m.sb("mean", [EXPERTS_0, D]), m.sb("products", [EXPERTS_0, D])
        logit, spread = m.sb("logit", [EXPERTS_0, 1]), m.sb("spread", [EXPERTS_0, P])
        scores, shifted, odds = (m.sb(n, [P, EXPERTS_0]) for n in ("scores", "shifted", "odds"))
        top, total, best = m.sb("top", [P, 8]), m.sb("total", [P, 1]), m.sb("best", [P, 8], U32)
        work, turned = m.sb("work", [P, 2, D]), m.sb("turned", [P, 2, KD, NT])
        work_y = m.sb("work_y", [P, 2, D])
        n1 = Norm(m, "n1")
        ps_t, ps_mean = m.psum("ps_t", [P, 2, D]), m.psum("ps_mean", [P, D])
        ps_y, ps_scores = m.psum("ps_y", [P, 2, D]), m.psum("ps_scores", [P, EXPERTS_0])
        names = "arrived normed copied summed logits scored shifted_ready odds_ready chosen fetched turned_out turned_ready linear_done taken chain used"
        s = {n: m.sem(n) for n in names.split()}
        block = stack.enter_context(nc.Block())

        @block.sync
        def _(sp):
            sp.dma_start(gate_w[:], A["L0_ffn_Wg"]).then_inc(s["arrived"], 16)
            sp.dma_start(gate_b[:], A["L0_ffn_bg"].rearrange("(e a) -> e a", a=1)).then_inc(s["arrived"], 16)
            sp.wait_ge(s["chosen"], 1)
            e = sp.value_load(best[0:1, 0:1], min_val=0, max_val=EXPERTS_0 - 1)
            sp.dma_start(expert[:], A["L0_ffn_We"][bass.ds(e, 1)].squeeze(0).rearrange("(k p) n -> p k n", p=P)).then_inc(s["fetched"], 16)
            sp.dma_start(bias[:], A["L0_ffn_be"][bass.ds(e, 1)].squeeze(0).partition_broadcast(P)).then_inc(s["fetched"], 16)
            sp.wait_ge(s["arrived"], 32)
            sp.wait_ge(s["fetched"], 32)

        @block.gpsimd
        def _(pool):
            def copy(t, u):
                pool.wait_ge(s["turned_out"], t + 1)
                pool.wait_ge(s["normed"], t + 1)
                nc.gpsimd.tensor_copy(work[0:NT, u, :], tile(g.xn, t)).then_inc(s["copied"], 1)

            staggered(Steps(pool, s["used"]), 0, copy, nothing, nothing)

        @block.scalar
        def _(act):
            n1.root(nc, act)
            act.wait_ge(s["shifted_ready"], 1)
            nc.scalar.activation(odds[:], shifted[:], ACT.Exp, accum_out=total[:]).then_inc(s["odds_ready"], 1)

            def evacuate(t, u):
                act.wait_ge(s["turned_out"], t + 3)
                act.wait_ge(s["linear_done"], t + 1)
                nc.scalar.copy(turned[:, u].rearrange("p k n -> p (k n)"), ps_t[:, u, 0:KD * NT]).then_inc(s["turned_ready"], 1)

            staggered(Steps(act, s["used"]), 0, evacuate, nothing, nothing)

        @block.vector
        def _(dve):
            v = nc.vector
            c = Steps(dve, s["chain"])
            r, er = slice(0, NT), slice(0, EXPERTS_0)
            n1.all_stats(nc, c, g.x)
            n1.variance(nc, c)
            with c.rounds(T // 2, 0) as j:
                for u in range(2):
                    t = j * 2 + u
                    n1.apply(nc, tile(g.xn, t), tile(g.x, t), t).then_inc(s["normed"], 1)
            dve.wait_ge(s["summed"], 1)
            dve.wait_ge(s["arrived"], 32)
            c.link(v.tensor_scalar(mean[:], ps_mean[er, :], 1.0 / NODES, None, ALU.mult))
            c.link(v.tensor_tensor(products[:], mean[:], gate_w[:], ALU.mult))
            c.link(v.reduce_sum(logit[:], products[:], AX_X))
            c.link(v.tensor_tensor(logit[:], logit[:], gate_b[:], ALU.add))
            v.tensor_scalar(spread[:], g.ones[er, :], logit[:, 0:1], None, ALU.mult).then_inc(s["logits"], 1)
            dve.wait_ge(s["scored"], 1)
            c.link(v.tensor_copy(scores[:], ps_scores[:]))
            c.link(v.max(top[:], scores[:]))
            v.tensor_scalar(shifted[:], scores[:], top[:, 0:1], None, ALU.subtract).then_inc(s["shifted_ready"], 1)
            dve.wait_ge(s["odds_ready"], 1)
            c.link(v.reciprocal(total[:], total[:]))
            c.link(v.tensor_scalar(scores[:], odds[:], total[:, 0:1], None, ALU.mult))
            c.link(v.max(top[:], scores[:]))
            v.max_index(best[:], top[:], scores[:]).then_inc(s["chosen"], 1)
            dve.wait_ge(s["fetched"], 32)

            def combine(t, u):
                dve.wait_ge(s["linear_done"], t + 3)
                v.tensor_tensor(work_y[r, u, :], ps_y[r, u, :], bias[r, :], ALU.add).then_inc(s["taken"], 1)
                dve.wait_ge(s["taken"], t + 3)
                c.step(v.scalar_tensor_tensor(tile(g.x, t), work_y[r, u, :], top[r, 0:1], tile(g.x, t), ALU.mult, ALU.add))
                c.settle()

            staggered(c, 2, nothing, combine, nothing)

        @block.tensor
        def _(pe):
            for n in ("turned_out", "linear_done", "taken"):
                pe.sem_inc(s[n], 2)

            def add_up(t, u):
                pe.wait_ge(s["normed"], t + 1)
                last = pe.matmul(ps_mean[:], g.ones[0:NT, :], tile(g.xn, t), start=is_tile(t, 0), stop=is_tile(t, T - 1))
                if is_tile(t, T - 1):
                    last.then_inc(s["summed"], 1)

            staggered(Steps(pe, s["used"]), 0, nothing, add_up, nothing)
            pe.wait_ge(s["logits"], 1)
            pe.matmul(ps_scores[:], spread[:], g.ident[0:EXPERTS_0, 0:EXPERTS_0], start=True, stop=True).then_inc(s["scored"], 1)

            def turn(t, u):
                pe.wait_ge(s["copied"], t + 1)
                for k in range(KD):
                    last = pe.transpose(ps_t[:, u, k * NT:(k + 1) * NT], work[0:NT, u, k * P:(k + 1) * P],
                                        g.ident[0:NT, 0:NT])
                last.then_inc(s["turned_out"], 1)

            def linear(t, u):
                if is_tile(t, 0):
                    pe.wait_ge(s["fetched"], 32)
                pe.wait_ge(s["turned_ready"], t + 1)
                pe.wait_ge(s["taken"], t + 1)
                for k in range(KD):
                    last = pe.matmul(ps_y[0:NT, u, :], turned[:, u, k, :], expert[:, k, :], start=(k == 0), stop=(k == KD - 1))
                last.then_inc(s["linear_done"], 1)

            staggered(Steps(pe, s["used"]), 0, turn, linear, nothing)


def layer_1(nc, A, g, weights):
    with ExitStack() as stack:
        m = Memory(nc, stack, "l1_")
        w = {n: m.sb(n, [P, KD, D]) for n in ("Wq", "Wk", "Wv", "Wo")}
        w_conv, w_lin = m.sb("w_conv", [P, KD, GCN]), m.sb("w_lin", [P, D])
        rows = {n: m.sb(n, [P, D]) for n in ("bq", "bk", "bv", "bo")}
        b_lin, b_conv = m.sb("b_lin", [P, D]), m.sb("b_conv", [P, 1])
        temperature = m.sb("temperature", [P, 1])
        conv_spread = m.sb("conv_spread", [P, P])
        values, conv = m.sb("values", [P, T, D]), m.sb("conv", [P, T, GCN])
        work, turned = m.sb("work", [P, 2, D]), m.sb("turned", [P, 2, KD, NT])
        qw, kw, both = m.sb("qw", [P, 2, D]), m.sb("kw", [P, 2, D]), m.sb("both", [P, 2, D])
        around = m.sb("around", [P, 2 * NT])
        qk, q_sum, k_sum, sink, alloc, comp, scale, tmp = (
            m.sb(n, [P, T, HEADS]) for n in ("qk", "q_sum", "k_sum", "sink", "alloc", "comp", "scale", "tmp"))
        n1 = Norm(m, "n1")
        ps_t = m.psum("ps_t", [P, 2, D])
        ps_q, ps_k, ps_v = (m.psum(n, [P, D]) for n in ("ps_q", "ps_k", "ps_v"))
        ps_conv = m.psum("ps_conv", [P, D])
        ps_around, ps_row = m.psum("ps_around", [P, 2 * NT]), m.psum("ps_row", [P, D])
        names = ("arrived spread_ready row_done in_ready turned_out turned_ready q_done k_done v_done conv_done q_out k_out "
                 "v_out conv_out q_ready k_ready dotted alloc_in alloc_ready comp_in comp_ready "
                 "o_in o_turned o_ready around_done around_ready o_done o_out chain used")
        s = {n: m.sem(n) for n in names.split()}
        block = stack.enter_context(nc.Block())

        @block.sync
        def _(sp):
            for n in ("Wq", "Wk", "Wv"):
                load_matrix(sp, w[n], A["L1_mix_" + n], s["arrived"])
            load_matrix(sp, w_conv, A["L1_gnn_W_conv"], s["arrived"])
            for n in rows:
                load_row(sp, rows[n], A["L1_mix_" + n], s["arrived"])
            load_row(sp, b_lin, A["L1_gnn_b_lin"], s["arrived"])
            load_row(sp, temperature, A["L1_mix_temperature"], s["arrived"])
            sp.dma_start(b_conv[:], A["L1_gnn_b_conv"].rearrange("(p a) -> p a", a=1)).then_inc(s["arrived"], 16)
            sp.dma_start(w_lin[:], A["L1_gnn_W_lin"]).then_inc(s["arrived"], 16)
            load_matrix(sp, w["Wo"], A["L1_mix_Wo"], s["arrived"])
            sp.wait_ge(s["arrived"], 16 * 13)

        @block.vector
        def _(dve):
            v = nc.vector
            c = Steps(dve, s["chain"])
            r = slice(0, NT)
            dve.wait_ge(s["arrived"], 16 * 13)
            v.tensor_scalar(conv_spread[:], g.ones[:], b_conv[:, 0:1], None, ALU.mult).then_inc(s["spread_ready"], 1)
            n1.all_stats(nc, c, g.x)
            n1.variance(nc, c)
            c.link(v.tensor_tensor(b_lin[:], b_lin[:], rows["bo"][:], ALU.add))
            dve.wait_ge(s["row_done"], 1)
            c.link(v.tensor_tensor(b_lin[:], b_lin[:], ps_row[:], ALU.add))

            def prepare(t, u):
                dve.wait_ge(s["turned_out"], t + 1)
                n1.apply(nc, work[r, u, :], tile(g.x, t), t).then_inc(s["in_ready"], 1)
                c.step(n1.apply(nc, tile(g.xn, t), tile(g.x, t), t))

            def add_biases(t, u):
                for name, ps, to in (("q", ps_q, qw[r, u, :]), ("k", ps_k, kw[r, u, :]), ("v", ps_v, tile(values, t))):
                    dve.wait_ge(s[name + "_done"], t + 1)
                    v.tensor_tensor(to, ps[r, :], rows["b" + name][r, :], ALU.add).then_inc(s[name + "_out"], 1)
                dve.wait_ge(s["conv_done"], t + 3)
                v.tensor_scalar(tile(conv, t), ps_conv[r, 0:GCN], column(g.dinv, t), None, ALU.mult).then_inc(s["conv_out"], 1)

            def dots(t, u):
                dve.wait_ge(s["q_ready"], t + 1)
                dve.wait_ge(s["k_ready"], t + 1)
                c.step(v.tensor_tensor(both[r, u, :], qw[r, u, :], kw[r, u, :], ALU.mult))
                c.step(v.reduce_sum(tile(q_sum, t), heads(qw[r, u, :]), AX_X))
                c.link(v.reduce_sum(tile(k_sum, t), heads(kw[r, u, :]), AX_X))
                c.link(v.reduce_sum(tile(qk, t), heads(both[r, u, :]), AX_X))

            staggered(c, 10, prepare, add_biases, dots)
            c.settle()
            eps = FLOW_EPS
            c.link(v.tensor_tensor(tmp[r], q_sum[r], k_sum[r], ALU.add))
            c.link(v.scalar_tensor_tensor(sink[r], tmp[r], eps, qk[r], ALU.mult, ALU.add))
            c.link(v.tensor_scalar(sink[r], sink[r], DH * eps * eps + eps, None, ALU.add))
            c.link(v.reciprocal(sink[r], sink[r]))
            for ours, theirs, to in ((q_sum, k_sum, alloc), (k_sum, q_sum, comp)):
                c.link(v.scalar_tensor_tensor(tmp[r], theirs[r], eps, qk[r], ALU.mult, ALU.add))
                c.link(v.tensor_tensor(tmp[r], tmp[r], sink[r], ALU.mult))
                c.link(v.scalar_tensor_tensor(to[r], ours[r], eps, tmp[r], ALU.mult, ALU.add))
                c.link(v.tensor_scalar(to[r], to[r], DH * eps * eps + eps, None, ALU.add))
            c.link(v.reciprocal(temperature[:], temperature[:]))
            c.link(v.tensor_scalar(comp[r], comp[r], -1.0, 1.0, ALU.max, ALU.min))
            c.link(v.tensor_scalar(comp[r], comp[r], temperature[r, 0:1], None, ALU.mult))
            v.tensor_tensor(comp[r], comp[r], comp[r], ALU.subtract).then_inc(s["comp_in"], 1)
            dve.wait_ge(s["comp_ready"], 2)
            c.link(v.reciprocal(tmp[r], comp[r]))
            c.link(v.tensor_tensor(comp[r], comp[r], tmp[r], ALU.mult))
            c.link(v.scalar_tensor_tensor(scale[r], comp[r], float(D), qk[r], ALU.mult, ALU.mult))
            c.link(v.tensor_tensor(scale[r], scale[r], sink[r], ALU.mult))
            c.link(v.tensor_tensor(scale[r], scale[r], alloc[r], ALU.mult))

            def attend(t, u):
                dve.wait_ge(s["o_turned"], t + 1)
                v.tensor_tensor(heads(work[r, u, :]), heads(tile(values, t)), over_head(tile(scale, t)),
                                ALU.mult).then_inc(s["o_in"], 1)

            def combine(t, u):
                dve.wait_ge(s["o_done"], t + 3)
                c.step(v.tensor_tensor(both[r, u, :], ps_q[r, :], b_lin[r, :], ALU.add))
                c.link(v.tensor_tensor(tile(g.x, t), tile(g.x, t), tile(g.xn, t), ALU.add))
                v.scalar_tensor_tensor(both[r, u, :], ps_k[r, :], column(g.dinv, t), both[r, u, :], ALU.mult,
                                       ALU.add).then_inc(s["o_out"], 1)
                dve.wait_ge(s["o_out"], t + 2)
                c.link(v.tensor_tensor(tile(g.x, t), tile(g.x, t), both[r, u, :], ALU.add))

            staggered(c, 6, attend, nothing, combine)

        @block.scalar
        def _(act):
            n1.root(nc, act)
            a = Steps(act, s["used"])

            def copy_turned(done, ready, used):
                def f(t, u):
                    act.wait_ge(done, t + 3)
                    act.wait_ge(used, t + 1)
                    nc.scalar.copy(turned[:, u].rearrange("p k n -> p (k n)"), ps_t[:, u, 0:KD * NT]).then_inc(ready, 1)
                return f

            def sigmoids(t, u):
                for name, buf in (("q", qw), ("k", kw)):
                    act.wait_ge(s[name + "_out"], t + 2)
                    nc.scalar.activation(buf[0:NT, u, :], buf[0:NT, u, :], ACT.Sigmoid).then_inc(s[name + "_ready"], 1)

            staggered(a, 0, copy_turned(s["turned_out"], s["turned_ready"], s["conv_done"]), sigmoids, nothing)
            act.wait_ge(s["comp_in"], 1)
            nc.scalar.activation(alloc[0:NT], alloc[0:NT], ACT.Sigmoid).then_inc(s["comp_ready"], 1)
            nc.scalar.activation(comp[0:NT], comp[0:NT], ACT.Exp).then_inc(s["comp_ready"], 1)

            turned_o = copy_turned(s["o_turned"], s["o_ready"], s["o_done"])

            def around_out(t, u):
                if u == 0:
                    act.wait_ge(s["around_done"], t + 2)
                    act.wait_ge(s["o_done"], t + 2)
                    nc.scalar.copy(around[:], ps_around[:]).then_inc(s["around_ready"], 2)

            staggered(a, 0, turned_o, around_out, nothing)

        @block.tensor
        def _(pe):
            for n in ("turned_out", "conv_done", "o_turned", "o_done"):
                pe.sem_inc(s[n], 2)
            for n in ("q_out", "k_out", "v_out", "conv_out", "o_out"):
                pe.sem_inc(s[n], 1)
            b = Steps(pe, s["used"])
            pe.wait_ge(s["arrived"], 16 * 13)
            pe.wait_ge(s["spread_ready"], 1)
            pe.matmul(ps_row[:], conv_spread[:], w_lin[:], start=True, stop=True).then_inc(s["row_done"], 1)

            def turn(ready, done):
                def f(t, u):
                    pe.wait_ge(ready, t + 1)
                    for k in range(KD):
                        last = pe.transpose(ps_t[:, u, k * NT:(k + 1) * NT], work[0:NT, u, k * P:(k + 1) * P],
                                            g.ident[0:NT, 0:NT])
                    last.then_inc(done, 1)
                return f

            def project(t, u):
                pe.wait_ge(s["turned_ready"], t + 1)
                for name, ps, matrix in (("q", ps_q, w["Wq"]), ("k", ps_k, w["Wk"]), ("v", ps_v, w["Wv"]),
                                         ("conv", ps_conv, w_conv)):
                    pe.wait_ge(s[name + "_out"], t + 1)
                    for k in range(KD):
                        last = pe.matmul(ps[0:NT, 0:GCN] if name == "conv" else ps[0:NT, :], turned[:, u, k, :],
                                         matrix[:, k, :], start=(k == 0), stop=(k == KD - 1))
                    last.then_inc(s[name + "_done"], 1)

            staggered(b, 0, turn(s["in_ready"], s["turned_out"]), project, nothing)
            pe.wait_ge(s["conv_out"], T + 1)
            turn_o = turn(s["o_in"], s["o_turned"])

            def gather_and_turn(t, u):
                if u == 0:
                    for k in range(T):
                        into = weights[0:NT, k, t * NT:(t + 2) * NT] if isinstance(t, int) \
                            else weights[0:NT, k, bass.ds(t * NT, 2 * NT)]
                        last = pe.matmul(ps_around[:], conv[0:NT, k, :], into, start=(k == 0), stop=(k == T - 1))
                    last.then_inc(s["around_done"], 2)
                turn_o(t, u)

            def outputs(t, u):
                pe.wait_ge(s["o_ready"], t + 1)
                pe.wait_ge(s["o_out"], t + 1)
                if u == 0:
                    pe.wait_ge(s["around_ready"], t + 2)
                for k in range(KD):
                    pe.matmul(ps_q[0:NT, :], turned[:, u, k, :], w["Wo"][:, k, :], start=(k == 0), stop=(k == KD - 1))
                pe.matmul(ps_k[0:NT, :], around[:, u * NT:(u + 1) * NT], w_lin[:], start=True,
                          stop=True).then_inc(s["o_done"], 1)

            staggered(b, 0, gather_and_turn, outputs, nothing)


FT = DFF // P
FC = DFF // D
HALF = KD * DFF


class Experts:

    def __init__(self, nc, A, stack):
        m = Memory(nc, stack, "ex_")
        self.up, self.down = A["L1_ffn_W1"], A["L1_ffn_W2"]
        self.weights = m.sb("weights", [P, 2 * 2 * HALF])
        self.b1 = m.sb("b1", [P, EXPERTS * FT])
        self.ends = m.sb("ends", [P, EXPERTS], I32)
        self.expert_of, self.buffer_of = m.sb("expert_of", [P, SLOT_TILES], I32), m.sb("buffer_of", [P, SLOT_TILES], I32)
        self.loaded = {(u, part): m.sem(f"loaded{u}_{part}") for u in range(2) for part in ("up", "down")}

    def load(self, sp, e, u):
        up, down = (w[e] if isinstance(e, int) else w[bass.ds(e, 1)].squeeze(0) for w in (self.up, self.down))
        at = 2 * u * HALF
        sp.dma_start(self.weights[:, at:at + HALF].rearrange("p (k f) -> p k f", k=KD),
                     up.rearrange("(k p) f -> p k f", p=P)).then_inc(self.loaded[u, "up"], 16)
        sp.dma_start(self.weights[:, at + HALF:at + 2 * HALF].rearrange("p (f d) -> p f d", f=FT),
                     down.rearrange("(f p) d -> p f d", p=P)).then_inc(self.loaded[u, "down"], 16)


def routing(nc, A, g, x):
    with ExitStack() as stack:
        m = Memory(nc, stack, "ro_")
        router, router_b = m.sb("router", [P, KD, EXPERTS]), m.sb("router_b", [P, EXPERTS])
        ln_g, ln_b = m.sb("ln_g", [P, D]), m.sb("ln_b", [P, D])
        b1_rows, b2 = m.sb("b1_rows", [P, P]), m.sb("b2", [EXPERTS, D])
        work, turned = m.sb("work", [P, 2, D]), m.sb("turned", [P, 2, KD, NT])
        logits, equal, place, chosen, slot, gate_row, *pick = (m.sb(n, [P, T, EXPERTS]) for n in (
            "logits", "equal", "place", "chosen", "slot", "gate_row", "pick0", "pick1"))
        top = [m.sb("top0", [P, T]), m.sb("top1", [P, T])]
        least, odds = m.sb("least", [P, T]), m.sb("odds", [P, T])
        in_tiles, ends, first_slot = (m.sb(n, [P, EXPERTS]) for n in ("in_tiles", "ends", "first_slot"))
        in_tiles_i = m.sb("in_tiles_i", [P, EXPERTS], I32)
        before_tile = m.sb("before_tile", [P, T + 1, EXPERTS])
        past = m.sb("past", [P, SLOT_TILES, EXPERTS])
        tile_expert, odd = m.sb("tile_expert", [P, SLOT_TILES]), m.sb("odd", [P, SLOT_TILES])
        gates_t = m.sb("gates_t", [EXPERTS, 2, NT])
        n1, n2 = Norm(m, "n1"), Norm(m, "n2")
        ps_t = m.psum("ps_t", [P, 2, D])
        ps_logits, ps_counts, ps_b1 = m.psum("ps_logits", [P, T, EXPERTS]), m.psum("ps_counts", [P, 2, T, EXPERTS]), m.psum("ps_b1", [P, P])
        ps_gates, ps_bias = m.psum("ps_gates", [P, NT]), m.psum("ps_bias", [P, D])
        names = ("arrived normed in_ready turned_out turned_ready logits_done b1_turned b1_ready picked counted odds_in "
                 "odds_ready gates_in gates_turned gates_ready bias_done bias_out slots_ready chain used")
        s = {n: m.sem(n) for n in names.split()}
        block = stack.enter_context(nc.Block())

        @block.sync
        def _(sp):
            load_matrix(sp, router, A["L1_ffn_w_r"], s["arrived"])
            load_row(sp, router_b, A["L1_ffn_b_r"], s["arrived"])
            load_row(sp, ln_g, A["L1_ffn_ln_g"], s["arrived"])
            load_row(sp, ln_b, A["L1_ffn_ln_b"], s["arrived"])
            sp.dma_start(b1_rows[:], A["L1_ffn_b1"].rearrange("e (f p) -> (e f) p", p=P)).then_inc(s["arrived"], 16)
            sp.dma_start(b2[:], A["L1_ffn_b2"]).then_inc(s["arrived"], 16)
            x.load(sp, 0, 0)
            x.load(sp, 1, 1)
            sp.wait_ge(s["arrived"], 16 * 6)

        @block.gpsimd
        def _(pool):
            def copy(t, u):
                pool.wait_ge(s["turned_out"], t + 1)
                pool.wait_ge(s["normed"], t + 1)
                nc.gpsimd.tensor_copy(work[0:NT, u, :], tile(g.xn, t)).then_inc(s["in_ready"], 1)

            staggered(Steps(pool, s["used"]), 0, copy, nothing, nothing)
            pool.wait_ge(s["slots_ready"], 2)
            for n in range(2):
                for t in range(T):
                    nc.gpsimd.indirect_dma_start(
                        g.slot_rows, bass.IndirectOffsetOnAxis(ap=g.slots[0:NT, n, t:t + 1], axis=0),
                        g.xn[0:NT, t, :], None).then_inc(g.rows_scattered, 16)
            pool.wait_ge(g.rows_scattered, 16 * 2 * T)

        @block.vector
        def _(dve):
            v = nc.vector
            c = Steps(dve, s["chain"])
            r = slice(0, NT)
            n1.all_stats(nc, c, g.x)
            n1.variance(nc, c)
            with c.rounds(T // 2, 4) as j:
                for u in range(2):
                    c.step(n1.apply(nc, tile(g.xn, j * 2 + u), tile(g.x, j * 2 + u), j * 2 + u))
                c.settle()
                for u in range(2):
                    t = j * 2 + u
                    c.step(v.tensor_tensor(tile(g.x, t), tile(g.x, t), tile(g.xn, t), ALU.add))
            c.settle()
            n2.all_stats(nc, c, g.xn)
            n2.variance(nc, c)
            dve.wait_ge(s["arrived"], 16 * 6)
            with c.rounds(T // 2, 4) as j:
                for u in range(2):
                    t = j * 2 + u
                    c.link(n2.apply(nc, tile(g.xn, t), tile(g.xn, t), t))
                    c.link(v.tensor_tensor(tile(g.xn, t), tile(g.xn, t), ln_g[r, :], ALU.mult))
                    v.tensor_tensor(tile(g.xn, t), tile(g.xn, t), ln_b[r, :], ALU.add).then_inc(s["normed"], 1)
            c.step(v.memset(before_tile[:, 0, :], 0.0))
            dve.wait_ge(s["logits_done"], T + 2)
            all_ = [NT, T, EXPERTS]
            c.link(v.tensor_tensor(logits[r], ps_logits[r], router_b[r, :].unsqueeze(1).broadcast_to(all_), ALU.add))
            numbers = g.iota[r, 0:EXPERTS].unsqueeze(1).broadcast_to(all_)
            for n in range(2):
                c.link(v.tensor_reduce(top[n][r, :], logits[r], AX_X, ALU.max))
                c.link(v.tensor_tensor(equal[r], logits[r], top[n][r, :].unsqueeze(2).broadcast_to(all_), ALU.is_equal))
                c.link(v.scalar_tensor_tensor(place[r], equal[r], -float(EXPERTS), numbers, ALU.mult, ALU.add))
                c.link(v.tensor_reduce(least[r, :], place[r], AX_X, ALU.min))
                c.link(v.tensor_tensor(pick[n][r], place[r], least[r, :].unsqueeze(2).broadcast_to(all_), ALU.is_equal))
                if n == 0:
                    c.link(v.scalar_tensor_tensor(logits[r], pick[n][r], -3e38, logits[r], ALU.mult, ALU.add))
            v.tensor_tensor(chosen[r], pick[0][r], pick[1][r], ALU.add).then_inc(s["picked"], 1)
            v.tensor_tensor(odds[r, :], top[1][r, :], top[0][r, :], ALU.subtract).then_inc(s["odds_in"], 1)
            dve.wait_ge(s["counted"], 2)
            for t in range(T):
                c.link(v.tensor_tensor(before_tile[:, t + 1, :], before_tile[:, t, :], ps_counts[:, 1, t, :], ALU.add))
            c.link(v.tensor_scalar(in_tiles[:], before_tile[:, T, :], float(P - 1), None, ALU.add))
            c.link(v.tensor_copy(in_tiles_i[:], in_tiles[:]))
            c.link(v.tensor_scalar(in_tiles_i[:], in_tiles_i[:], 7, None, ALU.logical_shift_right))
            c.link(v.tensor_copy(in_tiles[:], in_tiles_i[:]))
            c.link(v.tensor_tensor_scan(ends[:], g.ones[:, 0:EXPERTS], in_tiles[:], 0.0, ALU.mult, ALU.add))
            c.step(v.tensor_copy(x.ends[:], ends[:]))
            c.link(v.tensor_tensor(first_slot[:], ends[:], in_tiles[:], ALU.subtract))
            c.link(v.tensor_scalar(first_slot[:], first_slot[:], float(P), None, ALU.mult))
            c.link(v.tensor_tensor(slot[r], before_tile[r, 0:T, :], first_slot[r, :].unsqueeze(1).broadcast_to(all_), ALU.add))
            c.link(v.tensor_tensor(slot[r], slot[r], ps_counts[r, 0], ALU.add))
            for n in range(2):
                c.link(v.tensor_tensor(place[r], slot[r], pick[n][r], ALU.mult))
                c.link(v.reduce_sum(least[r, :], place[r], AX_X))
                v.tensor_copy(g.slots[r, n, :], least[r, :]).then_inc(s["slots_ready"], 1)
                dve.wait_ge(s["slots_ready"], n + 1)
            tiles = [P, SLOT_TILES, EXPERTS]
            c.link(v.tensor_tensor(past[:], ends[:].unsqueeze(1).broadcast_to(tiles),
                                   g.iota[:, 0:SLOT_TILES].unsqueeze(2).broadcast_to(tiles), ALU.is_le))
            c.link(v.reduce_sum(tile_expert[:], past[:], AX_X))
            c.link(v.tensor_scalar(tile_expert[:], tile_expert[:], float(EXPERTS - 1), None, ALU.min))
            c.link(v.tensor_copy(x.expert_of[:], tile_expert[:]))
            c.link(v.tensor_scalar(x.buffer_of[:], x.expert_of[:], 1, None, ALU.bitwise_and))
            c.link(v.tensor_copy(odd[:], x.buffer_of[:]))
            c.link(v.tensor_scalar(odd[:], odd[:], float(2 * HALF), None, ALU.mult))
            c.link(v.tensor_copy(x.buffer_of[:], odd[:]))
            dve.wait_ge(s["odds_ready"], 1)
            c.link(v.tensor_scalar(g.gates[r, 0, :], odds[r, :], 1.0, None, ALU.add))
            c.link(v.reciprocal(g.gates[r, 0, :], g.gates[r, 0, :]))
            c.link(v.tensor_tensor(g.gates[r, 1, :], odds[r, :], g.gates[r, 0, :], ALU.mult))
            c.step(v.tensor_tensor(place[r], pick[0][r], g.gates[r, 0, :].unsqueeze(2).broadcast_to(all_), ALU.mult))
            c.link(v.tensor_tensor(equal[r], pick[1][r], g.gates[r, 1, :].unsqueeze(2).broadcast_to(all_), ALU.mult))
            v.tensor_tensor(gate_row[r], place[r], equal[r], ALU.add).then_inc(s["gates_in"], 1)
            for t in range(T):
                dve.wait_ge(s["gates_turned"], t + 1)
                v.tensor_copy(gates_t[:, t % 2, :], ps_gates[0:EXPERTS, :]).then_inc(s["gates_ready"], 1)
                dve.wait_ge(s["bias_done"], t + 1)
                v.tensor_tensor(g.x[r, t, :], g.x[r, t, :], ps_bias[r, :], ALU.add).then_inc(s["bias_out"], 1)
            dve.wait_ge(s["bias_out"], T)

        @block.scalar
        def _(act):
            n1.root(nc, act)
            n2.root(nc, act)
            act.wait_ge(s["b1_turned"], 1)
            nc.scalar.copy(x.b1[:], ps_b1[:]).then_inc(s["b1_ready"], 1)

            def evacuate(t, u):
                act.wait_ge(s["turned_out"], t + 3)
                act.wait_ge(s["logits_done"], t + 1)
                nc.scalar.copy(turned[:, u].rearrange("p k n -> p (k n)"), ps_t[:, u, 0:KD * NT]).then_inc(s["turned_ready"], 1)

            staggered(Steps(act, s["used"]), 0, evacuate, nothing, nothing)
            act.wait_ge(s["odds_in"], 1)
            nc.scalar.activation(odds[0:NT, :], odds[0:NT, :], ACT.Exp).then_inc(s["odds_ready"], 1)
            act.wait_ge(s["b1_ready"], 1)

        @block.tensor
        def _(pe):
            for n in ("turned_out", "logits_done"):
                pe.sem_inc(s[n], 2)
            pe.wait_ge(s["arrived"], 16 * 6)
            pe.transpose(ps_b1[:], b1_rows[:], g.ident[:]).then_inc(s["b1_turned"], 1)

            def turn(t, u):
                pe.wait_ge(s["in_ready"], t + 1)
                for k in range(KD):
                    last = pe.transpose(ps_t[:, u, k * NT:(k + 1) * NT], work[0:NT, u, k * P:(k + 1) * P],
                                        g.ident[0:NT, 0:NT])
                last.then_inc(s["turned_out"], 1)

            def score(t, u):
                pe.wait_ge(s["turned_ready"], t + 1)
                for k in range(KD):
                    last = pe.matmul(tile(ps_logits, t), turned[:, u, k, :], router[:, k, :], start=(k == 0), stop=(k == KD - 1))
                last.then_inc(s["logits_done"], 1)

            staggered(Steps(pe, s["used"]), 0, turn, score, nothing)
            pe.wait_ge(s["picked"], 1)
            picked = chosen[0:NT].rearrange("p t e -> p (t e)")
            pe.matmul(ps_counts[0:NT, 0].rearrange("p t e -> p (t e)"), g.before[0:NT, 0:NT], picked, start=True,
                      stop=True).then_inc(s["counted"], 1)
            pe.matmul(ps_counts[:, 1].rearrange("p t e -> p (t e)"), g.ones[0:NT, :], picked, start=True,
                      stop=True).then_inc(s["counted"], 1)
            pe.wait_ge(s["gates_in"], 1)
            for t in range(T):
                pe.matmul(ps_gates[0:EXPERTS, :], gate_row[0:NT, t, :], g.ident[0:NT, 0:NT], start=True,
                          stop=True).then_inc(s["gates_turned"], 1)
                pe.wait_ge(s["gates_ready"], t + 1)
                if t:
                    pe.wait_ge(s["bias_out"], t)
                pe.matmul(ps_bias[0:NT, :], gates_t[:, t % 2, :], b2[:], start=True, stop=True).then_inc(s["bias_done"], 1)


def expert_tiles(nc, g, x):
    with ExitStack() as stack:
        m = Memory(nc, stack, "et_")
        turned, hidden_t = m.sb("turned", [P, 2, KD, P]), m.sb("hidden_t", [P, 2, FT, P])
        rows_in, hidden, y = g.xn[:, 0:2, :], g.xn[:, 2:4, :], g.xn[:, 4:6, :]
        ps_t = m.psum("ps_t", [P, D])
        ps_h, ps_ht, ps_y = m.psum("ps_h", [P, 2, D]), m.psum("ps_ht", [P, 2, D]), m.psum("ps_y", [P, 2, D])
        names = ("weights_ready rows_loaded0 rows_loaded1 rows_turned rows_ready up_done up_out hidden_turned "
                 "hidden_ready tiles_done y_out y_stored0 y_stored1 used")
        s = {n: m.sem(n) for n in names.split()}
        block = stack.enter_context(nc.Block())

        def turns(t, u):
            return (t - u) * 8 + 16

        def entry(engine, table, t, most):
            return engine.value_load(table[0:1, t:t + 1] if isinstance(t, int) else table[0:1, bass.ds(t, 1)],
                                     min_val=0, max_val=most)

        @block.sync
        def _(sp):
            with sp.Fori(0, EXPERTS // 2 - 1) as j:
                for u in range(2):
                    last_tile = sp.value_load(x.ends[0:1, bass.ds(j * 2 + u, 1)], min_val=0, max_val=SLOT_TILES)
                    sp.wait_ge(s["tiles_done"], last_tile + 2)
                    x.load(sp, j * 2 + (u + 2), u)

        @block.gpsimd
        def _(pool):
            for e in range(EXPERTS):
                for part in ("up", "down"):
                    pool.wait_ge(x.loaded[e % 2, part], 16 * (e // 2 + 1))
                    pool.sem_inc(s["weights_ready"], 1)
            pool.wait_ge(s["weights_ready"], 2 * EXPERTS)

        @block.vector
        def _(dve):
            v = nc.vector

            def move_hidden(t, u):
                for f in range(FC):
                    dve.wait_ge(s["up_done"], t * FC + (f + 1))
                    dve.wait_ge(s["hidden_turned"], t * FC + (f + 1))
                    v.tensor_copy(hidden[:, f % 2, :], ps_h[:, f % 2, :]).then_inc(s["up_out"], 1)

            def move_y(t, u):
                dve.wait_ge(s["tiles_done"], t + 3)
                dve.wait_ge(s[f"y_stored{u}"], turns(t, u))
                v.tensor_copy(y[:, u, :], ps_y[:, u, :]).then_inc(s["y_out"], 1)

            staggered(Steps(dve, s["used"]), 0, nothing, move_hidden, move_y, SLOT_TILES)

        @block.scalar
        def _(act):
            out_rows = g.slot_out.rearrange("(n p) d -> n p d", p=P)
            in_rows = g.slot_rows.rearrange("(n p) d -> n p d", p=P)

            def of(rows, t):
                return rows[t] if isinstance(t, int) else rows[bass.ds(t, 1)].squeeze(0)

            def load_rows(t, u):
                act.wait_ge(s["rows_turned"], t + 1)
                act.dma_start(rows_in[:, u, :], of(in_rows, t)).then_inc(s[f"rows_loaded{u}"], 16)
                if is_tile(t, 0):
                    move_turned(0, 0)

            def move_turned(t, u):
                act.wait_ge(s["rows_turned"], t + 3)
                act.wait_ge(s["tiles_done"], t + 1)
                nc.scalar.copy(turned[:, u].rearrange("p k n -> p (k n)"), ps_t[:]).then_inc(s["rows_ready"], 1)

            def gelu(t, u):
                e = entry(act, x.expert_of, t, EXPERTS - 1)
                act.wait_ge(s["tiles_done"], t + 1)
                for f in range(FC):
                    act.wait_ge(s["hidden_turned"], t * FC + (f + 3))
                    for i in range(KD):
                        last = nc.scalar.activation(hidden_t[:, u, f * KD + i, :], ps_ht[:, f % 2, i * P:(i + 1) * P],
                                                    ACT.Gelu, bias=x.b1[:, bass.ds(e * FT + (f * KD + i), 1)])
                    last.then_inc(s["hidden_ready"], 1)
                    if f == 2 and not is_tile(t, SLOT_TILES - 1):
                        move_turned(t + 1, 1 - u)

            def store(t, u):
                act.wait_ge(s["y_out"], t + 3)
                act.dma_start(of(out_rows, t), y[:, u, :]).then_inc(s[f"y_stored{u}"], 16)

            staggered(Steps(act, s["used"]), 0, load_rows, gelu, store, SLOT_TILES)
            act.wait_ge(s["y_stored0"], 16 * ((SLOT_TILES + 1) // 2) + 16)
            act.wait_ge(s["y_stored1"], 16 * (SLOT_TILES // 2) + 16)

        @block.tensor
        def _(pe):
            for n in ("rows_turned", "up_out", "hidden_turned", "hidden_ready", "tiles_done", "y_out"):
                pe.sem_inc(s[n], 2)
            for n in ("y_stored0", "y_stored1"):
                pe.sem_inc(s[n], 16)

            def turn_rows(t, u):
                pe.wait_ge(s[f"rows_loaded{u}"], turns(t, u))
                for k in range(KD):
                    last = pe.transpose(ps_t[:, k * P:(k + 1) * P], rows_in[:, u, k * P:(k + 1) * P], g.ident[:])
                last.then_inc(s["rows_turned"], 1)

            def run_expert(t, u):
                e = entry(pe, x.expert_of, t, EXPERTS - 1)
                at = entry(pe, x.buffer_of, t, 2 * HALF)

                def up(f):
                    pe.wait_ge(s["up_out"], t * FC + (f + 1))
                    for k in range(KD):
                        last = pe.matmul(ps_h[:, f % 2, :], turned[:, u, k, :],
                                         x.weights[:, bass.ds(at + (k * DFF + f * D), D)], start=(k == 0), stop=(k == KD - 1))
                    last.then_inc(s["up_done"], 1)

                def turn_hidden(f):
                    pe.wait_ge(s["up_out"], t * FC + (f + 3))
                    pe.wait_ge(s["hidden_ready"], t * FC + (f + 1))
                    for i in range(KD):
                        last = pe.transpose(ps_ht[:, f % 2, i * P:(i + 1) * P], hidden[:, f % 2, i * P:(i + 1) * P], g.ident[:])
                    last.then_inc(s["hidden_turned"], 1)

                def down(f):
                    pe.wait_ge(s["hidden_ready"], t * FC + (f + 3))
                    for i in range(f * KD, (f + 1) * KD):
                        last = pe.matmul(ps_y[:, u, :], hidden_t[:, u, i, :],
                                         x.weights[:, bass.ds(at + (HALF + i * D), D)], start=(i == 0), stop=(i == FT - 1))
                    return last

                pe.wait_ge(s["rows_ready"], t + 1)
                pe.wait_ge(s["weights_ready"], e * 2 + 1)
                up(0)
                up(1)
                turn_hidden(0)
                up(2)
                turn_hidden(1)
                up(3)
                turn_hidden(2)
                if not is_tile(t, SLOT_TILES - 1):
                    turn_rows(t + 1, 1 - u)
                turn_hidden(3)
                pe.wait_ge(s["weights_ready"], e * 2 + 2)
                pe.wait_ge(s["y_out"], t + 1)
                for f in range(FC - 1):
                    down(f)
                down(FC - 1).then_inc(s["tiles_done"], 1)

            turn_rows(0, 0)
            staggered(Steps(pe, s["used"]), 0, nothing, run_expert, nothing, SLOT_TILES)


def gather_experts(nc, A, g):
    with ExitStack() as stack:
        m = Memory(nc, stack, "ge_")
        y = m.sb("y", [P, 2, T, D])
        half, summed, stored = m.sem("half"), m.sem("summed"), m.sem("stored")
        block = stack.enter_context(nc.Block())

        @block.gpsimd
        def _(pool):
            for t in range(T):
                for n in range(2):
                    nc.gpsimd.indirect_dma_start(
                        y[0:NT, n, t, :], None, g.slot_out,
                        bass.IndirectOffsetOnAxis(ap=g.slots[0:NT, n, t:t + 1], axis=0)).then_inc(g.gathered[t], 16)

        @block.vector
        def _(dve):
            for t in range(T):
                dve.wait_ge(g.gathered[t], 32)
                for n, done in ((0, half), (1, summed)):
                    nc.vector.scalar_tensor_tensor(g.x[0:NT, t, :], y[0:NT, n, t, :], g.gates[0:NT, n, t:t + 1],
                                                   g.x[0:NT, t, :], ALU.mult, ALU.add).then_inc(done, 1)
                    dve.wait_ge(done, t + 1)

        @block.sync
        def _(sp):
            for t in range(T):
                sp.wait_ge(summed, t + 1)
                sp.dma_start(A["out"][t * NT:(t + 1) * NT], g.x[0:NT, t, :]).then_inc(stored, 16)
            sp.wait_ge(stored, 16 * T)


def program(nc, A):
    with ExitStack() as stack:
        g = Shared(nc, stack)
        edge_positions(nc, A, g)
        flow_attention(nc, A, g)
        with ExitStack() as graph:
            weights = Memory(nc, graph).sb("edge_weights", [P, T, DST])
            with ExitStack() as first:
                counts = Memory(nc, first).sb("edge_counts", [P, T, DST])
                adjacency(nc, g, counts, weights)
                graph_conv_0(nc, A, g, counts, weights)
            expert_choice_0(nc, A, g)
            layer_1(nc, A, g, weights)
        with ExitStack() as layer:
            x = Experts(nc, A, layer)
            routing(nc, A, g, x)
            expert_tiles(nc, g, x)
        gather_experts(nc, A, g)


def kernel(**inputs):
    import numpy as _np
    import concourse.bacc as _bacc
    from concourse import mybir as _mybir
    from concourse.bass_utils import run_bass_kernel_spmd as _run

    nc = _bacc.Bacc("TRN2", target_bir_lowering=False, num_devices=1)
    arrays, A = {}, {}
    for name, a in inputs.items():
        a = _np.asarray(a)
        if name in ("L0_gnn_W_self", "L0_gnn_W_neigh", "L0_ffn_Wg", "L1_ffn_w_r"):
            a = a.T
        a = _np.ascontiguousarray(a)
        arrays[name] = a
        A[name] = nc.dram_tensor(name, a.shape, _mybir.dt.from_np(a.dtype), kind="ExternalInput").ap()
    A["out"] = nc.dram_tensor("out", (NODES, D), F32, kind="ExternalOutput").ap()
    program(nc, A)
    r = _run(nc, [arrays], core_ids=[0])
    return r.results[0]["out"]
```

```python
from contextlib import ExitStack, contextmanager

import concourse.bass as bass
from concourse import mybir

ALU = mybir.AluOpType
ACT = mybir.ActivationFunctionType
F32 = mybir.dt.float32
F32R = mybir.dt.float32r
I32 = mybir.dt.int32
U32 = mybir.dt.uint32
AX_X = mybir.AxisListType.X

P = 128
D = 512
KD = D // P
NODES = 1250
NT = 125
T = NODES // NT
HEADS, DH = 8, 64
LN_EPS = 1e-5
FLOW_EPS = 1e-6

EDGES = 40000
EP = EDGES // NT
BUCKET = 32
NB = -(-NODES // BUCKET)
GROUP = 512
NG = (EDGES + NB * (GROUP - 1)) // GROUP
NG += NG % 2
CHUNKS = GROUP // P
SLOTS_PER_P = NG * CHUNKS
ONE_HOT = T * BUCKET
DST = NB * BUCKET

EXPERTS_0 = 16
EXPERTS = 8
DFF = 2048
GCN = 128
FULL_TILES = 2 * NODES // P
SLOT_TILES = (2 * NODES + EXPERTS * (P - 1)) // P


class Steps:

    def __init__(self, engine, semaphore):
        self.engine, self.semaphore = engine, semaphore
        self.before, self.done, self.round, self.per_round = 0, 0, None, 0

    def count(self):
        if self.round is None:
            return self.before + self.done
        return self.round * self.per_round + (self.before + self.done)

    def step(self, instruction):
        instruction.then_inc(self.semaphore, 1)
        self.done += 1

    def settle(self):
        self.engine.wait_ge(self.semaphore, self.count())

    def link(self, instruction):
        self.step(instruction)
        self.settle()

    @contextmanager
    def rounds(self, n, per_round):
        self.before, self.done = self.before + self.done, 0
        with self.engine.Fori(0, n) as j:
            self.round, self.per_round = j, per_round
            yield j
            assert self.done == per_round, (self.done, per_round)
        self.before, self.done, self.round = self.before + n * per_round, 0, None


def staggered(steps, per_round, first, second, third, n=T, ways=2):
    first(0, 0)
    first(1, 1)
    second(0, 0)
    first(2, 2 % ways)
    second(1, 1)
    third(0, 0)
    rounds = (n - 3) // ways
    with steps.rounds(rounds, per_round) as j:
        for i in range(2, 2 + ways):
            t = j * ways + i
            first(t + 1, (i + 1) % ways)
            second(t, i % ways)
            third(t - 1, (i - 1) % ways)
    for t in range(2 + ways * rounds, n):
        if t + 1 < n:
            first(t + 1, (t + 1) % ways)
        second(t, t % ways)
        third(t - 1, (t - 1) % ways)
    third(n - 1, (n - 1) % ways)


def nothing(t, u):
    pass


def is_tile(t, n):
    return isinstance(t, int) and t == n


def tile(a, t):
    return a[0:NT, t, :] if isinstance(t, int) else a[0:NT, bass.ds(t, 1), :].squeeze(1)


def column(a, t):
    return a[0:NT, t:t + 1] if isinstance(t, int) else a[0:NT, bass.ds(t, 1)]


def heads(a):
    return a.rearrange("p (h d) -> p h d", h=HEADS)


def over_head(a):
    return a.unsqueeze(2).broadcast_to([NT, HEADS, DH])


class Memory:

    def __init__(self, nc, stack, prefix=""):
        self.nc, self.stack, self.prefix, self.numbers = nc, stack, prefix, []
        if prefix:
            stack.callback(self.clear)

    def sb(self, name, shape, dtype=F32):
        return self.stack.enter_context(self.nc.sbuf_tensor(self.prefix + name, shape, dtype))

    def psum(self, name, shape, dtype=F32):
        return self.stack.enter_context(self.nc.psum_tensor(self.prefix + name, shape, dtype))

    def sem(self, name):
        semaphore = self.stack.enter_context(self.nc.semaphore(self.prefix + name))
        self.numbers.append(semaphore.num)
        return semaphore

    def clear(self):
        first = self.numbers[0]
        for i, number in enumerate(self.numbers):
            if i + 1 == len(self.numbers) or self.numbers[i + 1] != number + 1:
                self.nc.gpsimd.sem_clear(range(first, number + 1))
                first = self.numbers[min(i + 1, len(self.numbers) - 1)]


class Norm:

    def __init__(self, m, name):
        self.stats = m.sb(name + "_stats", [P, T, 6])
        self.mean, self.diff, self.var, self.std, self.rstd = (
            m.sb(f"{name}_{n}", [P, T]) for n in ("mean", "diff", "var", "std", "rstd"))
        self.var_ready = m.sem(name + "_var_ready")
        self.std_ready = m.sem(name + "_std_ready")

    def tile_stats(self, t):
        return self.stats[0:NT, t, :] if isinstance(t, int) else self.stats[0:NT, bass.ds(t, 1), :].squeeze(1)

    def all_stats(self, nc, steps, x):
        with steps.rounds(T // 2, 2) as j:
            for u in range(2):
                t = j * 2 + u
                steps.step(nc.vector.bn_stats(tile(self.stats, t), tile(x, t)))
        steps.settle()

    def variance(self, nc, steps, t=None):
        v = nc.vector
        mean, diff, var, std, rstd = (a[0:NT, :] if t is None else column(a, t)
                                      for a in (self.mean, self.diff, self.var, self.std, self.rstd))
        stats = self.stats[0:NT] if t is None else self.tile_stats(t)
        mean0, mean1, var0, var1 = ((stats[:, :, i] if t is None else stats[:, i:i + 1]) for i in (1, 4, 2, 5))
        steps.step(v.tensor_tensor(mean, mean0, mean1, ALU.add))
        steps.step(v.tensor_tensor(diff, mean0, mean1, ALU.subtract))
        steps.link(v.tensor_tensor(var, var0, var1, ALU.add))
        steps.step(v.tensor_scalar(mean, mean, 0.5, None, ALU.mult))
        steps.step(v.tensor_tensor(diff, diff, diff, ALU.mult))
        steps.link(v.tensor_scalar(var, var, 1.0 / D, LN_EPS, ALU.mult, ALU.add))
        v.scalar_tensor_tensor(var, diff, 0.25, var, ALU.mult, ALU.add).then_inc(self.var_ready, 1)
        steps.engine.wait_ge(self.std_ready, 1 if t is None else t + 1)
        steps.link(v.reciprocal(rstd, std))
        steps.link(v.tensor_tensor(std, rstd, rstd, ALU.mult))
        steps.link(v.tensor_tensor(std, std, var, ALU.mult))
        steps.link(v.tensor_scalar(std, std, -0.5, 1.5, ALU.mult, ALU.add))
        steps.link(v.tensor_tensor(rstd, rstd, std, ALU.mult))

    def root(self, nc, act, t=None):
        act.wait_ge(self.var_ready, 1 if t is None else t + 1)
        std, var = (a[0:NT, :] if t is None else column(a, t) for a in (self.std, self.var))
        nc.scalar.activation(std, var, ACT.Sqrt).then_inc(self.std_ready, 1)

    def apply(self, nc, out, x, t):
        return nc.vector.tensor_scalar(out, x, column(self.mean, t), column(self.rstd, t),
                                       ALU.subtract, ALU.mult)


def edge_positions(nc, A, g):
    with ExitStack() as stack:
        m = Memory(nc, stack, "ep_")
        src_i, dst_i = m.sb("src_i", [P, EP], I32), m.sb("dst_i", [P, EP], I32)
        weight = m.sb("weight", [P, EP])
        bucket_i, low_i = m.sb("bucket_i", [P, EP], I32), m.sb("low_i", [P, EP], I32)
        bucket, low, block, rank = (m.sb(n, [P, EP]) for n in ("bucket", "low", "block", "rank"))
        high_r = m.sb("high_r", [P, EP], F32R)
        bucket_no, in_buckets = m.sb("bucket_no", [P, NB]), m.sb("in_buckets", [P, 8, EP])
        ones_e = m.sb("ones_e", [P, EP])
        counts, totals_f, groups_f, ends = (m.sb(n, [P, NB]) for n in ("counts", "totals_f", "groups_f", "ends"))
        totals_i = m.sb("totals_i", [P, NB], I32)
        first_rank, ones_b = m.sb("first_rank", [P, NB]), m.sb("ones_b", [P, NB])
        member, running, placed = m.sb("member", [P, 2, EP]), m.sb("running", [P, 2, EP]), m.sb("placed", [P, 2, EP])
        before = m.sb("before", [P, P])
        group_no, past = m.sb("group_no", [P, 2]), m.sb("past", [P, 2, NB])
        group_bucket = m.sb("group_bucket", [P, 2])
        fill, zeros = m.sb("fill", [P, SLOTS_PER_P, 4]), m.sb("zeros", [P, D])
        ps_before, ps_total = m.psum("ps_before", [P, NB]), m.psum("ps_total", [P, NB])
        ps_table = m.psum("ps_table", [P, 2 * NG // 2])
        loaded = m.sem("loaded")
        made, table_ready = m.sem("made"), m.sem("table_ready")
        counted, summed, chain = m.sem("counted"), m.sem("summed"), m.sem("chain")
        filled = m.sem("filled")
        half = NG // 2
        block_ctx = stack.enter_context(nc.Block())

        @block_ctx.sync
        def _(sp):
            sp.dma_start(dst_i[0:NT, :], A["dst"].rearrange("(p e) -> p e", e=EP)).then_inc(loaded, 16)
            sp.dma_start(src_i[0:NT, :], A["src"].rearrange("(p e) -> p e", e=EP)).then_inc(loaded, 16)
            sp.dma_start(weight[0:NT, :], A["edge_weight"].rearrange("(p e) -> p e", e=EP)).then_inc(loaded, 16)
            sp.dma_start(g.x[0:NT], A["x"].rearrange("(t p) d -> p t d", p=NT)).then_inc(g.x_loaded, 16)
            sp.wait_ge(made, 7)
            sp.dma_start(g.sorted_edges.rearrange("(p s) f -> p s f", p=P), fill[:]).then_inc(filled, 16)
            sp.dma_start(g.slot_rows.rearrange("(n p) d -> p n d", p=P),
                         zeros[:].unsqueeze(1).broadcast_to([P, g.slot_tiles, D])).then_inc(filled, 16)
            unsure = SLOT_TILES - FULL_TILES
            sp.dma_start(g.slot_out[FULL_TILES * P:].rearrange("(n p) d -> p n d", p=P),
                         zeros[:].unsqueeze(1).broadcast_to([P, unsure, D])).then_inc(filled, 16)
            sp.wait_ge(filled, 48)
            sp.wait_ge(g.x_loaded, 16)

        @block_ctx.gpsimd
        def _(pool):
            nc.gpsimd.memset(g.ones[:], 1.0).then_inc(made, 1)
            nc.gpsimd.memset(g.ident[:], 0.0).then_inc(made, 1)
            nc.gpsimd.iota(bucket_no[:], pattern=[[1, NB]], base=0, channel_multiplier=0,
                           allow_small_or_imprecise_dtypes=True).then_inc(made, 1)
            nc.gpsimd.memset(fill[:], -1.0).then_inc(made, 1)
            nc.gpsimd.memset(zeros[:], 0.0).then_inc(made, 1)
            pool.wait_ge(made, 2)
            nc.gpsimd.affine_select(out=g.ident[:], in_=g.ident[:], compare_op=ALU.not_equal, fill=1.0, base=0,
                                    pattern=[[-1, P]], channel_multiplier=1).then_inc(made, 1)
            nc.gpsimd.affine_select(out=before[:], in_=g.ones[:], compare_op=ALU.is_gt, fill=0.0, base=0,
                                    pattern=[[1, P]], channel_multiplier=-1).then_inc(made, 1)
            nc.gpsimd.affine_select(out=g.before[:], in_=g.ones[:], compare_op=ALU.is_gt, fill=0.0, base=0,
                                    pattern=[[1, P]], channel_multiplier=-1).then_inc(made, 1)
            nc.gpsimd.iota(g.iota[:], pattern=[[1, ONE_HOT]], base=0, channel_multiplier=0,
                           allow_small_or_imprecise_dtypes=True).then_inc(made, 1)
            nc.gpsimd.iota(group_no[:], pattern=[[half, 2]], base=0, channel_multiplier=1,
                           allow_small_or_imprecise_dtypes=True).then_inc(made, 1)
            pool.wait_ge(made, 10)

        @block_ctx.vector
        def _(dve):
            c = Steps(dve, chain)
            r = slice(0, NT)
            v = nc.vector
            dve.wait_ge(loaded, 48)
            c.step(v.memset(ones_e[:], 1.0))
            c.step(v.memset(ones_b[:], 1.0))
            c.step(v.memset(block[:], 0.0))
            c.step(v.memset(rank[:], -1.0))
            c.step(v.tensor_scalar(bucket_i[r, :], dst_i[r, :], 5, None, ALU.logical_shift_right))
            c.link(v.tensor_scalar(low_i[r, :], dst_i[r, :], BUCKET - 1, None, ALU.bitwise_and))
            c.link(v.tensor_copy(bucket[r, :], bucket_i[r, :]))
            dve.wait_ge(made, 10)
            for b in range(0, NB, 8):
                c.link(v.tensor_tensor(in_buckets[r], bucket[r, :].unsqueeze(1).broadcast_to([NT, 8, EP]),
                                       bucket_no[r, b:b + 8].unsqueeze(2).broadcast_to([NT, 8, EP]), ALU.is_equal))
                if b == NB - 8:
                    v.reduce_sum(counts[r, b:b + 8], in_buckets[r], AX_X).then_inc(counted, 1)
                else:
                    c.link(v.reduce_sum(counts[r, b:b + 8], in_buckets[r], AX_X))
            src_f = placed[r, 0, :]
            c.step(v.tensor_copy(low[r, :], low_i[r, :]))
            c.link(v.tensor_copy(src_f, src_i[r, :]))
            for n in range(1, T):
                c.link(v.scalar_tensor_tensor(block[r, :], src_f, float(NT * n), block[r, :], ALU.is_ge, ALU.add))
            c.step(v.scalar_tensor_tensor(g.records[r, :, 0], block[r, :], -float(NT), src_f, ALU.mult, ALU.add))
            c.step(v.scalar_tensor_tensor(g.records[r, :, 1], block[r, :], float(BUCKET), low[r, :], ALU.mult, ALU.add))
            c.link(v.tensor_copy(high_r[r, :], weight[r, :]))
            c.step(v.tensor_copy(g.records[r, :, 2], high_r[r, :]))
            c.link(v.tensor_tensor(g.records[r, :, 3], weight[r, :], high_r[r, :], ALU.subtract))
            dve.wait_ge(summed, 2)
            c.link(v.tensor_scalar(totals_f[r, :], ps_total[r, :], float(GROUP - 1), None, ALU.add))
            c.link(v.tensor_copy(totals_i[r, :], totals_f[r, :]))
            c.link(v.tensor_scalar(totals_i[r, :], totals_i[r, :], 9, None, ALU.logical_shift_right))
            c.link(v.tensor_copy(groups_f[r, :], totals_i[r, :]))
            c.link(v.tensor_tensor_scan(ends[r, :], ones_b[r, :], groups_f[r, :], 0.0, ALU.mult, ALU.add))
            c.link(v.tensor_tensor(first_rank[r, :], ends[r, :], groups_f[r, :], ALU.subtract))
            c.link(v.scalar_tensor_tensor(first_rank[r, :], first_rank[r, :], float(GROUP), ps_before[r, :],
                                          ALU.mult, ALU.add))
            for h in range(2):
                c.link(v.tensor_scalar(past[0:half, h, :], ends[0:half, :], group_no[0:half, h:h + 1], None, ALU.is_le))
            c.link(v.reduce_sum(group_bucket[0:half, :], past[0:half], AX_X))
            v.tensor_scalar(group_bucket[0:half, :], group_bucket[0:half, :], float(NB - 1), float(BUCKET),
                            ALU.min, ALU.mult).then_inc(table_ready, 1)
            with c.rounds(NB // 2, 8) as j:
                for u in range(2):
                    c.step(v.tensor_scalar(member[r, u, :], bucket[r, :], bucket_no[r, bass.ds(j * 2 + u, 1)], None,
                                           ALU.is_equal))
                c.settle()
                for u in range(2):
                    c.step(v.tensor_tensor_scan(running[r, u, :], ones_e[r, :], member[r, u, :],
                                                first_rank[r, bass.ds(j * 2 + u, 1)], ALU.mult, ALU.add))
                c.settle()
                for u in range(2):
                    c.step(v.tensor_tensor(placed[r, u, :], running[r, u, :], member[r, u, :], ALU.mult))
                c.settle()
                for u in range(2):
                    c.link(v.tensor_tensor(rank[r, :], rank[r, :], placed[r, u, :], ALU.add))
            c.link(v.tensor_copy(dst_i[r, :], rank[r, :]))
            c.step(v.tensor_scalar(low_i[r, :], dst_i[r, :], P - 1, None, ALU.bitwise_and))
            c.link(v.tensor_scalar(bucket_i[r, :], dst_i[r, :], 7, None, ALU.logical_shift_right))
            c.link(v.scalar_tensor_tensor(g.edge_slot[r, :], low_i[r, :], float(SLOTS_PER_P), bucket_i[r, :],
                                          ALU.mult, ALU.add))
            dve.wait_ge(summed, 3)
            c.link(v.tensor_copy(g.group_offset[0:1, :], ps_table[0:1, :]))

        @block_ctx.tensor
        def _(pe):
            pe.wait_ge(made, 10)
            pe.wait_ge(counted, 1)
            pe.matmul(ps_before[0:NT, :], before[0:NT, 0:NT], counts[0:NT, :], start=True, stop=True).then_inc(summed, 1)
            pe.matmul(ps_total[0:NT, :], g.ones[0:NT, 0:NT], counts[0:NT, :], start=True, stop=True).then_inc(summed, 1)
            pe.wait_ge(table_ready, 1)
            for h in range(2):
                last = pe.matmul(ps_table[0:1, h * half:(h + 1) * half], group_bucket[0:half, h:h + 1],
                                 g.ident[0:half, 0:half], start=True, stop=True)
            last.then_inc(summed, 1)


class Shared:

    def __init__(self, nc, stack):
        m = Memory(nc, stack)
        self.x, self.xn = m.sb("x_rows", [P, T, D]), m.sb("xn_rows", [P, T, D])
        self.ones, self.ident = m.sb("ones", [P, P]), m.sb("ident", [P, P])
        self.before, self.iota = m.sb("before", [P, P]), m.sb("iota", [P, ONE_HOT])
        self.records = m.sb("records", [P, EP, 4])
        self.edge_slot = m.sb("edge_slot", [P, EP], U32)
        self.slots, self.gates = m.sb("slots", [P, 2, T], U32), m.sb("gates", [P, 2, T])
        self.dinv = m.sb("dinv", [P, T])
        self.group_offset = m.sb("group_offset", [1, NG], I32)
        self.x_loaded = m.sem("x_loaded")
        self.scattered, self.rows_scattered = m.sem("scattered"), m.sem("rows_scattered")
        self.gathered = [m.sem(f"gathered{t}") for t in range(T)]
        self.slot_tiles = SLOT_TILES + 2
        self.sorted_edges = nc.dram_tensor("sorted_edges", (NG * GROUP, 4), F32).ap()
        self.slot_rows = nc.dram_tensor("slot_rows", (self.slot_tiles * P, D), F32).ap()
        self.slot_out = nc.dram_tensor("slot_out", (SLOT_TILES * P, D), F32).ap()
def load_matrix(sp, buffer, matrix, arrived):
    sp.dma_start(buffer[:], matrix.rearrange("(k p) n -> p k n", p=P)).then_inc(arrived, 16)


def load_row(sp, buffer, vector, arrived):
    sp.dma_start(buffer[:], vector.partition_broadcast(P)).then_inc(arrived, 16)


def flow_attention(nc, A, g):
    with ExitStack() as stack:
        m = Memory(nc, stack, "fa_")
        w = {n: m.sb(n, [P, KD, D]) for n in ("Wq", "Wk", "Wv", "Wo")}
        w1, w2 = m.sb("W1", [P, KD, 2 * P]), m.sb("W2", [P, 2, D])
        rows = {n: m.sb(n, [P, D]) for n in ("bq", "bk", "bv", "bo", "g1", "be1", "g2", "be2", "b2")}
        b1 = m.sb("b1", [P, 2])
        q, k, v_ = (m.sb(n, [P, T, D]) for n in ("q", "k", "v"))
        k_sum, q_sum = m.sb("k_sum", [P, D]), m.sb("q_sum", [P, D])
        work = m.sb("work", [P, 2, D])
        work2 = m.sb("work2", [P, 2, D])
        turned = m.sb("turned", [P, 2, KD, NT])
        hidden = m.sb("hidden", [P, 2, 2, NT])
        sink, source = m.sb("sink", [P, T, HEADS]), m.sb("source", [P, T, HEADS])
        to_sink, to_source = m.sb("to_sink", [P, T, HEADS]), m.sb("to_source", [P, T, HEADS])
        share, e_sum = m.sb("share", [P, T, HEADS]), m.sb("e_sum", [P, HEADS])
        kv_t = m.sb("kv_t", [P, KD, P])
        mixed_w = m.sb("mixed_w", [P, KD, D])
        n1, n2, n3 = Norm(m, "n1"), Norm(m, "n2"), Norm(m, "n3")
        ps_t = m.psum("ps_t", [P, 2, D])
        ps_a, ps_b, ps_c = (m.psum(n, [P, D]) for n in ("ps_a", "ps_b", "ps_c"))
        ps_k, ps_q = m.psum("ps_k", [P, D]), m.psum("ps_q", [P, D])
        ps_e = m.psum("ps_e", [P, HEADS])
        names = ("weights in_ready turned_out turned_ready q_done k_done v_done q_out k_out v_out q_ready k_ready "
                 "sums_done sums_out scaled_ready scaled_used sums2_done sums2_out allocated exponent clipped "
                 "w_ready w_used kv_done kv_out mix_done mix_out x1_ready "
                 "d_in d_turned d_ready d_done d_out f_in f_turned f_ready h_done h_ready f_done f_out chain")
        s = {n: m.sem(n) for n in names.split()}
        block = stack.enter_context(nc.Block())

        def out(ps, t_rows=NT):
            return ps[0:NT, :]

        @block.sync
        def _(sp):
            for n in ("Wq", "Wk", "Wv"):
                load_matrix(sp, w[n], A["L0_mix_" + n], s["weights"])
            for n in ("g1", "be1", "bq", "bk", "bv", "g2", "be2", "bo", "b2"):
                load_row(sp, rows[n], A["L0_mix_" + n], s["weights"])
            load_matrix(sp, w["Wo"], A["L0_mix_Wo"], s["weights"])
            load_matrix(sp, w1, A["L0_mix_W1"], s["weights"])
            load_matrix(sp, w2, A["L0_mix_W2"], s["weights"])
            sp.dma_start(b1[:], A["L0_mix_b1"].rearrange("(k p) -> p k", p=P), allow_slow_non_contiguous=True).then_inc(s["weights"], 16)
            sp.wait_ge(s["weights"], 16 * 16)

        @block.gpsimd
        def _(pool):
            for e in range(EP):
                nc.gpsimd.indirect_dma_start(
                    g.sorted_edges, bass.IndirectOffsetOnAxis(ap=g.edge_slot[0:NT, e:e + 1], axis=0),
                    g.records[0:NT, e, :], None).then_inc(g.scattered, 16)
            pool.wait_ge(g.scattered, 16 * EP)

        @block.vector
        def _(dve):
            v = nc.vector
            c = Steps(dve, s["chain"])
            r = slice(0, NT)
            dve.wait_ge(g.x_loaded, 16)
            n1.all_stats(nc, c, g.x)
            n1.variance(nc, c)
            with c.rounds(T // 2, 2) as j:
                for u in range(2):
                    t = j * 2 + u
                    c.step(n1.apply(nc, tile(g.xn, t), tile(g.x, t), t))
            c.settle()
            n2.all_stats(nc, c, g.xn)
            n2.variance(nc, c)
            dve.wait_ge(s["weights"], 16 * 16)

            def prepare(t, u):
                dve.wait_ge(s["turned_out"], t + 1)
                c.link(n2.apply(nc, work[r, u, :], tile(g.xn, t), t))
                c.link(v.tensor_tensor(work[r, u, :], work[r, u, :], rows["g1"][r, :], ALU.mult))
                v.tensor_tensor(work[r, u, :], work[r, u, :], rows["be1"][r, :], ALU.add).then_inc(s["in_ready"], 1)

            def add_biases(t, u):
                for name, ps, to in (("q", ps_a, q), ("k", ps_b, k), ("v", ps_c, v_)):
                    dve.wait_ge(s[name + "_done"], t + (3 if name == "v" else 1))
                    v.tensor_tensor(tile(to, t), out(ps), rows["b" + name][r, :], ALU.add).then_inc(s[name + "_out"], 1)

            staggered(c, 4, prepare, add_biases, nothing)

            def softened(ps, to):
                c.step(v.tensor_scalar(to[:], ps[:], FLOW_EPS, None, ALU.add))

            def dots(sink_to, source_to):
                with c.rounds(T // 2, 8) as j:
                    for u in range(2):
                        t = j * 2 + u
                        for buf, a, b_, to in ((work, q, k_sum, sink_to), (work2, k, q_sum, source_to)):
                            c.step(v.scalar_tensor_tensor(buf[r, u, :], tile(a, t), FLOW_EPS, b_[r, :], ALU.add, ALU.mult))
                    c.settle()
                    for u in range(2):
                        t = j * 2 + u
                        for buf, to in ((work, sink_to), (work2, source_to)):
                            c.step(v.reduce_sum(tile(to, t), heads(buf[r, u, :]), AX_X))
                    c.settle()

            dve.wait_ge(s["q_ready"], T)
            dve.wait_ge(s["k_ready"], T)
            dve.wait_ge(s["sums_done"], 1)
            softened(ps_k, k_sum)
            softened(ps_q, q_sum)
            c.settle()
            dots(sink, source)
            c.settle()
            c.step(v.reciprocal(sink[r], sink[r]))
            c.link(v.reciprocal(source[r], source[r]))

            with c.rounds(T // 2, 0) as j:
                for u in range(2):
                    t = j * 2 + u
                    dve.wait_ge(s["scaled_used"], t + 1)
                    v.tensor_tensor(heads(work[r, u, :]), heads(tile(q, t)), over_head(tile(sink, t)),
                                    ALU.mult).then_inc(s["scaled_ready"], 1)
                    v.tensor_tensor(heads(work2[r, u, :]), heads(tile(k, t)), over_head(tile(source, t)),
                                    ALU.mult).then_inc(s["scaled_ready"], 1)
            dve.wait_ge(s["sums2_done"], 1)
            softened(ps_k, k_sum)
            softened(ps_q, q_sum)
            c.settle()
            dots(to_sink, to_source)
            c.settle()
            v.tensor_scalar(to_source[r], to_source[r], -1.0, 1.0, ALU.max, ALU.min).then_inc(s["clipped"], 1)
            dve.wait_ge(s["exponent"], 2)
            c.link(v.tensor_tensor(sink[r], sink[r], to_sink[r], ALU.mult))

            with c.rounds(T // 2, 0) as j:
                for u in range(2):
                    t = j * 2 + u
                    dve.wait_ge(s["w_used"], t + 1)
                    v.tensor_tensor(heads(work[r, u, :]), heads(tile(v_, t)), over_head(tile(share, t)),
                                    ALU.mult).then_inc(s["w_ready"], 1)
            c.step(v.memset(kv_t[:], 0.0))
            dve.wait_ge(s["kv_done"], 1)
            c.link(v.reciprocal(e_sum[r, :], ps_e[r, :]))
            c.link(v.tensor_scalar(e_sum[r, :], e_sum[r, :], float(NODES), None, ALU.mult))
            c.step(v.tensor_tensor(sink[r], sink[r], e_sum[r, :].unsqueeze(1).broadcast_to([NT, T, HEADS]), ALU.mult))
            kv = ps_a[:].rearrange("p (k n) -> p k n", k=KD)
            v.tensor_copy(kv_t[0:DH, :, 0:DH], kv[0:DH, :, 0:DH]).then_inc(s["kv_out"], 1)
            v.tensor_copy(kv_t[DH:P, :, DH:P], kv[DH:P, :, DH:P]).then_inc(s["kv_out"], 1)
            c.settle()

            def scale_q(t, u):
                dve.wait_ge(s["d_turned"], t + 1)
                v.tensor_tensor(heads(work[r, u, :]), heads(tile(q, t)), over_head(tile(sink, t)),
                                ALU.mult).then_inc(s["d_in"], 1)

            def attended(t, u):
                dve.wait_ge(s["d_done"], t + 3)
                c.link(v.tensor_tensor(work2[r, u, :], out(ps_b), rows["bo"][r, :], ALU.add))
                v.tensor_tensor(tile(v_, t), work2[r, u, :], tile(g.xn, t), ALU.add).then_inc(s["d_out"], 1)

            staggered(c, 2, scale_q, attended, nothing)
            dve.wait_ge(s["d_out"], T + 1)
            n3.all_stats(nc, c, v_)
            n3.variance(nc, c)

            def prepare_ff(t, u):
                dve.wait_ge(s["f_turned"], t + 1)
                c.link(n3.apply(nc, work[r, u, :], tile(v_, t), t))
                c.link(v.tensor_tensor(work[r, u, :], work[r, u, :], rows["g2"][r, :], ALU.mult))
                v.tensor_tensor(work[r, u, :], work[r, u, :], rows["be2"][r, :], ALU.add).then_inc(s["f_in"], 1)

            def add_up(t, u):
                c.link(v.tensor_tensor(work2[r, u, :], tile(v_, t), rows["b2"][r, :], ALU.add))
                dve.wait_ge(s["f_done"], t + 3)
                v.tensor_tensor(work2[r, u, :], work2[r, u, :], ps_c[r, :], ALU.add).then_inc(s["f_out"], 1)
                dve.wait_ge(s["f_out"], t + 2)
                c.step(v.tensor_tensor(tile(g.x, t), tile(g.x, t), work2[r, u, :], ALU.add))

            staggered(c, 8, prepare_ff, nothing, add_up)
            c.settle()

        @block.scalar
        def _(act):
            n1.root(nc, act)
            n2.root(nc, act)

            def copy_turned(done, ready, used, t, u):
                act.wait_ge(done, t + 3)
                act.wait_ge(used, t + 1)
                nc.scalar.copy(turned[:, u].rearrange("p k n -> p (k n)"), ps_t[:, u, 0:KD * NT]).then_inc(ready, 1)

            def evacuate(t, u):
                copy_turned(s["turned_out"], s["turned_ready"], s["v_done"], t, u)

            def sigmoids(t, u):
                for name, to in (("q", q), ("k", k)):
                    act.wait_ge(s[name + "_out"], t + 2)
                    nc.scalar.activation(tile(to, t), tile(to, t), ACT.Sigmoid).then_inc(s[name + "_ready"], 1)

            a = Steps(act, s["allocated"])
            staggered(a, 0, evacuate, sigmoids, nothing)
            act.wait_ge(s["clipped"], 1)
            nc.scalar.activation(to_sink[0:NT], to_sink[0:NT], ACT.Sigmoid).then_inc(s["exponent"], 1)
            nc.scalar.activation(share[0:NT], to_source[0:NT], ACT.Exp).then_inc(s["exponent"], 1)
            for i in range(KD):
                act.wait_ge(s["mix_done"], i + 1)
                nc.scalar.copy(mixed_w[:, i, :], (ps_b, ps_c)[i % 2][:]).then_inc(s["mix_out"], 1)
            staggered(a, 0, lambda t, u: copy_turned(s["d_turned"], s["d_ready"], s["d_done"], t, u), nothing, nothing)
            n3.root(nc, act)

            def evacuate_ff(t, u):
                copy_turned(s["f_turned"], s["f_ready"], s["h_done"], t, u)

            def gelu(t, u):
                act.wait_ge(s["h_done"], t + 3)
                act.wait_ge(s["f_done"], t + 1)
                nc.scalar.activation(hidden[:, u, 0, :], ps_a[:, 0:NT], ACT.Gelu, bias=b1[:, 0:1]).then_inc(s["h_ready"], 1)
                nc.scalar.activation(hidden[:, u, 1, :], ps_b[:, 0:NT], ACT.Gelu, bias=b1[:, 1:2]).then_inc(s["h_ready"], 1)

            staggered(a, 0, evacuate_ff, gelu, nothing)

        @block.tensor
        def _(pe):
            for n in ("turned_out", "v_done", "scaled_used", "w_used", "d_turned", "d_done", "f_turned", "h_done", "f_done"):
                pe.sem_inc(s[n], 2)
            pe.sem_inc(s["q_out"], 1)
            pe.sem_inc(s["k_out"], 1)
            pe.sem_inc(s["v_out"], 1)
            pe.sem_inc(s["d_out"], 1)
            pe.sem_inc(s["f_out"], 1)
            pe.sem_inc(s["h_ready"], 2)
            pe.wait_ge(s["weights"], 16 * 16)
            b = Steps(pe, s["allocated"])
            ones = g.ones[0:NT, :]

            def turn(ready, done, source):
                def f(t, u):
                    pe.wait_ge(ready, t + 1)
                    for i in range(KD):
                        last = pe.transpose(ps_t[:, u, i * NT:(i + 1) * NT], source[0:NT, u, i * P:(i + 1) * P],
                                            g.ident[0:NT, 0:NT])
                    last.then_inc(done, 1)
                return f

            def linear(ps, u, weight):
                for i in range(KD):
                    last = pe.matmul(ps[0:NT, :], turned[:, u, i, :], weight[:, i, :], start=(i == 0), stop=(i == KD - 1))
                return last

            def project(t, u):
                pe.wait_ge(s["turned_ready"], t + 1)
                for name, ps in (("q", ps_a), ("k", ps_b), ("v", ps_c)):
                    pe.wait_ge(s[name + "_out"], t + 1)
                    linear(ps, u, w["W" + name]).then_inc(s[name + "_done"], 1)

            def add_sums(t, u):
                pe.wait_ge(s["q_ready"], t + 1)
                pe.matmul(ps_q[:], ones, tile(q, t), start=is_tile(t, 0), stop=is_tile(t, T - 1))
                pe.wait_ge(s["k_ready"], t + 1)
                last = pe.matmul(ps_k[:], ones, tile(k, t), start=is_tile(t, 0), stop=is_tile(t, T - 1))
                if is_tile(t, T - 1):
                    last.then_inc(s["sums_done"], 1)

            staggered(b, 0, turn(s["in_ready"], s["turned_out"], work), project, add_sums)

            def add_scaled(t, u):
                pe.wait_ge(s["scaled_ready"], t * 2 + 2)
                pe.matmul(ps_q[:], ones, work[0:NT, u, :], start=is_tile(t, 0), stop=is_tile(t, T - 1))
                pe.matmul(ps_k[:], ones, work2[0:NT, u, :], start=is_tile(t, 0),
                          stop=is_tile(t, T - 1)).then_inc(s["scaled_used"], 1)
                if is_tile(t, T - 1):
                    pe.wait_ge(s["scaled_used"], T + 2)
                    pe.sem_inc(s["sums2_done"], 1)

            staggered(b, 0, nothing, add_scaled, nothing)

            def products(t, u):
                pe.wait_ge(s["w_ready"], t + 1)
                pe.matmul(ps_e[:], ones, tile(share, t), start=is_tile(t, 0), stop=is_tile(t, T - 1))
                for i in range(KD):
                    last = pe.matmul(ps_a[:, i * P:(i + 1) * P], work[0:NT, u, i * P:(i + 1) * P],
                                     tile(k, t)[:, i * P:(i + 1) * P], start=is_tile(t, 0) and i == 0,
                                     stop=is_tile(t, T - 1), skip_group_check=True)
                last.then_inc(s["w_used"], 1)
                if is_tile(t, T - 1):
                    pe.wait_ge(s["w_used"], T + 2)
                    pe.sem_inc(s["kv_done"], 1)

            staggered(b, 0, nothing, products, nothing)
            pe.wait_ge(s["kv_out"], 2)
            for i in range(KD):
                if i >= 2:
                    pe.wait_ge(s["mix_out"], i - 1)
                pe.matmul((ps_b, ps_c)[i % 2][:], kv_t[:, i, :], w["Wo"][:, i, :], start=True,
                          stop=True).then_inc(s["mix_done"], 1)
            pe.wait_ge(s["mix_out"], KD)

            def attend(t, u):
                pe.wait_ge(s["d_ready"], t + 1)
                pe.wait_ge(s["d_out"], t + 1)
                linear(ps_b, u, mixed_w).then_inc(s["d_done"], 1)

            staggered(b, 0, turn(s["d_in"], s["d_turned"], work), attend, nothing)
            pe.wait_ge(s["d_out"], T + 1)

            def ff_up(t, u):
                pe.wait_ge(s["f_ready"], t + 1)
                pe.wait_ge(s["h_ready"], t * 2 + 2)
                for half, ps in enumerate((ps_a, ps_b)):
                    for i in range(KD):
                        last = pe.matmul(ps[:, 0:NT], w1[:, i, half * P:(half + 1) * P], turned[:, u, i, :],
                                         start=(i == 0), stop=(i == KD - 1))
                last.then_inc(s["h_done"], 1)

            def ff_down(t, u):
                pe.wait_ge(s["h_ready"], t * 2 + 4)
                pe.wait_ge(s["f_out"], t + 1)
                for i in range(2):
                    last = pe.matmul(ps_c[0:NT, :], hidden[:, u, i, :], w2[:, i, :], start=(i == 0), stop=(i == 1))
                last.then_inc(s["f_done"], 1)

            staggered(b, 0, turn(s["f_in"], s["f_turned"], work), ff_up, ff_down)


def adjacency(nc, g, counts, weights):
    BUFS = 4
    POOL_ROWS = 3
    POOL_LOW = 1
    with ExitStack() as stack:
        m = Memory(nc, stack, "ad_")
        edges = m.sb("edges", [P, SLOTS_PER_P, 4])
        to = m.sb("to", [P, BUFS, CHUNKS, ONE_HOT], F32R)
        row, row_high, row_low = (m.sb(n, [P, BUFS, CHUNKS, P], F32R) for n in ("row", "row_high", "row_low"))
        row_no = m.sb("row_no", [P, BUFS, POOL_ROWS])
        ps_c, ps_w = m.psum("ps_c", [P, BUFS, 512]), m.psum("ps_w", [P, BUFS, 512])
        loaded, zeroed, columns_made, rows_made, scaled, low_scaled, used, numbered, begun, added, chain = (m.sem(n) for n in (
            "loaded", "zeroed", "columns_made", "rows_made", "scaled", "low_scaled", "used", "numbered", "begun", "added", "chain"))
        block = stack.enter_context(nc.Block())

        def field(t, c, f):
            s = t * CHUNKS + c
            return edges[:, s, f:f + 1] if isinstance(s, int) else edges[:, bass.ds(s, 1), f:f + 1].squeeze(1)

        def over_columns(t, n, f):
            s = t * CHUNKS + (CHUNKS - n)
            part = edges[:, s:s + n, f] if isinstance(s, int) else edges[:, bass.ds(s, n), f]
            return part.unsqueeze(2).broadcast_to([P, n, P])

        @block.sync
        def _(sp):
            sp.dma_start(edges[:], g.sorted_edges.rearrange("(p s) f -> p s f", p=P)).then_inc(loaded, 16)
            sp.wait_ge(loaded, 16)

        @block.gpsimd
        def _(pool):
            nc.gpsimd.memset(weights[:], 0.0).then_inc(zeroed, 1)
            pool.wait_ge(loaded, 16)

            def fetch_numbers(t, u):
                at = t * CHUNKS
                part = edges[:, at:at + POOL_ROWS, 0] if isinstance(t, int) else edges[:, bass.ds(at, POOL_ROWS), 0]
                nc.gpsimd.tensor_copy(row_no[:, u, :], part).then_inc(numbered, 1)

            def build_rows(t, u):
                pool.wait_ge(used, t + 1)
                pool.wait_ge(numbered, t + 1)
                pool.sem_inc(begun, 1)
                for c in range(POOL_ROWS):
                    last = nc.gpsimd.tensor_scalar(row[:, u, c, :], g.iota[:, 0:P], row_no[:, u, c:c + 1], None, ALU.is_equal)
                last.then_inc(rows_made, 1)

            def scale_low(t, u):
                pool.wait_ge(columns_made, t + 1)
                nc.gpsimd.tensor_tensor(row_low[:, u, CHUNKS - POOL_LOW:], row[:, u, CHUNKS - POOL_LOW:].bitcast(F32),
                                        over_columns(t, POOL_LOW, 3), ALU.mult).then_inc(low_scaled, 1)

            staggered(Steps(pool, chain), 0, fetch_numbers, build_rows, scale_low, NG, BUFS)
            pool.wait_ge(begun, NG)

        @block.vector
        def _(dve):
            v = nc.vector
            v.memset(counts[:], 0.0).then_inc(chain, 1)
            dve.wait_ge(chain, 1)
            dve.wait_ge(zeroed, 1)
            dve.wait_ge(loaded, 16)

            def build_columns(t, u):
                dve.wait_ge(used, t + 1)
                for c in range(CHUNKS):
                    v.tensor_scalar(to[:, u, c, :], g.iota[:], field(t, c, 1), None, ALU.is_equal)
                for c in range(POOL_ROWS, CHUNKS):
                    last = v.tensor_scalar(row[:, u, c, :], g.iota[:, 0:P], field(t, c, 0), None, ALU.is_equal)
                last.then_inc(columns_made, 1)

            def add(t, u):
                at = dve.value_load(g.group_offset[0:1, t:t + 1] if isinstance(t, int)
                                    else g.group_offset[0:1, bass.ds(t, 1)], min_val=0, max_val=DST - BUCKET)
                dve.wait_ge(used, t + (BUFS + 1))
                dve.wait_ge(added, t + BUFS)
                for ps, total in ((ps_c, counts), (ps_w, weights)):
                    part = total[:, :, bass.ds(at, BUCKET)]
                    last = v.tensor_tensor(part, part, ps[:, u, 0:ONE_HOT].rearrange("p (b n) -> p b n", b=T), ALU.add)
                last.then_inc(added, 1)

            staggered(Steps(dve, chain), 0, build_columns, nothing, add, NG, BUFS)
            dve.wait_ge(added, NG + BUFS)
            for b in range(T):
                own = weights[0:NT, b, b * NT:(b + 1) * NT]
                last = v.tensor_tensor(own, own, g.ident[0:NT, 0:NT], ALU.add)
            last.then_inc(chain, 1)
            dve.wait_ge(chain, 2)

        @block.scalar
        def _(act):
            act.wait_ge(loaded, 16)

            def scale(t, u):
                act.wait_ge(rows_made, t + 1)
                act.wait_ge(columns_made, t + 1)
                for c in range(CHUNKS):
                    last = nc.scalar.activation(row_high[:, u, c, :], row[:, u, c, :].bitcast(F32), ACT.Copy, scale=field(t, c, 2))
                    if c < CHUNKS - POOL_LOW:
                        nc.scalar.activation(row_low[:, u, c, :], row[:, u, c, :].bitcast(F32), ACT.Copy, scale=field(t, c, 3))
                last.then_inc(scaled, 1)

            staggered(Steps(act, chain), 0, nothing, scale, nothing, NG, BUFS)

        @block.tensor
        def _(pe):
            pe.sem_inc(used, BUFS)
            pe.sem_inc(added, BUFS)

            def product(t, u):
                pe.wait_ge(columns_made, t + 1)
                pe.wait_ge(added, t + 1)
                pe.wait_ge(rows_made, t + 1)
                for c in range(CHUNKS):
                    pe.matmul(ps_c[:, u, 0:ONE_HOT], row[:, u, c, :], to[:, u, c, :], start=(c == 0), stop=(c == CHUNKS - 1))
                pe.wait_ge(scaled, t + 1)
                pe.wait_ge(low_scaled, t + 1)
                for c in range(CHUNKS):
                    pe.matmul(ps_w[:, u, 0:ONE_HOT], row_high[:, u, c, :], to[:, u, c, :], start=(c == 0), stop=False)
                    last = pe.matmul(ps_w[:, u, 0:ONE_HOT], row_low[:, u, c, :], to[:, u, c, :], start=False,
                                     stop=(c == CHUNKS - 1))
                last.then_inc(used, 1)

            staggered(Steps(pe, chain), 0, nothing, product, nothing, NG, BUFS)


def graph_conv_0(nc, A, g, counts, weights):
    with ExitStack() as stack:
        m = Memory(nc, stack, "gc_")
        w_self, w_neigh = m.sb("w_self", [P, KD, D]), m.sb("w_neigh", [P, KD, D])
        rows = {n: m.sb(n, [P, D]) for n in ("bias", "gamma", "beta")}
        h = m.sb("h", [P, T, D])
        work, turned, around = m.sb("work", [P, 2, D]), m.sb("turned", [P, 2, KD, NT]), m.sb("around", [P, KD, 2 * NT])
        in_sum = h[:].rearrange("p t d -> p (t d)")[:, T * D - 2 * DST:].rearrange("p (m n) -> p m n", m=2)
        degree, inverse, positive = m.sb("degree", [P, T]), m.sb("inverse", [P, T]), m.sb("positive", [P, T])
        n1 = Norm(m, "n1")
        ps_t = m.psum("ps_t", [P, 2, D])
        ps_around = m.psum("ps_around", [P, KD, 256])
        ps_self, ps_neigh = m.psum("ps_self", [P, D]), m.psum("ps_neigh", [P, D])
        ps_degree = m.psum("ps_degree", [P, 2, T])
        names = "arrived copied turned_out turned_ready around_done around_ready linear_done taken summed degrees root root_ready used chain"
        s = {n: m.sem(n) for n in names.split()}
        block = stack.enter_context(nc.Block())

        @block.sync
        def _(sp):
            load_matrix(sp, w_self, A["L0_gnn_W_self"], s["arrived"])
            load_matrix(sp, w_neigh, A["L0_gnn_W_neigh"], s["arrived"])
            for n in rows:
                load_row(sp, rows[n], A["L0_gnn_" + n], s["arrived"])
            sp.wait_ge(s["arrived"], 16 * 5)

        @block.gpsimd
        def _(pool):
            def copy(t, u):
                pool.wait_ge(s["turned_out"], t + 1)
                nc.gpsimd.tensor_copy(work[0:NT, u, :], tile(g.xn, t)).then_inc(s["copied"], 1)

            staggered(Steps(pool, s["used"]), 0, copy, nothing, nothing)

        @block.scalar
        def _(act):
            def evacuate(t, u):
                act.wait_ge(s["turned_out"], t + 3)
                act.wait_ge(s["linear_done"], t + 1)
                nc.scalar.copy(turned[:, u].rearrange("p k n -> p (k n)"), ps_t[:, u, 0:KD * NT]).then_inc(s["turned_ready"], 1)

            def evacuate_around(t, u):
                if u == 0:
                    act.wait_ge(s["around_done"], t + 2)
                    act.wait_ge(s["linear_done"], t + 2)
                    nc.scalar.copy(around[:], ps_around[:, :, 0:2 * NT]).then_inc(s["around_ready"], 2)

            def root(t, u):
                n1.root(nc, act, t)

            staggered(Steps(act, s["used"]), 0, evacuate, evacuate_around, root)
            act.wait_ge(s["root"], 1)
            nc.scalar.activation(inverse[0:NT, :], degree[0:NT, :], ACT.Sqrt).then_inc(s["root_ready"], 1)

        @block.vector
        def _(dve):
            v = nc.vector
            c = Steps(dve, s["chain"])
            r = slice(0, NT)
            v.reduce_sum(in_sum[:, 0, :], counts[:].rearrange("p b n -> p n b"), AX_X).then_inc(s["summed"], 1)
            v.reduce_sum(in_sum[:, 1, :], weights[:].rearrange("p b n -> p n b"), AX_X).then_inc(s["summed"], 1)
            dve.wait_ge(s["degrees"], 1)
            c.link(v.tensor_scalar(degree[r, :], ps_degree[r, 0, :], 1.0, None, ALU.max))
            c.link(v.reciprocal(degree[r, :], degree[r, :]))
            dve.wait_ge(s["arrived"], 16 * 5)

            def combine(t, u):
                dve.wait_ge(s["linear_done"], t + 3)
                c.link(v.scalar_tensor_tensor(tile(h, t), ps_neigh[r, :], column(degree, t), rows["bias"][r, :],
                                              ALU.mult, ALU.add))
                v.tensor_tensor(tile(h, t), tile(h, t), ps_self[r, :], ALU.add).then_inc(s["taken"], 1)
                dve.wait_ge(s["taken"], t + 2)
                c.link(v.bn_stats(n1.tile_stats(t), tile(h, t)))
                n1.variance(nc, c, t)
                c.link(n1.apply(nc, tile(h, t), tile(h, t), t))
                c.link(v.tensor_tensor(tile(h, t), tile(h, t), rows["gamma"][r, :], ALU.mult))
                c.link(v.tensor_tensor(tile(h, t), tile(h, t), rows["beta"][r, :], ALU.add))
                c.step(v.tensor_tensor(tile(g.x, t), tile(g.x, t), tile(h, t), ALU.add))

            staggered(c, 34, nothing, combine, nothing)
            c.link(v.tensor_scalar(positive[r, :], ps_degree[r, 1, :], 0.0, None, ALU.is_gt))
            c.link(v.tensor_tensor(degree[r, :], ps_degree[r, 1, :], positive[r, :], ALU.mult))
            c.link(v.tensor_tensor(degree[r, :], degree[r, :], positive[r, :], ALU.subtract))
            v.tensor_scalar(degree[r, :], degree[r, :], 1.0, None, ALU.add).then_inc(s["root"], 1)
            dve.wait_ge(s["root_ready"], 1)
            c.link(v.reciprocal(g.dinv[r, :], inverse[r, :]))
            c.link(v.tensor_tensor(inverse[r, :], g.dinv[r, :], g.dinv[r, :], ALU.mult))
            c.link(v.tensor_tensor(inverse[r, :], inverse[r, :], degree[r, :], ALU.mult))
            c.link(v.tensor_scalar(inverse[r, :], inverse[r, :], -0.5, 1.5, ALU.mult, ALU.add))
            c.link(v.tensor_tensor(g.dinv[r, :], g.dinv[r, :], inverse[r, :], ALU.mult))
            c.link(v.tensor_tensor(g.dinv[r, :], g.dinv[r, :], positive[r, :], ALU.mult))
            c.settle()

        @block.tensor
        def _(pe):
            for n in ("turned_out", "linear_done"):
                pe.sem_inc(s[n], 2)
            pe.sem_inc(s["taken"], 1)
            pe.wait_ge(s["arrived"], 16 * 5)

            def degrees():
                pe.wait_ge(s["summed"], 2)
                for n in range(2):
                    for t in range(T):
                        last = pe.matmul(ps_degree[0:NT, n, t:t + 1], in_sum[0:NT, n, t * NT:(t + 1) * NT],
                                         g.ones[0:NT, 0:1], start=True, stop=True)
                last.then_inc(s["degrees"], 1)

            def gather_and_turn(t, u):
                if u == 0:
                    for k in range(KD):
                        for b in range(T):
                            into = counts[0:NT, b, t * NT:(t + 2) * NT] if isinstance(t, int) \
                                else counts[0:NT, b, bass.ds(t * NT, 2 * NT)]
                            last = pe.matmul(ps_around[:, k, 0:2 * NT], g.xn[0:NT, b, k * P:(k + 1) * P], into,
                                             start=(b == 0), stop=(b == T - 1))
                    last.then_inc(s["around_done"], 2)
                pe.wait_ge(s["copied"], t + 1)
                for k in range(KD):
                    last = pe.transpose(ps_t[:, u, k * NT:(k + 1) * NT], work[0:NT, u, k * P:(k + 1) * P],
                                        g.ident[0:NT, 0:NT])
                last.then_inc(s["turned_out"], 1)
                if is_tile(t, 0):
                    degrees()

            def linears(t, u):
                pe.wait_ge(s["turned_ready"], t + 1)
                pe.wait_ge(s["taken"], t + 1)
                if u == 0:
                    pe.wait_ge(s["around_ready"], t + 2)
                for k in range(KD):
                    pe.matmul(ps_self[0:NT, :], turned[:, u, k, :], w_self[:, k, :], start=(k == 0), stop=(k == KD - 1))
                for k in range(KD):
                    last = pe.matmul(ps_neigh[0:NT, :], around[:, k, u * NT:(u + 1) * NT], w_neigh[:, k, :],
                                     start=(k == 0), stop=(k == KD - 1))
                last.then_inc(s["linear_done"], 1)

            staggered(Steps(pe, s["used"]), 0, gather_and_turn, linears, nothing)


def expert_choice_0(nc, A, g):
    with ExitStack() as stack:
        m = Memory(nc, stack, "ec_")
        gate_w, gate_b = m.sb("gate_w", [EXPERTS_0, D]), m.sb("gate_b", [EXPERTS_0, 1])
        expert, bias = m.sb("expert", [P, KD, D]), m.sb("bias", [P, D])
        mean, products = m.sb("mean", [EXPERTS_0, D]), m.sb("products", [EXPERTS_0, D])
        logit, spread = m.sb("logit", [EXPERTS_0, 1]), m.sb("spread", [EXPERTS_0, P])
        scores, shifted, odds = (m.sb(n, [P, EXPERTS_0]) for n in ("scores", "shifted", "odds"))
        top, total, best = m.sb("top", [P, 8]), m.sb("total", [P, 1]), m.sb("best", [P, 8], U32)
        work, turned = m.sb("work", [P, 2, D]), m.sb("turned", [P, 2, KD, NT])
        work_y = m.sb("work_y", [P, 2, D])
        n1 = Norm(m, "n1")
        ps_t, ps_mean = m.psum("ps_t", [P, 2, D]), m.psum("ps_mean", [P, D])
        ps_y, ps_scores = m.psum("ps_y", [P, 2, D]), m.psum("ps_scores", [P, EXPERTS_0])
        names = "arrived normed copied summed logits scored shifted_ready odds_ready chosen fetched turned_out turned_ready linear_done taken chain used"
        s = {n: m.sem(n) for n in names.split()}
        block = stack.enter_context(nc.Block())

        @block.sync
        def _(sp):
            sp.dma_start(gate_w[:], A["L0_ffn_Wg"]).then_inc(s["arrived"], 16)
            sp.dma_start(gate_b[:], A["L0_ffn_bg"].rearrange("(e a) -> e a", a=1)).then_inc(s["arrived"], 16)
            sp.wait_ge(s["chosen"], 1)
            e = sp.value_load(best[0:1, 0:1], min_val=0, max_val=EXPERTS_0 - 1)
            sp.dma_start(expert[:], A["L0_ffn_We"][bass.ds(e, 1)].squeeze(0).rearrange("(k p) n -> p k n", p=P)).then_inc(s["fetched"], 16)
            sp.dma_start(bias[:], A["L0_ffn_be"][bass.ds(e, 1)].squeeze(0).partition_broadcast(P)).then_inc(s["fetched"], 16)
            sp.wait_ge(s["arrived"], 32)
            sp.wait_ge(s["fetched"], 32)

        @block.gpsimd
        def _(pool):
            def copy(t, u):
                pool.wait_ge(s["turned_out"], t + 1)
                pool.wait_ge(s["normed"], t + 1)
                nc.gpsimd.tensor_copy(work[0:NT, u, :], tile(g.xn, t)).then_inc(s["copied"], 1)

            staggered(Steps(pool, s["used"]), 0, copy, nothing, nothing)

        @block.scalar
        def _(act):
            n1.root(nc, act)
            act.wait_ge(s["shifted_ready"], 1)
            nc.scalar.activation(odds[:], shifted[:], ACT.Exp, accum_out=total[:]).then_inc(s["odds_ready"], 1)

            def evacuate(t, u):
                act.wait_ge(s["turned_out"], t + 3)
                act.wait_ge(s["linear_done"], t + 1)
                nc.scalar.copy(turned[:, u].rearrange("p k n -> p (k n)"), ps_t[:, u, 0:KD * NT]).then_inc(s["turned_ready"], 1)

            staggered(Steps(act, s["used"]), 0, evacuate, nothing, nothing)

        @block.vector
        def _(dve):
            v = nc.vector
            c = Steps(dve, s["chain"])
            r, er = slice(0, NT), slice(0, EXPERTS_0)
            n1.all_stats(nc, c, g.x)
            n1.variance(nc, c)
            with c.rounds(T // 2, 0) as j:
                for u in range(2):
                    t = j * 2 + u
                    n1.apply(nc, tile(g.xn, t), tile(g.x, t), t).then_inc(s["normed"], 1)
            dve.wait_ge(s["summed"], 1)
            dve.wait_ge(s["arrived"], 32)
            c.link(v.tensor_scalar(mean[:], ps_mean[er, :], 1.0 / NODES, None, ALU.mult))
            c.link(v.tensor_tensor(products[:], mean[:], gate_w[:], ALU.mult))
            c.link(v.reduce_sum(logit[:], products[:], AX_X))
            c.link(v.tensor_tensor(logit[:], logit[:], gate_b[:], ALU.add))
            v.tensor_scalar(spread[:], g.ones[er, :], logit[:, 0:1], None, ALU.mult).then_inc(s["logits"], 1)
            dve.wait_ge(s["scored"], 1)
            c.link(v.tensor_copy(scores[:], ps_scores[:]))
            c.link(v.max(top[:], scores[:]))
            v.tensor_scalar(shifted[:], scores[:], top[:, 0:1], None, ALU.subtract).then_inc(s["shifted_ready"], 1)
            dve.wait_ge(s["odds_ready"], 1)
            c.link(v.reciprocal(total[:], total[:]))
            c.link(v.tensor_scalar(scores[:], odds[:], total[:, 0:1], None, ALU.mult))
            c.link(v.max(top[:], scores[:]))
            v.max_index(best[:], top[:], scores[:]).then_inc(s["chosen"], 1)
            dve.wait_ge(s["fetched"], 32)

            def combine(t, u):
                dve.wait_ge(s["linear_done"], t + 3)
                v.tensor_tensor(work_y[r, u, :], ps_y[r, u, :], bias[r, :], ALU.add).then_inc(s["taken"], 1)
                dve.wait_ge(s["taken"], t + 3)
                c.step(v.scalar_tensor_tensor(tile(g.x, t), work_y[r, u, :], top[r, 0:1], tile(g.x, t), ALU.mult, ALU.add))
                c.settle()

            staggered(c, 2, nothing, combine, nothing)

        @block.tensor
        def _(pe):
            for n in ("turned_out", "linear_done", "taken"):
                pe.sem_inc(s[n], 2)

            def add_up(t, u):
                pe.wait_ge(s["normed"], t + 1)
                last = pe.matmul(ps_mean[:], g.ones[0:NT, :], tile(g.xn, t), start=is_tile(t, 0), stop=is_tile(t, T - 1))
                if is_tile(t, T - 1):
                    last.then_inc(s["summed"], 1)

            staggered(Steps(pe, s["used"]), 0, nothing, add_up, nothing)
            pe.wait_ge(s["logits"], 1)
            pe.matmul(ps_scores[:], spread[:], g.ident[0:EXPERTS_0, 0:EXPERTS_0], start=True, stop=True).then_inc(s["scored"], 1)

            def turn(t, u):
                pe.wait_ge(s["copied"], t + 1)
                for k in range(KD):
                    last = pe.transpose(ps_t[:, u, k * NT:(k + 1) * NT], work[0:NT, u, k * P:(k + 1) * P],
                                        g.ident[0:NT, 0:NT])
                last.then_inc(s["turned_out"], 1)

            def linear(t, u):
                if is_tile(t, 0):
                    pe.wait_ge(s["fetched"], 32)
                pe.wait_ge(s["turned_ready"], t + 1)
                pe.wait_ge(s["taken"], t + 1)
                for k in range(KD):
                    last = pe.matmul(ps_y[0:NT, u, :], turned[:, u, k, :], expert[:, k, :], start=(k == 0), stop=(k == KD - 1))
                last.then_inc(s["linear_done"], 1)

            staggered(Steps(pe, s["used"]), 0, turn, linear, nothing)


def layer_1(nc, A, g, weights):
    with ExitStack() as stack:
        m = Memory(nc, stack, "l1_")
        w = {n: m.sb(n, [P, KD, D]) for n in ("Wq", "Wk", "Wv", "Wo")}
        w_conv, w_lin = m.sb("w_conv", [P, KD, GCN]), m.sb("w_lin", [P, D])
        rows = {n: m.sb(n, [P, D]) for n in ("bq", "bk", "bv", "bo")}
        b_lin, b_conv = m.sb("b_lin", [P, D]), m.sb("b_conv", [P, 1])
        temperature = m.sb("temperature", [P, 1])
        conv_spread = m.sb("conv_spread", [P, P])
        values, conv = m.sb("values", [P, T, D]), m.sb("conv", [P, T, GCN])
        work, turned = m.sb("work", [P, 2, D]), m.sb("turned", [P, 2, KD, NT])
        qw, kw, both = m.sb("qw", [P, 2, D]), m.sb("kw", [P, 2, D]), m.sb("both", [P, 2, D])
        around = m.sb("around", [P, 2 * NT])
        qk, q_sum, k_sum, sink, alloc, comp, scale, tmp = (
            m.sb(n, [P, T, HEADS]) for n in ("qk", "q_sum", "k_sum", "sink", "alloc", "comp", "scale", "tmp"))
        n1 = Norm(m, "n1")
        ps_t = m.psum("ps_t", [P, 2, D])
        ps_q, ps_k, ps_v = (m.psum(n, [P, D]) for n in ("ps_q", "ps_k", "ps_v"))
        ps_conv = m.psum("ps_conv", [P, D])
        ps_around, ps_row = m.psum("ps_around", [P, 2 * NT]), m.psum("ps_row", [P, D])
        names = ("arrived spread_ready row_done in_ready turned_out turned_ready q_done k_done v_done conv_done q_out k_out "
                 "v_out conv_out q_ready k_ready dotted alloc_in alloc_ready comp_in comp_ready "
                 "o_in o_turned o_ready around_done around_ready o_done o_out chain used")
        s = {n: m.sem(n) for n in names.split()}
        block = stack.enter_context(nc.Block())

        @block.sync
        def _(sp):
            for n in ("Wq", "Wk", "Wv"):
                load_matrix(sp, w[n], A["L1_mix_" + n], s["arrived"])
            load_matrix(sp, w_conv, A["L1_gnn_W_conv"], s["arrived"])
            for n in rows:
                load_row(sp, rows[n], A["L1_mix_" + n], s["arrived"])
            load_row(sp, b_lin, A["L1_gnn_b_lin"], s["arrived"])
            load_row(sp, temperature, A["L1_mix_temperature"], s["arrived"])
            sp.dma_start(b_conv[:], A["L1_gnn_b_conv"].rearrange("(p a) -> p a", a=1)).then_inc(s["arrived"], 16)
            sp.dma_start(w_lin[:], A["L1_gnn_W_lin"]).then_inc(s["arrived"], 16)
            load_matrix(sp, w["Wo"], A["L1_mix_Wo"], s["arrived"])
            sp.wait_ge(s["arrived"], 16 * 13)

        @block.vector
        def _(dve):
            v = nc.vector
            c = Steps(dve, s["chain"])
            r = slice(0, NT)
            dve.wait_ge(s["arrived"], 16 * 13)
            v.tensor_scalar(conv_spread[:], g.ones[:], b_conv[:, 0:1], None, ALU.mult).then_inc(s["spread_ready"], 1)
            n1.all_stats(nc, c, g.x)
            n1.variance(nc, c)
            c.link(v.tensor_tensor(b_lin[:], b_lin[:], rows["bo"][:], ALU.add))
            dve.wait_ge(s["row_done"], 1)
            c.link(v.tensor_tensor(b_lin[:], b_lin[:], ps_row[:], ALU.add))

            def prepare(t, u):
                dve.wait_ge(s["turned_out"], t + 1)
                n1.apply(nc, work[r, u, :], tile(g.x, t), t).then_inc(s["in_ready"], 1)
                c.step(n1.apply(nc, tile(g.xn, t), tile(g.x, t), t))

            def add_biases(t, u):
                for name, ps, to in (("q", ps_q, qw[r, u, :]), ("k", ps_k, kw[r, u, :]), ("v", ps_v, tile(values, t))):
                    dve.wait_ge(s[name + "_done"], t + 1)
                    v.tensor_tensor(to, ps[r, :], rows["b" + name][r, :], ALU.add).then_inc(s[name + "_out"], 1)
                dve.wait_ge(s["conv_done"], t + 3)
                v.tensor_scalar(tile(conv, t), ps_conv[r, 0:GCN], column(g.dinv, t), None, ALU.mult).then_inc(s["conv_out"], 1)

            def dots(t, u):
                dve.wait_ge(s["q_ready"], t + 1)
                dve.wait_ge(s["k_ready"], t + 1)
                c.step(v.tensor_tensor(both[r, u, :], qw[r, u, :], kw[r, u, :], ALU.mult))
                c.step(v.reduce_sum(tile(q_sum, t), heads(qw[r, u, :]), AX_X))
                c.link(v.reduce_sum(tile(k_sum, t), heads(kw[r, u, :]), AX_X))
                c.link(v.reduce_sum(tile(qk, t), heads(both[r, u, :]), AX_X))

            staggered(c, 10, prepare, add_biases, dots)
            c.settle()
            eps = FLOW_EPS
            c.link(v.tensor_tensor(tmp[r], q_sum[r], k_sum[r], ALU.add))
            c.link(v.scalar_tensor_tensor(sink[r], tmp[r], eps, qk[r], ALU.mult, ALU.add))
            c.link(v.tensor_scalar(sink[r], sink[r], DH * eps * eps + eps, None, ALU.add))
            c.link(v.reciprocal(sink[r], sink[r]))
            for ours, theirs, to in ((q_sum, k_sum, alloc), (k_sum, q_sum, comp)):
                c.link(v.scalar_tensor_tensor(tmp[r], theirs[r], eps, qk[r], ALU.mult, ALU.add))
                c.link(v.tensor_tensor(tmp[r], tmp[r], sink[r], ALU.mult))
                c.link(v.scalar_tensor_tensor(to[r], ours[r], eps, tmp[r], ALU.mult, ALU.add))
                c.link(v.tensor_scalar(to[r], to[r], DH * eps * eps + eps, None, ALU.add))
            c.link(v.reciprocal(temperature[:], temperature[:]))
            c.link(v.tensor_scalar(comp[r], comp[r], -1.0, 1.0, ALU.max, ALU.min))
            c.link(v.tensor_scalar(comp[r], comp[r], temperature[r, 0:1], None, ALU.mult))
            v.tensor_tensor(comp[r], comp[r], comp[r], ALU.subtract).then_inc(s["comp_in"], 1)
            dve.wait_ge(s["comp_ready"], 2)
            c.link(v.reciprocal(tmp[r], comp[r]))
            c.link(v.tensor_tensor(comp[r], comp[r], tmp[r], ALU.mult))
            c.link(v.scalar_tensor_tensor(scale[r], comp[r], float(D), qk[r], ALU.mult, ALU.mult))
            c.link(v.tensor_tensor(scale[r], scale[r], sink[r], ALU.mult))
            c.link(v.tensor_tensor(scale[r], scale[r], alloc[r], ALU.mult))

            def attend(t, u):
                dve.wait_ge(s["o_turned"], t + 1)
                v.tensor_tensor(heads(work[r, u, :]), heads(tile(values, t)), over_head(tile(scale, t)),
                                ALU.mult).then_inc(s["o_in"], 1)

            def combine(t, u):
                dve.wait_ge(s["o_done"], t + 3)
                c.step(v.tensor_tensor(both[r, u, :], ps_q[r, :], b_lin[r, :], ALU.add))
                c.link(v.tensor_tensor(tile(g.x, t), tile(g.x, t), tile(g.xn, t), ALU.add))
                v.scalar_tensor_tensor(both[r, u, :], ps_k[r, :], column(g.dinv, t), both[r, u, :], ALU.mult,
                                       ALU.add).then_inc(s["o_out"], 1)
                dve.wait_ge(s["o_out"], t + 2)
                c.link(v.tensor_tensor(tile(g.x, t), tile(g.x, t), both[r, u, :], ALU.add))

            staggered(c, 6, attend, nothing, combine)

        @block.scalar
        def _(act):
            n1.root(nc, act)
            a = Steps(act, s["used"])

            def copy_turned(done, ready, used):
                def f(t, u):
                    act.wait_ge(done, t + 3)
                    act.wait_ge(used, t + 1)
                    nc.scalar.copy(turned[:, u].rearrange("p k n -> p (k n)"), ps_t[:, u, 0:KD * NT]).then_inc(ready, 1)
                return f

            def sigmoids(t, u):
                for name, buf in (("q", qw), ("k", kw)):
                    act.wait_ge(s[name + "_out"], t + 2)
                    nc.scalar.activation(buf[0:NT, u, :], buf[0:NT, u, :], ACT.Sigmoid).then_inc(s[name + "_ready"], 1)

            staggered(a, 0, copy_turned(s["turned_out"], s["turned_ready"], s["conv_done"]), sigmoids, nothing)
            act.wait_ge(s["comp_in"], 1)
            nc.scalar.activation(alloc[0:NT], alloc[0:NT], ACT.Sigmoid).then_inc(s["comp_ready"], 1)
            nc.scalar.activation(comp[0:NT], comp[0:NT], ACT.Exp).then_inc(s["comp_ready"], 1)

            turned_o = copy_turned(s["o_turned"], s["o_ready"], s["o_done"])

            def around_out(t, u):
                if u == 0:
                    act.wait_ge(s["around_done"], t + 2)
                    act.wait_ge(s["o_done"], t + 2)
                    nc.scalar.copy(around[:], ps_around[:]).then_inc(s["around_ready"], 2)

            staggered(a, 0, turned_o, around_out, nothing)

        @block.tensor
        def _(pe):
            for n in ("turned_out", "conv_done", "o_turned", "o_done"):
                pe.sem_inc(s[n], 2)
            for n in ("q_out", "k_out", "v_out", "conv_out", "o_out"):
                pe.sem_inc(s[n], 1)
            b = Steps(pe, s["used"])
            pe.wait_ge(s["arrived"], 16 * 13)
            pe.wait_ge(s["spread_ready"], 1)
            pe.matmul(ps_row[:], conv_spread[:], w_lin[:], start=True, stop=True).then_inc(s["row_done"], 1)

            def turn(ready, done):
                def f(t, u):
                    pe.wait_ge(ready, t + 1)
                    for k in range(KD):
                        last = pe.transpose(ps_t[:, u, k * NT:(k + 1) * NT], work[0:NT, u, k * P:(k + 1) * P],
                                            g.ident[0:NT, 0:NT])
                    last.then_inc(done, 1)
                return f

            def project(t, u):
                pe.wait_ge(s["turned_ready"], t + 1)
                for name, ps, matrix in (("q", ps_q, w["Wq"]), ("k", ps_k, w["Wk"]), ("v", ps_v, w["Wv"]),
                                         ("conv", ps_conv, w_conv)):
                    pe.wait_ge(s[name + "_out"], t + 1)
                    for k in range(KD):
                        last = pe.matmul(ps[0:NT, 0:GCN] if name == "conv" else ps[0:NT, :], turned[:, u, k, :],
                                         matrix[:, k, :], start=(k == 0), stop=(k == KD - 1))
                    last.then_inc(s[name + "_done"], 1)

            staggered(b, 0, turn(s["in_ready"], s["turned_out"]), project, nothing)
            pe.wait_ge(s["conv_out"], T + 1)
            turn_o = turn(s["o_in"], s["o_turned"])

            def gather_and_turn(t, u):
                if u == 0:
                    for k in range(T):
                        into = weights[0:NT, k, t * NT:(t + 2) * NT] if isinstance(t, int) \
                            else weights[0:NT, k, bass.ds(t * NT, 2 * NT)]
                        last = pe.matmul(ps_around[:], conv[0:NT, k, :], into, start=(k == 0), stop=(k == T - 1))
                    last.then_inc(s["around_done"], 2)
                turn_o(t, u)

            def outputs(t, u):
                pe.wait_ge(s["o_ready"], t + 1)
                pe.wait_ge(s["o_out"], t + 1)
                if u == 0:
                    pe.wait_ge(s["around_ready"], t + 2)
                for k in range(KD):
                    pe.matmul(ps_q[0:NT, :], turned[:, u, k, :], w["Wo"][:, k, :], start=(k == 0), stop=(k == KD - 1))
                pe.matmul(ps_k[0:NT, :], around[:, u * NT:(u + 1) * NT], w_lin[:], start=True,
                          stop=True).then_inc(s["o_done"], 1)

            staggered(b, 0, gather_and_turn, outputs, nothing)


FT = DFF // P
FC = DFF // D
HALF = KD * DFF


class Experts:

    def __init__(self, nc, A, stack):
        m = Memory(nc, stack, "ex_")
        self.up, self.down = A["L1_ffn_W1"], A["L1_ffn_W2"]
        self.weights = m.sb("weights", [P, 2 * 2 * HALF])
        self.b1 = m.sb("b1", [P, EXPERTS * FT])
        self.ends = m.sb("ends", [P, EXPERTS], I32)
        self.expert_of, self.buffer_of = m.sb("expert_of", [P, SLOT_TILES], I32), m.sb("buffer_of", [P, SLOT_TILES], I32)
        self.loaded = {(u, part): m.sem(f"loaded{u}_{part}") for u in range(2) for part in ("up", "down")}

    def load(self, sp, e, u):
        up, down = (w[e] if isinstance(e, int) else w[bass.ds(e, 1)].squeeze(0) for w in (self.up, self.down))
        at = 2 * u * HALF
        sp.dma_start(self.weights[:, at:at + HALF].rearrange("p (k f) -> p k f", k=KD),
                     up.rearrange("(k p) f -> p k f", p=P)).then_inc(self.loaded[u, "up"], 16)
        sp.dma_start(self.weights[:, at + HALF:at + 2 * HALF].rearrange("p (f d) -> p f d", f=FT),
                     down.rearrange("(f p) d -> p f d", p=P)).then_inc(self.loaded[u, "down"], 16)


def routing(nc, A, g, x):
    with ExitStack() as stack:
        m = Memory(nc, stack, "ro_")
        router, router_b = m.sb("router", [P, KD, EXPERTS]), m.sb("router_b", [P, EXPERTS])
        ln_g, ln_b = m.sb("ln_g", [P, D]), m.sb("ln_b", [P, D])
        b1_rows, b2 = m.sb("b1_rows", [P, P]), m.sb("b2", [EXPERTS, D])
        work, turned = m.sb("work", [P, 2, D]), m.sb("turned", [P, 2, KD, NT])
        logits, equal, place, chosen, slot, gate_row, *pick = (m.sb(n, [P, T, EXPERTS]) for n in (
            "logits", "equal", "place", "chosen", "slot", "gate_row", "pick0", "pick1"))
        top = [m.sb("top0", [P, T]), m.sb("top1", [P, T])]
        least, odds = m.sb("least", [P, T]), m.sb("odds", [P, T])
        in_tiles, ends, first_slot = (m.sb(n, [P, EXPERTS]) for n in ("in_tiles", "ends", "first_slot"))
        in_tiles_i = m.sb("in_tiles_i", [P, EXPERTS], I32)
        before_tile = m.sb("before_tile", [P, T + 1, EXPERTS])
        past = m.sb("past", [P, SLOT_TILES, EXPERTS])
        tile_expert = m.sb("tile_expert", [P, SLOT_TILES])
        gates_t = m.sb("gates_t", [EXPERTS, 2, NT])
        n1, n2 = Norm(m, "n1"), Norm(m, "n2")
        ps_t = m.psum("ps_t", [P, 2, D])
        ps_logits, ps_counts, ps_b1 = m.psum("ps_logits", [P, T, EXPERTS]), m.psum("ps_counts", [P, 2, T, EXPERTS]), m.psum("ps_b1", [P, P])
        ps_gates, ps_bias = m.psum("ps_gates", [P, NT]), m.psum("ps_bias", [P, D])
        names = ("arrived normed in_ready turned_out turned_ready logits_done b1_turned b1_ready picked counted odds_in "
                 "odds_ready gates_in gates_turned gates_ready bias_done bias_out slots_ready chain used")
        s = {n: m.sem(n) for n in names.split()}
        block = stack.enter_context(nc.Block())

        @block.sync
        def _(sp):
            load_matrix(sp, router, A["L1_ffn_w_r"], s["arrived"])
            load_row(sp, router_b, A["L1_ffn_b_r"], s["arrived"])
            load_row(sp, ln_g, A["L1_ffn_ln_g"], s["arrived"])
            load_row(sp, ln_b, A["L1_ffn_ln_b"], s["arrived"])
            sp.dma_start(b1_rows[:], A["L1_ffn_b1"].rearrange("e (f p) -> (e f) p", p=P)).then_inc(s["arrived"], 16)
            sp.dma_start(b2[:], A["L1_ffn_b2"]).then_inc(s["arrived"], 16)
            x.load(sp, 0, 0)
            x.load(sp, 1, 1)
            sp.wait_ge(s["arrived"], 16 * 6)

        @block.gpsimd
        def _(pool):
            def copy(t, u):
                pool.wait_ge(s["turned_out"], t + 1)
                pool.wait_ge(s["normed"], t + 1)
                nc.gpsimd.tensor_copy(work[0:NT, u, :], tile(g.xn, t)).then_inc(s["in_ready"], 1)

            staggered(Steps(pool, s["used"]), 0, copy, nothing, nothing)
            pool.wait_ge(s["slots_ready"], 2)
            for n in range(2):
                for t in range(T):
                    nc.gpsimd.indirect_dma_start(
                        g.slot_rows, bass.IndirectOffsetOnAxis(ap=g.slots[0:NT, n, t:t + 1], axis=0),
                        g.xn[0:NT, t, :], None).then_inc(g.rows_scattered, 16)
            pool.wait_ge(g.rows_scattered, 16 * 2 * T)

        @block.vector
        def _(dve):
            v = nc.vector
            c = Steps(dve, s["chain"])
            r = slice(0, NT)
            n1.all_stats(nc, c, g.x)
            n1.variance(nc, c)
            with c.rounds(T // 2, 4) as j:
                for u in range(2):
                    c.step(n1.apply(nc, tile(g.xn, j * 2 + u), tile(g.x, j * 2 + u), j * 2 + u))
                c.settle()
                for u in range(2):
                    t = j * 2 + u
                    c.step(v.tensor_tensor(tile(g.x, t), tile(g.x, t), tile(g.xn, t), ALU.add))
            c.settle()
            n2.all_stats(nc, c, g.xn)
            n2.variance(nc, c)
            dve.wait_ge(s["arrived"], 16 * 6)
            with c.rounds(T // 2, 4) as j:
                for u in range(2):
                    t = j * 2 + u
                    c.link(n2.apply(nc, tile(g.xn, t), tile(g.xn, t), t))
                    c.link(v.tensor_tensor(tile(g.xn, t), tile(g.xn, t), ln_g[r, :], ALU.mult))
                    v.tensor_tensor(tile(g.xn, t), tile(g.xn, t), ln_b[r, :], ALU.add).then_inc(s["normed"], 1)
            c.step(v.memset(before_tile[:, 0, :], 0.0))
            dve.wait_ge(s["logits_done"], T + 2)
            all_ = [NT, T, EXPERTS]
            c.link(v.tensor_tensor(logits[r], ps_logits[r], router_b[r, :].unsqueeze(1).broadcast_to(all_), ALU.add))
            numbers = g.iota[r, 0:EXPERTS].unsqueeze(1).broadcast_to(all_)
            for n in range(2):
                c.link(v.tensor_reduce(top[n][r, :], logits[r], AX_X, ALU.max))
                c.link(v.tensor_tensor(equal[r], logits[r], top[n][r, :].unsqueeze(2).broadcast_to(all_), ALU.is_equal))
                c.link(v.scalar_tensor_tensor(place[r], equal[r], -float(EXPERTS), numbers, ALU.mult, ALU.add))
                c.link(v.tensor_reduce(least[r, :], place[r], AX_X, ALU.min))
                c.link(v.tensor_tensor(pick[n][r], place[r], least[r, :].unsqueeze(2).broadcast_to(all_), ALU.is_equal))
                if n == 0:
                    c.link(v.scalar_tensor_tensor(logits[r], pick[n][r], -3e38, logits[r], ALU.mult, ALU.add))
            v.tensor_tensor(chosen[r], pick[0][r], pick[1][r], ALU.add).then_inc(s["picked"], 1)
            v.tensor_tensor(odds[r, :], top[1][r, :], top[0][r, :], ALU.subtract).then_inc(s["odds_in"], 1)
            dve.wait_ge(s["counted"], 2)
            for t in range(T):
                c.link(v.tensor_tensor(before_tile[:, t + 1, :], before_tile[:, t, :], ps_counts[:, 1, t, :], ALU.add))
            c.link(v.tensor_scalar(in_tiles[:], before_tile[:, T, :], float(P - 1), None, ALU.add))
            c.link(v.tensor_copy(in_tiles_i[:], in_tiles[:]))
            c.link(v.tensor_scalar(in_tiles_i[:], in_tiles_i[:], 7, None, ALU.logical_shift_right))
            c.link(v.tensor_copy(in_tiles[:], in_tiles_i[:]))
            c.link(v.tensor_tensor_scan(ends[:], g.ones[:, 0:EXPERTS], in_tiles[:], 0.0, ALU.mult, ALU.add))
            c.step(v.tensor_copy(x.ends[:], ends[:]))
            c.link(v.tensor_tensor(first_slot[:], ends[:], in_tiles[:], ALU.subtract))
            c.link(v.tensor_scalar(first_slot[:], first_slot[:], float(P), None, ALU.mult))
            c.link(v.tensor_tensor(slot[r], before_tile[r, 0:T, :], first_slot[r, :].unsqueeze(1).broadcast_to(all_), ALU.add))
            c.link(v.tensor_tensor(slot[r], slot[r], ps_counts[r, 0], ALU.add))
            for n in range(2):
                c.link(v.tensor_tensor(place[r], slot[r], pick[n][r], ALU.mult))
                c.link(v.reduce_sum(least[r, :], place[r], AX_X))
                v.tensor_copy(g.slots[r, n, :], least[r, :]).then_inc(s["slots_ready"], 1)
                dve.wait_ge(s["slots_ready"], n + 1)
            tiles = [P, SLOT_TILES, EXPERTS]
            c.link(v.tensor_tensor(past[:], ends[:].unsqueeze(1).broadcast_to(tiles),
                                   g.iota[:, 0:SLOT_TILES].unsqueeze(2).broadcast_to(tiles), ALU.is_le))
            c.link(v.reduce_sum(tile_expert[:], past[:], AX_X))
            c.link(v.tensor_scalar(tile_expert[:], tile_expert[:], float(EXPERTS - 1), None, ALU.min))
            c.link(v.tensor_copy(x.expert_of[:], tile_expert[:]))
            c.link(v.tensor_scalar(x.buffer_of[:], x.expert_of[:], 1, None, ALU.bitwise_and))
            dve.wait_ge(s["odds_ready"], 1)
            c.link(v.tensor_scalar(g.gates[r, 0, :], odds[r, :], 1.0, None, ALU.add))
            c.link(v.reciprocal(g.gates[r, 0, :], g.gates[r, 0, :]))
            c.link(v.tensor_tensor(g.gates[r, 1, :], odds[r, :], g.gates[r, 0, :], ALU.mult))
            c.step(v.tensor_tensor(place[r], pick[0][r], g.gates[r, 0, :].unsqueeze(2).broadcast_to(all_), ALU.mult))
            c.link(v.tensor_tensor(equal[r], pick[1][r], g.gates[r, 1, :].unsqueeze(2).broadcast_to(all_), ALU.mult))
            v.tensor_tensor(gate_row[r], place[r], equal[r], ALU.add).then_inc(s["gates_in"], 1)
            for t in range(T):
                dve.wait_ge(s["gates_turned"], t + 1)
                v.tensor_copy(gates_t[:, t % 2, :], ps_gates[0:EXPERTS, :]).then_inc(s["gates_ready"], 1)
                dve.wait_ge(s["bias_done"], t + 1)
                v.tensor_tensor(g.x[r, t, :], g.x[r, t, :], ps_bias[r, :], ALU.add).then_inc(s["bias_out"], 1)
            dve.wait_ge(s["bias_out"], T)

        @block.scalar
        def _(act):
            n1.root(nc, act)
            n2.root(nc, act)
            act.wait_ge(s["b1_turned"], 1)
            nc.scalar.copy(x.b1[:], ps_b1[:]).then_inc(s["b1_ready"], 1)

            def evacuate(t, u):
                act.wait_ge(s["turned_out"], t + 3)
                act.wait_ge(s["logits_done"], t + 1)
                nc.scalar.copy(turned[:, u].rearrange("p k n -> p (k n)"), ps_t[:, u, 0:KD * NT]).then_inc(s["turned_ready"], 1)

            staggered(Steps(act, s["used"]), 0, evacuate, nothing, nothing)
            act.wait_ge(s["odds_in"], 1)
            nc.scalar.activation(odds[0:NT, :], odds[0:NT, :], ACT.Exp).then_inc(s["odds_ready"], 1)
            act.wait_ge(s["b1_ready"], 1)

        @block.tensor
        def _(pe):
            for n in ("turned_out", "logits_done"):
                pe.sem_inc(s[n], 2)
            pe.wait_ge(s["arrived"], 16 * 6)
            pe.transpose(ps_b1[:], b1_rows[:], g.ident[:]).then_inc(s["b1_turned"], 1)

            def turn(t, u):
                pe.wait_ge(s["in_ready"], t + 1)
                for k in range(KD):
                    last = pe.transpose(ps_t[:, u, k * NT:(k + 1) * NT], work[0:NT, u, k * P:(k + 1) * P],
                                        g.ident[0:NT, 0:NT])
                last.then_inc(s["turned_out"], 1)

            def score(t, u):
                pe.wait_ge(s["turned_ready"], t + 1)
                for k in range(KD):
                    last = pe.matmul(tile(ps_logits, t), turned[:, u, k, :], router[:, k, :], start=(k == 0), stop=(k == KD - 1))
                last.then_inc(s["logits_done"], 1)

            staggered(Steps(pe, s["used"]), 0, turn, score, nothing)
            pe.wait_ge(s["picked"], 1)
            picked = chosen[0:NT].rearrange("p t e -> p (t e)")
            pe.matmul(ps_counts[0:NT, 0].rearrange("p t e -> p (t e)"), g.before[0:NT, 0:NT], picked, start=True,
                      stop=True).then_inc(s["counted"], 1)
            pe.matmul(ps_counts[:, 1].rearrange("p t e -> p (t e)"), g.ones[0:NT, :], picked, start=True,
                      stop=True).then_inc(s["counted"], 1)
            pe.wait_ge(s["gates_in"], 1)
            for t in range(T):
                pe.matmul(ps_gates[0:EXPERTS, :], gate_row[0:NT, t, :], g.ident[0:NT, 0:NT], start=True,
                          stop=True).then_inc(s["gates_turned"], 1)
                pe.wait_ge(s["gates_ready"], t + 1)
                if t:
                    pe.wait_ge(s["bias_out"], t)
                pe.matmul(ps_bias[0:NT, :], gates_t[:, t % 2, :], b2[:], start=True, stop=True).then_inc(s["bias_done"], 1)


def expert_tiles(nc, g, x):
    with ExitStack() as stack:
        m = Memory(nc, stack, "et_")
        turned, hidden_t = m.sb("turned", [P, KD, P]), m.sb("hidden_t", [P, FT, P])
        rows_in, y = g.xn[:, 0, :], g.xn[:, 1, :]
        ps_t, ps_y = m.psum("ps_t", [P, D]), m.psum("ps_y", [P, D])
        ps_h = m.psum("ps_h", [P, 2, KD, P])
        names = ("weights_ready rows_loaded rows_turned rows_ready up_done hidden_ready tiles_done y_out y_stored finished")
        s = {n: m.sem(n) for n in names.split()}
        block = stack.enter_context(nc.Block())
        out_rows = g.slot_out.rearrange("(n p) d -> n p d", p=P)
        in_rows = g.slot_rows.rearrange("(n p) d -> n p d", p=P)

        def entry(engine, table, t, most):
            return engine.value_load(table[0:1, bass.ds(t, 1)], min_val=0, max_val=most)

        def last_end(engine):
            return engine.value_load(x.ends[0:1, EXPERTS - 1:EXPERTS], min_val=0, max_val=SLOT_TILES)

        @contextmanager
        def used_tiles(engine):
            total = last_end(engine)
            with engine.Fori(0, SLOT_TILES) as t:
                with engine.If(t < total):
                    yield t

        @block.sync
        def _(sp):
            with sp.Fori(0, EXPERTS // 2 - 1) as j:
                for u in range(2):
                    last_tile = sp.value_load(x.ends[0:1, bass.ds(j * 2 + u, 1)], min_val=0, max_val=SLOT_TILES)
                    sp.wait_ge(s["tiles_done"], last_tile + 1)
                    x.load(sp, j * 2 + (u + 2), u)

        @block.gpsimd
        def _(pool):
            for e in range(EXPERTS):
                for part in ("up", "down"):
                    pool.wait_ge(x.loaded[e % 2, part], 16 * (e // 2 + 1))
                    pool.sem_inc(s["weights_ready"], 1)
            pool.wait_ge(s["weights_ready"], 2 * EXPERTS)

        @block.vector
        def _(dve):
            def move_turned(t):
                dve.wait_ge(s["rows_turned"], t + 1)
                nc.vector.tensor_copy(turned[:].rearrange("p k n -> p (k n)"), ps_t[:]).then_inc(s["rows_ready"], 1)

            move_turned(0)
            with used_tiles(dve) as t:
                move_turned(t + 1)
                dve.wait_ge(s["tiles_done"], t + 2)
                dve.wait_ge(s["y_stored"], t * 16 + 16)
                nc.vector.tensor_copy(y, ps_y[:]).then_inc(s["y_out"], 1)

        @block.scalar
        def _(act):
            def load_rows(t):
                act.dma_start(rows_in, in_rows[t] if isinstance(t, int) else in_rows[bass.ds(t, 1)].squeeze(0)
                              ).then_inc(s["rows_loaded"], 16)

            load_rows(0)
            act.wait_ge(s["rows_turned"], 1)
            load_rows(1)
            with used_tiles(act) as t:
                e = entry(act, x.expert_of, t, EXPERTS - 1)
                act.wait_ge(s["tiles_done"], t + 1)
                for f in range(FC):
                    act.wait_ge(s["up_done"], t * FC + (f + 1))
                    for i in range(KD):
                        last = nc.scalar.activation(hidden_t[:, f * KD + i, :], ps_h[:, f % 2, i, :],
                                                    ACT.Gelu, bias=x.b1[:, bass.ds(e * FT + (f * KD + i), 1)])
                    last.then_inc(s["hidden_ready"], 1)
                act.wait_ge(s["rows_turned"], t + 2)
                load_rows(t + 2)
                act.wait_ge(s["y_out"], t + 2)
                act.dma_start(out_rows[bass.ds(t, 1)].squeeze(0), y).then_inc(s["y_stored"], 16)
            act.wait_ge(s["y_stored"], last_end(act) * 16 + 16)
            act.sem_inc(s["finished"], 1)
            act.wait_ge(s["rows_loaded"], last_end(act) * 16 + 32)
            act.sem_inc(s["finished"], 1)
            act.wait_ge(s["finished"], 2)

        @block.tensor
        def _(pe):
            pe.sem_inc(s["hidden_ready"], 2)
            pe.sem_inc(s["tiles_done"], 1)
            pe.sem_inc(s["y_out"], 1)
            pe.sem_inc(s["y_stored"], 16)

            def turn_rows(t):
                pe.wait_ge(s["rows_loaded"], t * 16 + 16)
                for k in range(KD):
                    last = pe.transpose(ps_t[:, k * P:(k + 1) * P], rows_in[:, k * P:(k + 1) * P], g.ident[:])
                last.then_inc(s["rows_turned"], 1)

            turn_rows(0)
            with used_tiles(pe) as t:
                e = entry(pe, x.expert_of, t, EXPERTS - 1)
                buffer = entry(pe, x.buffer_of, t, 1)
                pe.wait_ge(s["rows_ready"], t + 1)
                pe.wait_ge(s["weights_ready"], e * 2 + 1)
                for u in range(2):
                    with pe.If(buffer == u):
                        for f in range(FC):
                            pe.wait_ge(s["hidden_ready"], t * FC + (f + 1))
                            for i in range(KD):
                                for k in range(KD):
                                    at = 2 * u * HALF + k * DFF + (f * KD + i) * P
                                    last = pe.matmul(ps_h[:, f % 2, i, :], x.weights[:, at:at + P], turned[:, k, :],
                                                     start=(k == 0), stop=(k == KD - 1))
                            last.then_inc(s["up_done"], 1)
                turn_rows(t + 1)
                pe.wait_ge(s["weights_ready"], e * 2 + 2)
                pe.wait_ge(s["y_out"], t + 1)
                for f in range(FC):
                    pe.wait_ge(s["hidden_ready"], t * FC + (f + 3))
                    for i in range(f * KD, (f + 1) * KD):
                        last = pe.matmul(ps_y[:], hidden_t[:, i, :],
                                         x.weights[:, bass.ds(buffer * (2 * HALF) + (HALF + i * D), D)],
                                         start=(i == 0), stop=(i == FT - 1))
                last.then_inc(s["tiles_done"], 1)


def gather_experts(nc, A, g):
    with ExitStack() as stack:
        m = Memory(nc, stack, "ge_")
        y = m.sb("y", [P, 2, T, D])
        half, summed, stored = m.sem("half"), m.sem("summed"), m.sem("stored")
        block = stack.enter_context(nc.Block())

        @block.gpsimd
        def _(pool):
            for t in range(T):
                for n in range(2):
                    nc.gpsimd.indirect_dma_start(
                        y[0:NT, n, t, :], None, g.slot_out,
                        bass.IndirectOffsetOnAxis(ap=g.slots[0:NT, n, t:t + 1], axis=0)).then_inc(g.gathered[t], 16)

        @block.vector
        def _(dve):
            for t in range(T):
                dve.wait_ge(g.gathered[t], 32)
                for n, done in ((0, half), (1, summed)):
                    nc.vector.scalar_tensor_tensor(g.x[0:NT, t, :], y[0:NT, n, t, :], g.gates[0:NT, n, t:t + 1],
                                                   g.x[0:NT, t, :], ALU.mult, ALU.add).then_inc(done, 1)
                    dve.wait_ge(done, t + 1)

        @block.sync
        def _(sp):
            for t in range(T):
                sp.wait_ge(summed, t + 1)
                sp.dma_start(A["out"][t * NT:(t + 1) * NT], g.x[0:NT, t, :]).then_inc(stored, 16)
            sp.wait_ge(stored, 16 * T)


def program(nc, A):
    with ExitStack() as stack:
        g = Shared(nc, stack)
        edge_positions(nc, A, g)
        flow_attention(nc, A, g)
        with ExitStack() as graph:
            weights = Memory(nc, graph).sb("edge_weights", [P, T, DST])
            with ExitStack() as first:
                counts = Memory(nc, first).sb("edge_counts", [P, T, DST])
                adjacency(nc, g, counts, weights)
                graph_conv_0(nc, A, g, counts, weights)
            expert_choice_0(nc, A, g)
            layer_1(nc, A, g, weights)
        with ExitStack() as layer:
            x = Experts(nc, A, layer)
            routing(nc, A, g, x)
            expert_tiles(nc, g, x)
        gather_experts(nc, A, g)


def kernel(**inputs):
    import numpy as _np
    import concourse.bacc as _bacc
    from concourse import mybir as _mybir
    from concourse.bass_utils import run_bass_kernel_spmd as _run

    nc = _bacc.Bacc("TRN2", target_bir_lowering=False, num_devices=1)
    arrays, A = {}, {}
    for name, a in inputs.items():
        a = _np.asarray(a)
        if name in ("L0_gnn_W_self", "L0_gnn_W_neigh", "L0_ffn_Wg", "L1_ffn_w_r"):
            a = a.T
        a = _np.ascontiguousarray(a)
        arrays[name] = a
        A[name] = nc.dram_tensor(name, a.shape, _mybir.dt.from_np(a.dtype), kind="ExternalInput").ap()
    A["out"] = nc.dram_tensor("out", (NODES, D), F32, kind="ExternalOutput").ap()
    program(nc, A)
    r = _run(nc, [arrays], core_ids=[0])
    return r.results[0]["out"]
```
